# Optimizing a Trainium2 kernel written in Bass

```python
import numpy as np
import jax
import jax.numpy as jnp

def _softmax(x, axis=-1):
    return jax.nn.softmax(x, axis=axis)

def _gelu(x):
    return jax.nn.gelu(x, approximate=True)

def _silu(x):
    return jax.nn.silu(x)

def _sigmoid(x):
    return jax.nn.sigmoid(x)

def _layernorm(x, axis=-1, eps=1e-05):
    m = jnp.mean(x, axis=axis, keepdims=True)
    v = jnp.var(x, axis=axis, keepdims=True)
    return (x - m) / jnp.sqrt(v + eps)

def _scatter_add(tgt, idx, src, axis=0):
    return tgt.at[idx].add(src)

def _segment_sum(src, seg, n):
    return jax.ops.segment_sum(src, seg, n)
kernel_name = 'mk_gnn_preln_d4_gnn_r8_3103aa'

def setup_inputs(seed: int=0):
    np.random.seed(seed)
    _w = jnp.asarray

    def _rec_inputs():
        import jax
        import jax.numpy as jnp
        _gk = jax.random.key(seed)
        x = -0.0003713 + 1 * jax.random.normal(jax.random.fold_in(_gk, 1), (6250, 256), jnp.float32)
        _s = jax.random.randint(jax.random.fold_in(_gk, 2), (50000,), 0, 6250, jnp.int32)
        _d = jax.random.randint(jax.random.fold_in(_gk, 3), (50000,), 0, 6250, jnp.int32)
        _loop = jnp.arange(6250, dtype=jnp.int32)
        src = jnp.concatenate([_s, _d, _loop])
        dst = jnp.concatenate([_d, _s, _loop])
        _o = jnp.argsort(dst, stable=True)
        src = src[_o]
        dst = dst[_o]
        edge_attr_16 = -0.000153872 + 1.00011 * jax.random.normal(jax.random.fold_in(_gk, 12), (106250, 16), jnp.float32)
        edge_attr_4 = 0.0007022 + 0.999661 * jax.random.normal(jax.random.fold_in(_gk, 13), (106250, 4), jnp.float32)
        edge_attr_64 = 0.000189758 + 1.00013 * jax.random.normal(jax.random.fold_in(_gk, 14), (106250, 64), jnp.float32)
        return (x, src, dst, edge_attr_16, edge_attr_4, edge_attr_64)
    x, src, dst, edge_attr_16, edge_attr_4, edge_attr_64 = _rec_inputs()

    def _L0_gnn_setup():
        import jax, jax.numpy as jnp
        import numpy as np
        N, E, C, R, HID = (6250, 62500, 64, 16, 64)
        key = jax.random.key(seed)
        ks = jax.random.split(key, 24)
        g = lambda k, shape, s=1.0: jax.random.normal(k, shape, dtype=jnp.float32) * s
        cs = C ** (-0.5)
        inp = {'h': g(ks[0], (N, 4 * C)), 'edge_index': jax.random.randint(ks[1], (2, E), 0, N), 'edge_sh': g(ks[2], (E, 4)), 'edge_rbf': g(ks[3], (E, R)), 'W_up0': g(ks[4], (C, C), cs), 'W_up1': g(ks[5], (C, C), cs), 'M1': g(ks[6], (R, HID), R ** (-0.5)), 'M2': g(ks[7], (HID, HID), HID ** (-0.5)), 'M3': g(ks[8], (HID, HID), HID ** (-0.5)), 'M4': g(ks[9], (HID, 4 * C), HID ** (-0.5)), 'W_lin0': g(ks[10], (C, C), cs), 'W_lin1': g(ks[11], (C, C), cs), 'Wsc0': g(ks[12], (C, C), cs), 'Wsc1': g(ks[13], (C, C), cs), 'Wc0': g(ks[14], (C, 5)), 'Wc1': g(ks[15], (C, 4)), 'WB0': g(ks[16], (C, C), cs), 'WB1': g(ks[17], (C, C), cs), 'gamma0': jnp.ones((C,), jnp.float32), 'beta0': jnp.zeros((C,), jnp.float32), 'gamma1': jnp.ones((C,), jnp.float32)}
        return inp
    _L0_gnn_all = _L0_gnn_setup()
    _L0_gnn_in = {k: v for k, v in _L0_gnn_all.items() if k in ('W_up0', 'W_up1', 'M1', 'M2', 'M3', 'M4', 'W_lin0', 'W_lin1', 'Wsc0', 'Wsc1', 'Wc0', 'Wc1', 'WB0', 'WB1', 'gamma0', 'beta0', 'gamma1')}
    del _L0_gnn_all

    def _L1_gnn_setup():
        import jax, jax.numpy as jnp
        import numpy as np
        N_NODES = 8192
        N_EDGES = 131072
        HEADS = 4
        HEAD_DIM = 64
        DIM = 256
        BN_EPS = 1e-05
        key = jax.random.key(seed)
        k1, k2, k3, k4 = jax.random.split(key, 4)
        features = jax.random.normal(k1, (N_NODES, DIM), dtype=jnp.float32)
        src = jax.random.randint(k2, (N_EDGES,), 0, N_NODES, dtype=jnp.int64)
        dst = jax.random.randint(k3, (N_EDGES,), 0, N_NODES, dtype=jnp.int64)
        W_src = jax.random.normal(k4, (DIM, HEADS * HEAD_DIM), dtype=jnp.float32) * (1.0 / np.sqrt(DIM))
        gamma = jnp.ones((DIM,), dtype=jnp.float32)
        beta = jnp.zeros((DIM,), dtype=jnp.float32)
        return {'features': features, 'src': src, 'dst': dst, 'W_src': W_src, 'gamma': gamma, 'beta': beta}
    _L1_gnn_all = _L1_gnn_setup()
    _L1_gnn_in = {k: v for k, v in _L1_gnn_all.items() if k in ('W_src', 'gamma', 'beta')}
    del _L1_gnn_all

    def _L2_gnn_setup():
        import jax, jax.numpy as jnp
        import numpy as np
        N, E = (6250, 100000)
        HID, EDIM, HEADS = (256, 64, 8)
        C = HID // HEADS
        NEG_SLOPE = 0.2
        LN_EPS = 1e-05

        def _gat_block(x, edge_index, edge_attr, W, W_e, att_src, att_dst, att_edge, bias, gamma, beta):
            n = x.shape[0]
            src, dst = (edge_index[0], edge_index[1])
            xp = (x @ W).reshape(n, HEADS, C)
            a_src = jnp.einsum('nhc,hc->nh', xp, att_src)
            a_dst = jnp.einsum('nhc,hc->nh', xp, att_dst)
            ep = (edge_attr @ W_e).reshape(-1, HEADS, C)
            a_edge = jnp.einsum('ehc,hc->eh', ep, att_edge)
            alpha = a_src[src] + a_dst[dst] + a_edge
            alpha = jax.nn.leaky_relu(alpha, NEG_SLOPE)
            m = jax.ops.segment_max(alpha, dst, num_segments=n)
            m = jnp.where(jnp.isfinite(m), m, 0.0)
            ea = jnp.exp(alpha - m[dst])
            den = jax.ops.segment_sum(ea, dst, num_segments=n)
            attn = ea / (den[dst] + 1e-16)
            msg = xp[src] * attn[:, :, None]
            out = jax.ops.segment_sum(msg, dst, num_segments=n)
            h = out.reshape(n, HEADS * C) + bias
            y = x + h
            mu = jnp.mean(y, axis=-1, keepdims=True)
            var = jnp.var(y, axis=-1, keepdims=True)
            return (y - mu) * jax.lax.rsqrt(var + LN_EPS) * gamma + beta
        key = jax.random.key(seed)
        ks = jax.random.split(key, 12)
        s = 1.0 / np.sqrt(HID)
        se = 1.0 / np.sqrt(EDIM)
        return {'x': jax.random.normal(ks[0], (N, HID), jnp.float32), 'edge_index': jax.random.randint(ks[1], (2, E), 0, N, jnp.int32), 'edge_attr': jax.random.normal(ks[2], (E, EDIM), jnp.float32), 'W': jax.random.uniform(ks[3], (HID, HEADS * C), jnp.float32, -s, s), 'W_e': jax.random.uniform(ks[4], (EDIM, HEADS * C), jnp.float32, -se, se), 'att_src': jax.random.normal(ks[5], (HEADS, C), jnp.float32) * 0.1, 'att_dst': jax.random.normal(ks[6], (HEADS, C), jnp.float32) * 0.1, 'att_edge': jax.random.normal(ks[7], (HEADS, C), jnp.float32) * 0.1, 'bias': jnp.zeros((HEADS * C,), jnp.float32), 'gamma': jnp.ones((HID,), jnp.float32), 'beta': jnp.zeros((HID,), jnp.float32)}
    _L2_gnn_all = _L2_gnn_setup()
    _L2_gnn_in = {k: v for k, v in _L2_gnn_all.items() if k in ('W', 'W_e', 'att_src', 'att_dst', 'att_edge', 'bias', 'gamma', 'beta')}
    del _L2_gnn_all

    def _L3_gnn_setup():
        import jax, jax.numpy as jnp
        import numpy as np
        N, E = (6250, 100000)
        IN, H, C = (256, 8, 32)
        NEG_SLOPE = 0.2
        EPS = 1e-05
        key = jax.random.key(seed)
        ks = jax.random.split(key, 6)
        x = jax.random.normal(ks[0], (N, IN), jnp.float32)
        edge_index = jax.random.randint(ks[1], (2, E), 0, N, dtype=jnp.int32)
        W = jax.random.normal(ks[2], (IN, H * C), jnp.float32) / np.sqrt(IN).astype(np.float32)
        att_src = jax.random.normal(ks[3], (H, C), jnp.float32) * 0.1
        att_dst = jax.random.normal(ks[4], (H, C), jnp.float32) * 0.1
        bias = jnp.zeros((H * C,), jnp.float32)
        gamma = jnp.ones((H * C,), jnp.float32)
        beta = jnp.zeros((H * C,), jnp.float32)
        return {'x': x, 'edge_index': edge_index, 'W': W, 'att_src': att_src, 'att_dst': att_dst, 'bias': bias, 'gamma': gamma, 'beta': beta}
    _L3_gnn_all = _L3_gnn_setup()
    _L3_gnn_in = {k: v for k, v in _L3_gnn_all.items() if k in ('W', 'att_src', 'att_dst', 'bias', 'gamma', 'beta')}
    del _L3_gnn_all
    return {'x': x, 'src': src, 'dst': dst, 'edge_attr_16': edge_attr_16, 'edge_attr_4': edge_attr_4, 'edge_attr_64': edge_attr_64, 'L0_gnn_W_up0': _L0_gnn_in['W_up0'], 'L0_gnn_W_up1': _L0_gnn_in['W_up1'], 'L0_gnn_M1': _L0_gnn_in['M1'], 'L0_gnn_M2': _L0_gnn_in['M2'], 'L0_gnn_M3': _L0_gnn_in['M3'], 'L0_gnn_M4': _L0_gnn_in['M4'], 'L0_gnn_W_lin0': _L0_gnn_in['W_lin0'], 'L0_gnn_W_lin1': _L0_gnn_in['W_lin1'], 'L0_gnn_Wsc0': _L0_gnn_in['Wsc0'], 'L0_gnn_Wsc1': _L0_gnn_in['Wsc1'], 'L0_gnn_Wc0': _L0_gnn_in['Wc0'], 'L0_gnn_Wc1': _L0_gnn_in['Wc1'], 'L0_gnn_WB0': _L0_gnn_in['WB0'], 'L0_gnn_WB1': _L0_gnn_in['WB1'], 'L0_gnn_gamma0': _L0_gnn_in['gamma0'], 'L0_gnn_beta0': _L0_gnn_in['beta0'], 'L0_gnn_gamma1': _L0_gnn_in['gamma1'], 'L1_gnn_W_src': _L1_gnn_in['W_src'], 'L1_gnn_gamma': _L1_gnn_in['gamma'], 'L1_gnn_beta': _L1_gnn_in['beta'], 'L2_gnn_W': _L2_gnn_in['W'], 'L2_gnn_W_e': _L2_gnn_in['W_e'], 'L2_gnn_att_src': _L2_gnn_in['att_src'], 'L2_gnn_att_dst': _L2_gnn_in['att_dst'], 'L2_gnn_att_edge': _L2_gnn_in['att_edge'], 'L2_gnn_bias': _L2_gnn_in['bias'], 'L2_gnn_gamma': _L2_gnn_in['gamma'], 'L2_gnn_beta': _L2_gnn_in['beta'], 'L3_gnn_W': _L3_gnn_in['W'], 'L3_gnn_att_src': _L3_gnn_in['att_src'], 'L3_gnn_att_dst': _L3_gnn_in['att_dst'], 'L3_gnn_bias': _L3_gnn_in['bias'], 'L3_gnn_gamma': _L3_gnn_in['gamma'], 'L3_gnn_beta': _L3_gnn_in['beta']}

def reference(x, src, dst, edge_attr_16, edge_attr_4, edge_attr_64, L0_gnn_W_up0, L0_gnn_W_up1, L0_gnn_M1, L0_gnn_M2, L0_gnn_M3, L0_gnn_M4, L0_gnn_W_lin0, L0_gnn_W_lin1, L0_gnn_Wsc0, L0_gnn_Wsc1, L0_gnn_Wc0, L0_gnn_Wc1, L0_gnn_WB0, L0_gnn_WB1, L0_gnn_gamma0, L0_gnn_beta0, L0_gnn_gamma1, L1_gnn_W_src, L1_gnn_gamma, L1_gnn_beta, L2_gnn_W, L2_gnn_W_e, L2_gnn_att_src, L2_gnn_att_dst, L2_gnn_att_edge, L2_gnn_bias, L2_gnn_gamma, L2_gnn_beta, L3_gnn_W, L3_gnn_att_src, L3_gnn_att_dst, L3_gnn_bias, L3_gnn_gamma, L3_gnn_beta):
    import jax
    import jax.numpy as jnp

    def _L0_gnn_ref(h, edge_index, edge_sh, edge_rbf, W_up0, W_up1, M1, M2, M3, M4, W_lin0, W_lin1, Wsc0, Wsc1, Wc0, Wc1, WB0, WB1, gamma0, beta0, gamma1):
        import jax, jax.numpy as jnp
        import numpy as np
        N, E, C, R, HID = (6250, 62500, 64, 16, 64)
        n = h.shape[0]
        h0 = h[:, :C]
        h1 = h[:, C:].reshape(n, C, 3)
        up0 = h0 @ W_up0
        up1 = jnp.einsum('ncx,cd->ndx', h1, W_up1)
        r = jax.nn.silu(edge_rbf @ M1)
        r = jax.nn.silu(r @ M2)
        r = jax.nn.silu(r @ M3)
        tpw = (r @ M4).reshape(-1, 4, C)
        snd, rcv = (edge_index[0], edge_index[1])
        x0 = up0[snd]
        x1 = up1[snd]
        sh0 = edge_sh[:, 0]
        sh1 = edge_sh[:, 1:]
        inv3 = 1.0 / jnp.sqrt(jnp.float32(3.0))
        m0e = tpw[:, 0] * x0 * sh0[:, None] + tpw[:, 3] * jnp.einsum('ecx,ex->ec', x1, sh1) * inv3
        m1e = tpw[:, 1][:, :, None] * x0[:, :, None] * sh1[:, None, :] + tpw[:, 2][:, :, None] * x1 * sh0[:, None, None]
        msg0 = jax.ops.segment_sum(m0e, rcv, num_segments=n)
        msg1 = jax.ops.segment_sum(m1e, rcv, num_segments=n)
        A0 = msg0 @ W_lin0
        A1 = jnp.einsum('ncx,cd->ndx', msg1, W_lin1)
        sc0 = h0 @ Wsc0
        sc1 = jnp.einsum('ncx,cd->ndx', h1, Wsc1)
        vv = jnp.sum(A1 * A1, -1)
        B0 = Wc0[:, 0] * A0 + Wc0[:, 1] * A0 * A0 + Wc0[:, 2] * vv + Wc0[:, 3] * A0 ** 3 + Wc0[:, 4] * A0 * vv
        B1 = (Wc1[:, 0] + Wc1[:, 1] * A0 + Wc1[:, 2] * A0 * A0 + Wc1[:, 3] * vv)[..., None] * A1
        o0 = B0 @ WB0 + sc0
        o1 = jnp.einsum('ncx,cd->ndx', B1, WB1) + sc1
        eps = jnp.float32(1e-05)
        mu = jnp.mean(o0, 0)
        xc = o0 - mu
        var = jnp.mean(xc * xc, 0)
        n0 = xc * jax.lax.rsqrt(var + eps) * gamma0 + beta0
        nrm1 = jnp.mean(jnp.sum(o1 * o1, -1) / 3.0, 0)
        n1 = o1 * (jax.lax.rsqrt(nrm1 + eps) * gamma1)[None, :, None]
        return jnp.concatenate([n0, n1.reshape(n, 3 * C)], -1)

    def _L1_gnn_ref(features, src, dst, W_src, gamma, beta):
        import jax, jax.numpy as jnp
        import numpy as np
        N_NODES = 8192
        N_EDGES = 131072
        HEADS = 4
        HEAD_DIM = 64
        DIM = 256
        BN_EPS = 1e-05
        n = features.shape[0]
        feat_src = (features @ W_src).reshape(n, HEADS, HEAD_DIM)
        msgs = feat_src[src]
        sums = jax.ops.segment_sum(msgs, dst, num_segments=n)
        deg = jax.ops.segment_sum(jnp.ones((msgs.shape[0],), dtype=features.dtype), dst, num_segments=n)
        rst = sums / jnp.maximum(deg, 1.0)[:, None, None]
        rst = rst + features.reshape(n, HEADS, HEAD_DIM)
        x = rst.reshape(n, DIM)
        mean = jnp.mean(x, axis=0)
        var = jnp.mean(jnp.square(x - mean), axis=0)
        x = (x - mean) * jax.lax.rsqrt(var + BN_EPS) * gamma + beta
        return jax.nn.relu(x)

    def _L2_gnn_ref(x, edge_index, edge_attr, W, W_e, att_src, att_dst, att_edge, bias, gamma, beta):
        import jax, jax.numpy as jnp
        import numpy as np
        N, E = (6250, 100000)
        HID, EDIM, HEADS = (256, 64, 8)
        C = HID // HEADS
        NEG_SLOPE = 0.2
        LN_EPS = 1e-05

        def _gat_block(x, edge_index, edge_attr, W, W_e, att_src, att_dst, att_edge, bias, gamma, beta):
            n = x.shape[0]
            src, dst = (edge_index[0], edge_index[1])
            xp = (x @ W).reshape(n, HEADS, C)
            a_src = jnp.einsum('nhc,hc->nh', xp, att_src)
            a_dst = jnp.einsum('nhc,hc->nh', xp, att_dst)
            ep = (edge_attr @ W_e).reshape(-1, HEADS, C)
            a_edge = jnp.einsum('ehc,hc->eh', ep, att_edge)
            alpha = a_src[src] + a_dst[dst] + a_edge
            alpha = jax.nn.leaky_relu(alpha, NEG_SLOPE)
            m = jax.ops.segment_max(alpha, dst, num_segments=n)
            m = jnp.where(jnp.isfinite(m), m, 0.0)
            ea = jnp.exp(alpha - m[dst])
            den = jax.ops.segment_sum(ea, dst, num_segments=n)
            attn = ea / (den[dst] + 1e-16)
            msg = xp[src] * attn[:, :, None]
            out = jax.ops.segment_sum(msg, dst, num_segments=n)
            h = out.reshape(n, HEADS * C) + bias
            y = x + h
            mu = jnp.mean(y, axis=-1, keepdims=True)
            var = jnp.var(y, axis=-1, keepdims=True)
            return (y - mu) * jax.lax.rsqrt(var + LN_EPS) * gamma + beta
        return _gat_block(x, edge_index, edge_attr, W, W_e, att_src, att_dst, att_edge, bias, gamma, beta)

    def _L3_gnn_ref(x, edge_index, W, att_src, att_dst, bias, gamma, beta):
        import jax, jax.numpy as jnp
        import numpy as np
        N, E = (6250, 100000)
        IN, H, C = (256, 8, 32)
        NEG_SLOPE = 0.2
        EPS = 1e-05
        n = x.shape[0]
        xl = (x @ W).reshape(n, H, C)
        a_src = jnp.einsum('nhc,hc->nh', xl, att_src)
        a_dst = jnp.einsum('nhc,hc->nh', xl, att_dst)
        loops = jnp.arange(n, dtype=edge_index.dtype)
        src = jnp.concatenate([edge_index[0], loops])
        dst = jnp.concatenate([edge_index[1], loops])
        logits = jax.nn.leaky_relu(a_src[src] + a_dst[dst], NEG_SLOPE)
        seg_max = jax.ops.segment_max(logits, dst, num_segments=n)
        ex = jnp.exp(logits - seg_max[dst])
        denom = jax.ops.segment_sum(ex, dst, num_segments=n)
        alpha = ex / denom[dst]
        msgs = xl[src] * alpha[:, :, None]
        out = jax.ops.segment_sum(msgs, dst, num_segments=n).reshape(n, H * C) + bias
        mu = jnp.mean(out, axis=-1, keepdims=True)
        var = jnp.var(out, axis=-1, keepdims=True)
        return (out - mu) / jnp.sqrt(var + EPS) * gamma + beta
    edge_index = jnp.stack([src, dst])
    h = jnp.maximum(_layernorm(x, axis=-1), 0.0)
    x = x + _L0_gnn_ref(h, edge_index, edge_attr_4, edge_attr_16, L0_gnn_W_up0, L0_gnn_W_up1, L0_gnn_M1, L0_gnn_M2, L0_gnn_M3, L0_gnn_M4, L0_gnn_W_lin0, L0_gnn_W_lin1, L0_gnn_Wsc0, L0_gnn_Wsc1, L0_gnn_Wc0, L0_gnn_Wc1, L0_gnn_WB0, L0_gnn_WB1, L0_gnn_gamma0, L0_gnn_beta0, L0_gnn_gamma1)
    h = jnp.maximum(_layernorm(x, axis=-1), 0.0)
    x = x + _L1_gnn_ref(h, src, dst, L1_gnn_W_src, L1_gnn_gamma, L1_gnn_beta)
    h = jnp.maximum(_layernorm(x, axis=-1), 0.0)
    x = x + _L2_gnn_ref(h, edge_index, edge_attr_64, L2_gnn_W, L2_gnn_W_e, L2_gnn_att_src, L2_gnn_att_dst, L2_gnn_att_edge, L2_gnn_bias, L2_gnn_gamma, L2_gnn_beta)
    h = jnp.maximum(_layernorm(x, axis=-1), 0.0)
    x = x + _L3_gnn_ref(h, edge_index, L3_gnn_W, L3_gnn_att_src, L3_gnn_att_dst, L3_gnn_bias, L3_gnn_gamma, L3_gnn_beta)
    return x

_drawn_inputs = setup_inputs


def setup_inputs(seed=0):
    import zlib

    import numpy as np

    out = dict(_drawn_inputs(seed))
    spreads = {'L0_gnn_gamma0': (1.0, 0.2),
     'L0_gnn_beta0': (0.0, 0.317),
     'L0_gnn_gamma1': (1.0, 0.2),
     'L1_gnn_gamma': (1.0, 0.2),
     'L1_gnn_beta': (0.0, 0.1),
     'L2_gnn_bias': (0.0, 0.1),
     'L2_gnn_gamma': (1.0, 0.2),
     'L2_gnn_beta': (0.0, 0.1),
     'L3_gnn_bias': (0.0, 0.1),
     'L3_gnn_gamma': (1.0, 0.2),
     'L3_gnn_beta': (0.0, 0.1)}
    factors = {'edge_attr_64': 5.255,
     'L2_gnn_W_e': 5.193,
     'L2_gnn_att_src': 5.5,
     'L2_gnn_att_dst': 8.0,
     'L2_gnn_att_edge': 5.029,
     'L3_gnn_att_dst': 3.285}
    for name, (base, spread) in spreads.items():
        noise = np.random.default_rng([zlib.crc32(name.encode()), seed]).standard_normal(out[name].shape)
        drawn = base * np.exp(spread * noise) if base else spread * noise
        out[name] = jnp.asarray(drawn.astype(out[name].dtype))
    for name, factor in factors.items():
        out[name] = (out[name] * factor).astype(out[name].dtype)
    return out
```

```python
from contextlib import ExitStack

import numpy as np
import concourse.bass as bass
from concourse import mybir

F32 = mybir.dt.float32
BF16 = mybir.dt.bfloat16
I32 = mybir.dt.int32
ALU = mybir.AluOpType
ACT = mybir.ActivationFunctionType
AX = mybir.AxisListType
DVE = mybir.EngineType.DVE
PE = mybir.EngineType.PE
ds = bass.ds

P = 125
N, E, D = 6250, 106250, 256
NT, ET = N // P, E // P
ST = ET + NT
U = 10
NB = ST // U
EB = ET // U
C = 64
H, CH = 8, 32
AW = D + 2 * H
CK = 10
CE, CT = E // CK, ET // CK
FAR = 1.0e6
LOW = -1.0e38
EPS = 1e-5


class Count:

    def __init__(self, sem):
        self.sem, self.base, self.n = sem, 0, 0

    def inc(self, ins, by=1):
        ins.then_inc(self.sem, by)
        self.n += by
        return ins

    def value(self):
        return self.base + self.n

    def enter(self, i, per):
        self.outer = self.base + self.n
        self.base, self.n, self.per = self.outer + i * per, 0, per

    def leave(self, times):
        assert self.n == self.per, (self.n, self.per)
        self.base, self.n = self.outer + times * self.per, 0


def scope(nc, sems, gathers=()):
    es = ExitStack()
    got = {s: es.enter_context(nc.semaphore(s)) for s in sems}

    def clear():
        ids = sorted(h.num for h in got.values())
        start = ids[0]
        for a, b in zip(ids, ids[1:] + [None]):
            if b != a + 1:
                nc.all_engine_barrier(sems_to_clear=range(start, a + 1))
                start = b

    es.callback(clear)
    return es, got | dict(gathers)


def pairs(eng, times, body):
    for b in range(2):
        body(b, b, 0)
    with eng.Fori(1, times // 2) as i:
        for b in range(2):
            body(i * 2 + b, b, i)
    if times % 2:
        body(times - 1, 0, times // 2)


def ends(eng, times, body):
    body(0, 0, 0, True)
    body(1, 1, 0, True)
    with eng.Fori(1, times // 2 - 1) as i:
        body(i * 2, 0, i, True)
        body(i * 2 + 1, 1, i, True)
    body(times - 2, 0, times // 2 - 1, True)
    body(times - 1, 1, times // 2 - 1, False)


def skewed(eng, times, ahead, behind):
    ahead(0, 0, 0)
    for t in range(1, 4):
        ahead(t, t % 2, t // 2)
        behind(t - 1, (t - 1) % 2, (t - 1) // 2)
    with eng.Fori(2, times // 2) as i:
        ahead(i * 2, 0, i)
        behind(i * 2 - 1, 1, i - 1)
        ahead(i * 2 + 1, 1, i)
        behind(i * 2, 0, i)
    behind(times - 1, (times - 1) % 2, (times - 1) // 2)


def later(i):
    return not isinstance(i, int) or i > 0


class Net:
    pass


def tiles(ap):
    return ap.rearrange("(t p) f -> p t f", p=P)


def prepare(nc, k):
    names = ["ld", "pool", "cast", "tr", "ev", "bc", "cmp", "red", "jw", "tb", "gx", "trx", "st", "v", "row",
             "rt", "rd"]
    es, s = scope(nc, ["prep_" + n for n in names], [("prep_gat", k.gathered.pop())])
    with es:
        S = {n: s["prep_" + n] for n in names + ["gat"]}

        def sb(name, shape, dt=F32):
            return es.enter_context(nc.sbuf_tensor(name, shape, dt))

        Q = ET // U
        nat = sb("prep_nat", [Q, 2, U, P], I32)
        natf = sb("prep_natf", [Q, 2, U, P])
        dstf = sb("prep_dstf", [P, ET])
        first = sb("prep_first", [P, P])
        last = sb("prep_last", [P, P])
        thr = sb("prep_thr", [P, 1])
        ioti = sb("prep_ioti", [P, 128], I32)
        thri = sb("prep_thri", [P, 1], I32)
        pi = sb("prep_pi", [P, 1], I32)
        cmp = sb("prep_cmp", [NT, 2, ET])
        cnt = sb("prep_cnt", [NT, 2])
        jb = sb("prep_jb", [P, ET])
        tj = sb("prep_tj", [NT, 1])
        tji = k.tile_of
        base = sb("prep_base", [NT, 1])
        ok = sb("prep_ok", [NT, 1])
        gx = sb("prep_gx", [NT, 2, P], I32)
        gxf = sb("prep_gxf", [NT, 2, P])
        rbx = sb("prep_rbx", [NT, P * 16])
        shx = sb("prep_shx", [NT, P * 4])
        jrow = sb("prep_jrow", [1, NT], I32)
        Z = ST // 9
        rows = sb("prep_rows", [Z, 9, P])
        ps = [es.enter_context(nc.psum_tensor(f"prep_ps{i}", [P, 512], F32)) for i in range(8)]
        block = es.enter_context(nc.Block())

        @block.sync
        def _(sp):
            sp.dma_start(nat[:, 0], k.src.rearrange("(q r p) -> q r p", r=U, p=P)).then_inc(S["ld"], 16)
            sp.dma_start(nat[:, 1], k.dst.rearrange("(q r p) -> q r p", r=U, p=P)).then_inc(S["ld"], 16)
            sp.dma_start(k.x[:, :, :], tiles(k.x_in)).then_inc(S["st"], 16)
            sp.wait_ge(S["gat"], 64)
            sp.dma_start(k.rbf_extra, rbx[:, :]).then_inc(S["st"], 16)
            sp.dma_start(k.sh_extra, shx[:, :]).then_inc(S["st"], 16)
            sp.wait_ge(S["rd"], 3)
            sp.dma_start(k.dst_rows.rearrange("(m q) p -> q m p", q=Z), rows[:, :, :]).then_inc(S["st"], 16)
            sp.wait_ge(S["st"], 64)

        @block.gpsimd
        def _(g):
            c = Count(S["pool"])
            c.inc(g.memset(k.ident[:, :], 0.0))
            c.inc(g.memset(k.ones[:, :], 1.0))
            c.inc(g.memset(first[:, :], 0.0))
            c.inc(g.memset(last[:, :], 0.0))
            c.inc(g.iota(ioti[:, :], pattern=[[1, 128]], base=0, channel_multiplier=0))
            c.inc(g.iota(thri[:, :], pattern=[[0, 1]], base=0, channel_multiplier=P))
            c.inc(g.iota(jrow[:, :], pattern=[[1, NT]], base=0, channel_multiplier=0))
            c.inc(g.iota(pi[:, :], pattern=[[0, 1]], base=0, channel_multiplier=1))
            g.wait_ge(c.sem, 4)
            c.inc(g.affine_select(out=k.ident[:, :], in_=k.ident[:, :], compare_op=ALU.not_equal, fill=1.0,
                                  base=0, pattern=[[-1, 128]], channel_multiplier=1))
            c.inc(g.affine_select(out=first[:, :], in_=first[:, :], compare_op=ALU.not_equal, fill=1.0,
                                  base=0, pattern=[[0, P]], channel_multiplier=1))
            c.inc(g.affine_select(out=last[:, :], in_=last[:, :], compare_op=ALU.not_equal, fill=1.0,
                                  base=1 - P, pattern=[[0, P]], channel_multiplier=1))
            g.wait_ge(S["tb"], 1)
            at = bass.IndirectOffsetOnAxis(ap=tji[:, :], axis=0)
            for out, table in ((gx[:, 0, :], k.src.rearrange("(t p) -> t p", p=P)),
                               (gx[:, 1, :], k.dst.rearrange("(t p) -> t p", p=P)),
                               (rbx[:, :], k.rbf.rearrange("(t p) f -> t (p f)", p=P)),
                               (shx[:, :], k.sh.rearrange("(t p) f -> t (p f)", p=P))):
                g.indirect_dma_start(out, None, table, at).then_inc(S["gat"], 16)

        @block.tensor
        def _(pe):
            pe.wait_ge(S["pool"], 11)
            pe.wait_ge(S["cast"], 2)
            for a in range(2):
                for r in range(U):
                    ins = nc.tensor.transpose(ps[2 * a + r // 5][:, (r % 5) * Q:(r % 5 + 1) * Q],
                                              natf[:, a, r, :], k.ident[0:Q, 0:Q])
            ins.then_inc(S["tr"], 1)
            pe.wait_ge(S["ev"], 4)
            for a, pick in enumerate((first, last)):
                for hf in range(2):
                    ins = nc.tensor.matmul(ps[4 + 2 * a + hf][:, 0:ET // 2], pick[:, :],
                                           dstf[:, hf * (ET // 2):(hf + 1) * (ET // 2)], start=True, stop=True)
            ins.then_inc(S["bc"], 1)
            pe.wait_ge(S["cmp"], 4)
            for hf in range(2):
                ins = nc.tensor.matmul(ps[hf][:, 0:ET // 2], k.ones[0:NT, 0:P],
                                       cmp[:, 0, hf * (ET // 2):(hf + 1) * (ET // 2)], start=True, stop=True)
            ins.then_inc(S["jw"], 1)
            pe.wait_ge(S["gx"], 2)
            for a in range(2):
                nc.tensor.transpose(ps[2][:, a * NT:(a + 1) * NT], gxf[:, a, :], k.ident[0:NT, 0:NT])
            nc.tensor.transpose(ps[3][0:1, 0:NT], tj[:, :], k.ident[0:NT, 0:NT]).then_inc(S["trx"], 1)
            pe.wait_ge(S["row"], 7)
            for m in range(9):
                ins = nc.tensor.transpose(ps[4 + m // 4][0:Z, (m % 4) * P:(m % 4 + 1) * P],
                                          k.dst_in[:, m * Z:(m + 1) * Z], k.ident[0:P, 0:P])
            ins.then_inc(S["rt"], 1)

        @block.vector
        def _(v):
            v.wait_ge(S["ld"], 32)
            nc.vector.tensor_copy(natf[:, 0], nat[:, 0]).then_inc(S["cast"], 1)
            nc.vector.tensor_copy(natf[:, 1], nat[:, 1]).then_inc(S["cast"], 1)
            v.wait_ge(S["pool"], 8)
            nc.vector.tensor_copy(k.iota[:, :], ioti[:, 0:P]).then_inc(S["v"], 1)
            nc.vector.tensor_copy(thr[:, :], thri[:, :]).then_inc(S["v"], 1)
            v.wait_ge(S["tr"], 1)
            for hf in range(2):
                r5 = slice(5 * hf, 5 * hf + 5)

                def by_tile(t):
                    return t[:, 0:ET].rearrange("p (q r) -> p r q", r=U)[:, r5, :]

                def of(n):
                    return ps[n][:, 0:5 * Q].rearrange("p (r q) -> p r q", q=Q)

                nc.vector.tensor_copy(by_tile(k.src_of), of(hf)).then_inc(S["ev"], 1)
                nc.vector.tensor_copy(by_tile(dstf), of(2 + hf)).then_inc(S["ev"], 1)
            v.wait_ge(S["ev"], 4)
            nc.vector.tensor_copy(k.lane[:, :], pi[:, :]).then_inc(S["row"], 1)
            v.wait_ge(S["bc"], 1)
            v.wait_ge(S["v"], 2)
            for a in range(2):
                for hf in range(2):
                    nc.vector.tensor_scalar(cmp[:, a, hf * (ET // 2):(hf + 1) * (ET // 2)],
                                            ps[4 + 2 * a + hf][0:NT, 0:ET // 2], thr[0:NT, 0:1], None,
                                            ALU.is_lt).then_inc(S["cmp"], 1)
            v.wait_ge(S["cmp"], 4)
            nc.vector.tensor_reduce(cnt[:, :], cmp[:, :, :], AX.X, ALU.add).then_inc(S["red"], 1)
            v.wait_ge(S["red"], 1)
            nc.vector.tensor_scalar(tj[:, :], cnt[:, 1:2], float(ET - 1), None, ALU.min).then_inc(S["red"], 1)
            nc.vector.tensor_tensor(ok[:, :], cnt[:, 0:1], cnt[:, 1:2], ALU.is_le).then_inc(S["red"], 1)
            v.wait_ge(S["red"], 3)
            nc.vector.tensor_copy(tji[:, :], tj[:, :]).then_inc(S["tb"], 1)
            nc.vector.scalar_tensor_tensor(out=base[:, :], in0=ok[:, :], scalar=FAR, in1=thr[0:NT, :],
                                           op0=ALU.mult, op1=ALU.add).then_inc(S["red"], 1)
            v.wait_ge(S["jw"], 1)
            for hf in range(2):
                nc.vector.tensor_scalar(jb[:, hf * (ET // 2):(hf + 1) * (ET // 2)], ps[hf][:, 0:ET // 2],
                                        -1.0, float(NT - 1), ALU.mult, ALU.add).then_inc(S["red"], 1)
            v.wait_ge(S["red"], 6)
            nc.vector.tensor_copy(k.node_tile[:, 0:ET], jb[0:1, :]).then_inc(S["row"], 1)
            nc.vector.tensor_copy(k.node_tile[:, ET:ST], jrow[:, :]).then_inc(S["row"], 1)
            nc.vector.scalar_tensor_tensor(out=k.dst_in[:, 0:ET], in0=jb[:, :], scalar=-float(P),
                                           in1=dstf[:, :], op0=ALU.mult, op1=ALU.add).then_inc(S["row"], 1)
            v.wait_ge(S["gat"], 64)
            nc.vector.tensor_copy(gxf[:, 0], gx[:, 0]).then_inc(S["gx"], 1)
            nc.vector.tensor_scalar(gxf[:, 1], gx[:, 1], base[:, 0:1], None, ALU.subtract).then_inc(S["gx"], 1)
            v.wait_ge(S["trx"], 1)
            nc.vector.tensor_copy(k.src_of[:, ET:ST], ps[2][:, 0:NT]).then_inc(S["row"], 1)
            nc.vector.tensor_copy(k.dst_in[:, ET:ST], ps[2][:, NT:2 * NT]).then_inc(S["row"], 1)
            nc.vector.tensor_copy(k.extra_at[:, :], ps[3][0:1, 0:NT]).then_inc(S["row"], 1)
            v.wait_ge(S["rt"], 1)
            for n, (m0, m1) in enumerate(((0, 4), (4, 8), (8, 9))):
                nc.vector.tensor_copy(rows[:, m0:m1, :], ps[4 + n][0:Z, 0:(m1 - m0) * P].rearrange(
                    "q (m p) -> q m p", p=P)).then_inc(S["rd"], 1)


def row_stats(nc, k, tag, src, width):
    es, s = scope(nc, [tag + n for n in ("st", "ag", "ep", "sq", "rc")])
    with es:
        raw = es.enter_context(nc.sbuf_tensor(tag + "raw", [P, NT, 6], F32))
        mv = es.enter_context(nc.sbuf_tensor(tag + "mv", [P, NT, 2], F32))
        std = es.enter_context(nc.sbuf_tensor(tag + "std", [P, NT], F32))
        block = es.enter_context(nc.Block())

        @block.vector
        def _(v):
            for j in range(NT):
                nc.vector.bn_stats(raw[:, j, :], src[:, j, 0:width]).then_inc(s[tag + "st"], 1)
            for j in range(NT):
                v.wait_ge(s[tag + "st"], j + 1)
                nc.vector.bn_aggr(mv[:, j, :], raw[:, j, :]).then_inc(s[tag + "ag"], 1)
            v.wait_ge(s[tag + "ag"], NT)
            nc.vector.tensor_copy(k.mean[:, :], mv[:, :, 0]).then_inc(s[tag + "ep"], 1)
            nc.vector.tensor_scalar(k.rstd[:, :], mv[:, :, 1], EPS, None, ALU.add).then_inc(s[tag + "ep"], 1)
            v.wait_ge(s[tag + "sq"], 1)
            nc.vector.reciprocal(k.rstd[:, :], std[:, :]).then_inc(s[tag + "rc"], 1)
            v.wait_ge(s[tag + "rc"], 1)
            nc.vector.scalar_tensor_tensor(out=k.shift[:, :], in0=k.mean[:, :], scalar=-1.0, in1=k.rstd[:, :],
                                           op0=ALU.mult, op1=ALU.mult).then_inc(s[tag + "rc"], 1)
            v.wait_ge(s[tag + "rc"], 2)

        @block.scalar
        def _(a):
            a.wait_ge(s[tag + "ep"], 2)
            nc.scalar.activation(std[:, :], k.rstd[:, :], ACT.Sqrt).then_inc(s[tag + "sq"], 1)


def project(nc, k, tag, load_weights, weight_loads, outputs, width, split=False, att=None, self_score=False):
    names = ["w", "h", "tr", "ht", "mm", "sc", "o", "sum", "fold", "st0", "st1", "kp"]
    es, s = scope(nc, [tag + n for n in names])
    with es:
        S = {n: s[tag + n] for n in names}

        def sb(name, shape, dt=F32):
            return es.enter_context(nc.sbuf_tensor(tag + name, shape, dt))

        w = sb("w", [128, 2, width // 2 if split else width])
        h = sb("hh", [P, 2, D])
        hT = sb("hT", [128, 2, 2, P])
        ow = width + (2 * H if self_score else 0)
        o = sb("o", [P, 2, ow])
        if att:
            vec = sb("vec", [128, 2, D])
            prod = sb("prod", [128, 2, 2, D])
        psT = es.enter_context(nc.psum_tensor(tag + "psT", [128, 2, 512], F32))
        psO = es.enter_context(nc.psum_tensor(tag + "psO", [P, 2, 512], F32))
        block = es.enter_context(nc.Block())
        stores = [S["st0"], S["st1"]]

        if split:
            @block.gpsimd
            def _(g):
                g.memset(w[:, :, :], 0.0).then_inc(S["fold"], 1)

        @block.sync
        def _(sp):
            if split:
                sp.wait_ge(S["fold"], 1)
            load_weights(sp, w, S["w"])
            if att:
                for q in range(2):
                    sp.dma_start(vec[:, q, :], att[q].rearrange("h c -> (h c)").partition_broadcast(128)
                                 ).then_inc(S["w"], 16)

            def store(t, b, i):
                sp.wait_ge(S["o"], t + 1)
                for table, off, wd in outputs:
                    sp.dma_start(table[ds(t * P, P), :], o[:, b, off:off + wd]).then_inc(stores[b], 16)

            pairs(sp, NT, store)
            for b in range(2):
                sp.wait_ge(stores[b], 16 * len(outputs) * (NT // 2))

        @block.scalar
        def _(a):
            def work(t, b, i):
                if later(i):
                    a.wait_ge(S["tr"], t - 1)
                hv = h[:, b, :]
                xv = k.x[:, ds(t, 1), :].rearrange("p a d -> p (a d)")
                sc, sh = k.rstd[:, ds(t, 1)], k.shift[:, ds(t, 1)]
                if split:
                    nc.scalar.activation(hv[:, 0:C], xv[:, 0:C], ACT.Relu, bias=sh, scale=sc)
                    nc.scalar.activation(hv[:, C:D].rearrange("p (x c) -> p x c", x=3),
                                         xv[:, C:D].rearrange("p (c x) -> p x c", x=3), ACT.Relu, bias=sh,
                                         scale=sc).then_inc(S["h"], 1)
                else:
                    nc.scalar.activation(hv, xv, ACT.Relu, bias=sh, scale=sc).then_inc(S["h"], 1)

            def evacuate(t, b, i):
                a.wait_ge(S["mm"], t + 1)
                if later(i):
                    a.wait_ge(stores[b], i * (16 * len(outputs)))
                    if att:
                        a.wait_ge(S["kp"], t - 1)
                done = S["sc" if self_score else "o"]
                if split:
                    pv = psO[:, b, :].rearrange("p (k q c) -> p q k c", k=2, q=2)
                    ov = o[:, b, 0:2 * D].rearrange("p (q k c) -> p q k c", k=2, q=2)
                    nc.scalar.activation(ov[:, 0], pv[:, 0], ACT.Copy)
                    nc.scalar.activation(ov[:, 1], pv[:, 1], ACT.Copy).then_inc(done, 1)
                else:
                    nc.scalar.activation(o[:, b, 0:width], psO[:, b, 0:width], ACT.Copy).then_inc(done, 1)

            skewed(a, NT, work, evacuate)

        @block.tensor
        def _(pe):
            pe.wait_ge(S["w"], 16 * (weight_loads + (2 if att else 0)))
            if att:
                pe.wait_ge(S["fold"], 2)

            def turn(t, b, i):
                pe.wait_ge(S["h"], t + 1)
                if later(i):
                    pe.wait_ge(S["ht"], t - 1)
                for q in range(2):
                    ins = nc.tensor.transpose(psT[:, b, q * P:(q + 1) * P], h[:, b, q * 128:(q + 1) * 128],
                                              k.ident[0:P, 0:P])
                ins.then_inc(S["tr"], 1)

            def multiply(t, b, i):
                pe.wait_ge(S["ht"], t + 1)
                if later(i):
                    pe.wait_ge(S["sc" if self_score else "o"], t - 1)
                for q in range(2):
                    if split:
                        ins = nc.tensor.matmul(psO[:, b, q * D:(q + 1) * D], hT[:, b, q, :], w[:, q, :],
                                               start=True, stop=True)
                    else:
                        ins = nc.tensor.matmul(psO[:, b, 0:width], hT[:, b, q, :], w[:, q, :],
                                               start=(q == 0), stop=(q == 1))
                ins.then_inc(S["mm"], 1)

            skewed(pe, NT, turn, multiply)

        @block.vector
        def _(v):
            if att:
                v.wait_ge(S["w"], 16 * (weight_loads + 2))
                for q in range(2):
                    for blk in range(2):
                        nc.vector.tensor_tensor(prod[:, blk, q, :], w[:, blk, 0:D], vec[:, q, :],
                                                ALU.mult).then_inc(S["sum"], 1)
                v.wait_ge(S["sum"], 4)
                for blk in range(2):
                    nc.vector.tensor_reduce(w[:, blk, D:D + 2 * H],
                                            prod[:, blk].rearrange("p q (h c) -> p (q h) c", c=CH),
                                            AX.X, ALU.add).then_inc(S["fold"], 1)

            def copy(t, b, i):
                v.wait_ge(S["tr"], t + 1)
                if later(i):
                    v.wait_ge(S["mm"], t - 1)
                nc.vector.tensor_copy(hT[:, b, :, :].rearrange("p q c -> p (q c)"),
                                      psT[:, b, 0:2 * P]).then_inc(S["ht"], 1)

            def own_score(t, b, i):
                v.wait_ge(S["sc"], t + 1)
                both = o[:, b, D + 3 * H:D + 4 * H]
                nc.vector.tensor_tensor(both, o[:, b, D:D + H], o[:, b, D + H:D + 2 * H],
                                        ALU.add).then_inc(S["sum"], 1)
                v.wait_ge(S["sum"], t + 5)
                nc.vector.scalar_tensor_tensor(out=o[:, b, D + 2 * H:D + 3 * H], in0=both, scalar=0.2, in1=both,
                                               op0=ALU.mult, op1=ALU.max).then_inc(S["o"], 1)

            def keep(t, b, i):
                v.wait_ge(S["o"], t + 1)
                w = 2 * H if self_score else H
                nc.vector.tensor_copy(k.recv[:, ds(t, 1), 0:w].rearrange("p a h -> p (a h)"),
                                      o[:, b, D + H:D + H + w]).then_inc(S["kp"], 1)

            def own(t, b, i):
                if self_score:
                    own_score(t, b, i)
                keep(t, b, i)

            if att:
                skewed(v, NT, copy, own)
            else:
                pairs(v, NT, copy)


def aggregate(nc, k, tag, table, weights=None, R=0, degree=False):
    names = ["idx0", "idx1", "lw0", "lw1", "sel", "msg", "mm", "acc", "wt", "ww", "cl", "go"]
    es, s = scope(nc, [tag + n for n in names], [(tag + "gat0", k.gathered.pop()), (tag + "gat1", k.gathered.pop())])
    with es:
        S = {n: s[tag + n] for n in names + ["gat0", "gat1"]}

        def sb(name, shape, dt=F32):
            return es.enter_context(nc.sbuf_tensor(tag + name, shape, dt))

        def pt(name, shape):
            return es.enter_context(nc.psum_tensor(tag + name, shape, F32))

        att = weights is not None
        W = D + R + (1 if degree else 0)
        idx = [sb(f"idx{b}", [P, U], I32) for b in range(2)]
        rows = [sb(f"rows{b}", [P, U, D]) for b in range(2)]
        sel = [sb(f"sel{b}", [P, U, P]) for b in range(2)]
        if att:
            msg = [sb(f"msg{b}", [P, U, AW]) for b in range(2)]
            wT = [sb(f"wT{b}", [R, U, P]) for b in range(2)]
            psW = pt("psW", [P, 2, 512])
        psA = pt("psA", [P, 4, 512])
        block = es.enter_context(nc.Block())
        g_sem, i_sem, l_sem = [S["gat0"], S["gat1"]], [S["idx0"], S["idx1"]], [S["lw0"], S["lw1"]]

        @block.sync
        def _(sp):
            def load(t, b, i):
                if later(i):
                    sp.wait_ge(g_sem[b], i * (16 * U))
                sp.dma_start(idx[b][:, :], k.src_of[:, ds(t * U, U)]).then_inc(i_sem[b], 16)
                if att:
                    if later(i):
                        sp.wait_ge(S["wt"], t - 1)
                    last = (weights[0][ds(t * U, U)] if not isinstance(t, int) or t < EB else
                            weights[1][(t - EB) * U:(t - EB + 1) * U])
                    sp.dma_start(wT[b][:, :, :], last.rearrange("t r e -> r t e")).then_inc(l_sem[b], 16)

            if att:
                load(0, 0, 0)
                load(1, 1, 0)
                with sp.Fori(1, EB // 2) as i:
                    load(i * 2, 0, i)
                    load(i * 2 + 1, 1, i)
                for t in range(EB // 2 * 2, NB):
                    load(t, t % 2, t // 2)
            else:
                pairs(sp, NB, load)

        @block.gpsimd
        def _(g):
            def gather(t, b, i):
                g.wait_ge(i_sem[b], i * 16 + 16)
                if later(i):
                    if att:
                        g.wait_ge(S["msg"], t - 1)
                    else:
                        g.wait_ge(S["mm"], (t - 1) * U)
                g.sem_inc(S["go"], 1)
                for u in range(U):
                    g.indirect_dma_start(rows[b][:, u, :], None, table,
                                         bass.IndirectOffsetOnAxis(ap=idx[b][:, u:u + 1], axis=0)
                                         ).then_inc(g_sem[b], 16)

            pairs(g, NB, gather)

        @block.scalar
        def _(a):
            if att:
                def place(t, b, i):
                    a.wait_ge(S["wt"], t + 1)
                    if later(i):
                        a.wait_ge(S["mm"], (t - 1) * U)
                    nc.scalar.activation(msg[b][:, :, D:D + R], psW[:, b, 0:U * R].rearrange(
                        "p (u r) -> p u r", r=R), ACT.Copy).then_inc(S["ww"], 1)

                pairs(a, NB, place)

        @block.tensor
        def _(pe):
            def turn(t, b, i):
                pe.wait_ge(l_sem[b], i * 16 + 16)
                if later(i):
                    pe.wait_ge(S["ww"], t - 1)
                pe.sem_inc(S["go"], 1)
                for u in range(U):
                    ins = nc.tensor.transpose(psW[:, b, u * R:(u + 1) * R], wT[b][:, u, :], k.ident[0:R, 0:R])
                ins.then_inc(S["wt"], 1)

            def multiply(t, b, i):
                pe.wait_ge(S["sel"], t + 1)
                if att:
                    pe.wait_ge(S["msg"], t + 1)
                else:
                    pe.wait_ge(g_sem[b], i * (16 * U) + 16 * U)
                for u in range(U):
                    if later(i) or b * U + u >= 4:
                        pe.wait_ge(S["acc"], t * U + (u - 3))
                    slot = psA[:, (b * U + u) % 4, :]
                    value = msg[b][:, u, 0:W] if att else rows[b][:, u, :]
                    ins = nc.tensor.matmul(slot[:, 0:(W if att else D)], sel[b][:, u, :], value,
                                           start=True, stop=True)
                    if degree:
                        ins = nc.tensor.matmul(slot[:, D:D + 1], sel[b][:, u, :], k.ones[0:P, 0:1],
                                               start=True, stop=True)
                    ins.then_inc(S["mm"], 1)

            if att:
                skewed(pe, NB, turn, multiply)
            else:
                pairs(pe, NB, multiply)

        @block.vector
        def _(v):
            nc.vector.memset(k.acc[:, :, 0:W], 0.0).then_inc(S["cl"], 1)

            def prepare_batch(t, b, i):
                if later(i):
                    v.wait_ge(S["mm"], (t - 1) * U)
                nc.vector.tensor_tensor(sel[b][:, :, :], k.iota[:, :].unsqueeze(1).broadcast_to([P, U, P]),
                                        k.dst_in[:, ds(t * U, U)].unsqueeze(2).broadcast_to([P, U, P]),
                                        ALU.is_equal).then_inc(S["sel"], 1)
                if att:
                    v.wait_ge(g_sem[b], i * (16 * U) + 16 * U)
                    v.wait_ge(S["ww"], t + 1)
                    for half in (slice(0, U // 2), slice(U // 2, U)):
                        ins = nc.vector.tensor_tensor(
                            msg[b][:, half, 0:D].rearrange("p u (h c) -> p u h c", c=CH),
                            rows[b][:, half, :].rearrange("p u (h c) -> p u h c", c=CH),
                            msg[b][:, half, D:D + H].unsqueeze(3).broadcast_to([P, U // 2, H, CH]), ALU.mult)
                    ins.then_inc(S["msg"], 1)

            def add(t, b, i):
                _, at = nc.values_load_multi_w_load_instructions(
                    k.node_tile[0:1, ds(t * U, U)], engines=[DVE], min_val=0, max_val=NT - 1)
                for u in range(U):
                    v.wait_ge(S["mm"], t * U + (u + 1))
                    if u == 0 and isinstance(t, int) and t == 0:
                        v.wait_ge(S["cl"], 1)
                    else:
                        v.wait_ge(S["acc"], t * U + u)
                    to = k.acc[:, ds(at[u], 1), 0:W].rearrange("p a d -> p (a d)")
                    nc.vector.tensor_tensor(to, to, psA[:, (b * U + u) % 4, 0:W], ALU.add).then_inc(S["acc"], 1)

            skewed(v, NB, prepare_batch, add)
            v.wait_ge(S["acc"], ST)
            if degree:
                nc.vector.tensor_copy(k.deg[:, :], k.acc[:, :, D]).then_inc(S["cl"], 1)
                v.wait_ge(S["cl"], 2)


def convolve(nc, k, tag):
    names = ["idx0", "idx1", "lw0", "lw1", "w", "wf", "sel", "sk", "msg", "mm", "acc",
             "rt", "rx", "m1", "a1", "m2", "a2", "m3", "a3", "tp", "cl", "go"]
    es, s = scope(nc, [tag + n for n in names], [(tag + "gat0", k.gathered.pop()), (tag + "gat1", k.gathered.pop())])
    QB = U // 2
    A, B = 3 * P, 2 * P
    with es:
        S = {n: s[tag + n] for n in names + ["gat0", "gat1"]}

        def sb(name, shape, dt=F32):
            return es.enter_context(nc.sbuf_tensor(tag + name, shape, dt))

        def pt(name, shape):
            return es.enter_context(nc.psum_tensor(tag + name, shape, F32))

        idx = [sb(f"idx{b}", [P, U], I32) for b in range(2)]
        rbf = [sb(f"rbf{b}", [P, U, 16]) for b in range(2)]
        sh = [sb(f"sh{b}", [P, U, 4]) for b in range(2)]
        rows = [sb(f"rows{b}", [P, U, D]) for b in range(2)]
        sel = [sb(f"sel{b}", [P, U, P]) for b in range(2)]
        m1 = sb("m1", [32, 128])
        m2 = sb("m2", [128, 128])
        m3 = sb("m3", [128, 128])
        m4 = sb("m4", [128, D])
        rT = sb("rT", [32, A + B])
        r1 = sb("r1", [128, A + B])
        r2 = sb("r2", [128, A + B])
        r3 = [sb(f"r3{b}", [128, A + B]) for b in range(2)]
        selk = sb("selk", [P, 2, 2, 4, P])
        prod = sb("prod", [P, 2, 2, 8, C])
        psM = pt("psM", [128, 2, 512])
        psT = pt("psT", [P, 2, 2, 512])
        psA = pt("psA", [P, 2, 512])
        block = es.enter_context(nc.Block())
        g_sem, i_sem, l_sem = [S["gat0"], S["gat1"]], [S["idx0"], S["idx1"]], [S["lw0"], S["lw1"]]

        @block.sync
        def _(sp):
            sp.wait_ge(S["wf"], 3)
            for o in (0, 1):
                for w, src, n in ((m1, k.w["M1"], 16), (m2, k.w["M2"], C), (m3, k.w["M3"], C)):
                    sp.dma_start(w[o * n:(o + 1) * n, o * C:(o + 1) * C], src).then_inc(S["w"], 16)
                sp.dma_start(m4[o * C:(o + 1) * C, :], k.w["M4"]).then_inc(S["w"], 16)

            def load(t, b, i):
                if later(i):
                    sp.wait_ge(g_sem[b], i * (16 * U))
                sp.dma_start(idx[b][:, :], k.src_of[:, ds(t * U, U)]).then_inc(i_sem[b], 16)
                if later(i):
                    sp.wait_ge(S["sk"], (t - 1) * QB)
                    sp.wait_ge(S["rt"], t - 1)
                    sp.sem_inc(S["go"], 1)
                if not isinstance(t, int) or t < EB:
                    f = tiles(k.rbf[ds(t * (U * P), U * P), :])
                    y = tiles(k.sh[ds(t * (U * P), U * P), :])
                else:
                    r = slice((t - EB) * U, (t - EB + 1) * U)
                    f = k.rbf_extra[r].rearrange("t (p f) -> p t f", p=P)
                    y = k.sh_extra[r].rearrange("t (p f) -> p t f", p=P)
                sp.dma_start(rbf[b][:, :, :], f).then_inc(l_sem[b], 16)
                sp.dma_start(sh[b][:, :, :], y).then_inc(l_sem[b], 16)

            load(0, 0, 0)
            load(1, 1, 0)
            with sp.Fori(1, EB // 2) as i:
                load(i * 2, 0, i)
                load(i * 2 + 1, 1, i)
            for t in range(EB // 2 * 2, NB):
                load(t, t % 2, t // 2)

        @block.gpsimd
        def _(g):
            for w in (m1, m2, m3):
                g.memset(w[:, :], 0.0).then_inc(S["wf"], 1)

            def gather(t, b, i):
                g.wait_ge(i_sem[b], i * 16 + 16)
                if later(i):
                    g.wait_ge(S["msg"], (t - 1) * QB)
                g.sem_inc(S["go"], 1)
                for u in range(U):
                    g.indirect_dma_start(rows[b][:, u, :], None, k.table,
                                         bass.IndirectOffsetOnAxis(ap=idx[b][:, u:u + 1], axis=0)
                                         ).then_inc(g_sem[b], 16)

            pairs(g, NB, gather)

        @block.scalar
        def _(a):
            def leave(n, out, src, act, free, freed):
                if free is not None:
                    a.wait_ge(S[free], freed)
                nc.scalar.activation(out[:, 0:A], src[:, 0, 0:A], act)
                nc.scalar.activation(out[:, A:A + B], src[:, 1, 0:B], act).then_inc(S[n], 1)

            def stage(q, t, b, i):
                first = isinstance(t, int) and t == 0
                if q == 0:
                    a.wait_ge(S["rt"], t + 1)
                    leave("rx", rT, psM[0:32], ACT.Copy, None if first else "m1", t)
                if q == 1:
                    a.wait_ge(S["m1"], t + 1)
                    leave("a1", r1, psM, ACT.Silu, None if first else "m2", t)
                if q == 2:
                    a.wait_ge(S["m2"], t + 1)
                    leave("a2", r2, psM, ACT.Silu, None if first else "m3", t)
                if q == 3:
                    a.wait_ge(S["m3"], t + 1)
                    leave("a3", r3[b], psM, ACT.Silu, "tp" if later(i) else None, (t - 1) * QB)

            def scale(t, b, i, q):
                if q == 0:
                    a.wait_ge(S["sel"], t + 1)
                    a.wait_ge(l_sem[b], i * 32 + 32)
                if later(i) or b * QB + q >= 2:
                    a.wait_ge(S["mm"], t * U + (2 * q - 2))
                par = (b * QB + q) % 2
                for u in range(2):
                    for y in range(4):
                        ins = nc.scalar.activation(selk[:, par, u, y, :], sel[b][:, 2 * q + u, :], ACT.Copy,
                                                   scale=sh[b][:, 2 * q + u, y:y + 1])
                ins.then_inc(S["sk"], 1)

            for q in range(4):
                stage(q, 0, 0, 0)
            scale(0, 0, 0, 0)

            def body(t, b, i, more):
                for q in range(QB):
                    if more and q < 4:
                        stage(q, t + 1, 1 - b, i + b)
                    if q < QB - 1:
                        scale(t, b, i, q + 1)
                    elif more:
                        scale(t + 1, 1 - b, i + b, 0)

            ends(a, NB, body)

        @block.tensor
        def _(pe):
            pe.wait_ge(S["w"], 16 * 8)
            pe.wait_ge(S["wf"], 4)

            def stage(q, t, b, i):
                first = isinstance(t, int) and t == 0
                if q == 0:
                    pe.wait_ge(l_sem[b], i * 32 + 32)
                    if not first:
                        pe.wait_ge(S["a3"], t)
                    for n in range(QB):
                        ins = nc.tensor.transpose(psM[0:32, n // 3, (n % 3) * P:(n % 3 + 1) * P],
                                                  rbf[b][:, 2 * n:2 * n + 2, :].rearrange("p u f -> p (u f)"),
                                                  k.ident[0:P, 0:P])
                    ins.then_inc(S["rt"], 1)
                else:
                    w, r, before, out = {1: (m1, rT, "rx", "m1"), 2: (m2, r1, "a1", "m2"),
                                         3: (m3, r2, "a2", "m3")}[q] if 1 <= q <= 3 else (None,) * 4
                    if w is None:
                        return
                    pe.wait_ge(S[before], t + 1)
                    nc.tensor.matmul(psM[:, 0, 0:A], w[:, :], r[:, 0:A], start=True, stop=True)
                    nc.tensor.matmul(psM[:, 1, 0:B], w[:, :], r[:, A:A + B], start=True,
                                     stop=True).then_inc(S[out], 1)

            def last_layer(t, b, i, q):
                if q == 0:
                    pe.wait_ge(S["a3"], t + 1)
                if later(i) or b * QB + q >= 2:
                    pe.wait_ge(S["msg"], t * QB + (q - 1))
                for u in range(2):
                    half = slice(u * C, u * C + C)
                    ins = nc.tensor.matmul(psT[:, (b * QB + q) % 2, u, 0:D], r3[b][half, q * P:(q + 1) * P],
                                           m4[half, :], start=True, stop=True)
                ins.then_inc(S["tp"], 1)

            def multiply(t, b, i, q):
                pe.wait_ge(S["msg"], t * QB + (q + 1))
                pe.wait_ge(S["sk"], t * QB + (q + 1))
                par = (b * QB + q) % 2
                for u in range(2):
                    if later(i) or b * U + 2 * q + u >= 2:
                        pe.wait_ge(S["acc"], t * U + (2 * q + u - 1))
                    out = psA[:, u, 0:D]
                    pr = prod[:, par, u, :, :]
                    nc.tensor.matmul(out, selk[:, par, u, 0, :], pr[:, 0:4, :].rearrange("p k c -> p (k c)"),
                                     start=True, stop=False)
                    for x in range(3):
                        ins = nc.tensor.matmul(out.rearrange("p (k c) -> p k c", k=4)[:, 0:x + 2:x + 1, :],
                                               selk[:, par, u, 1 + x, :], pr[:, 4 + x:8:3 - x, :],
                                               start=False, stop=(x == 2))
                    ins.then_inc(S["mm"], 1)

            for q in range(4):
                stage(q, 0, 0, 0)
            last_layer(0, 0, 0, 0)

            def body(t, b, i, more):
                for q in range(QB):
                    if more:
                        stage(q, t + 1, 1 - b, i + b)
                    if q < QB - 1:
                        last_layer(t, b, i, q + 1)
                    elif more:
                        last_layer(t + 1, 1 - b, i + b, 0)
                    multiply(t, b, i, q)

            ends(pe, NB, body)

        @block.vector
        def _(v):
            nc.vector.memset(k.acc[:, :, 0:D], 0.0).then_inc(S["cl"], 1)
            v.wait_ge(S["w"], 16 * 8)
            inv3 = float(1.0 / np.sqrt(np.float32(3.0)))
            nc.vector.tensor_scalar(m4[:, 3 * C:], m4[:, 3 * C:], inv3, None, ALU.mult).then_inc(S["wf"], 1)

            def select(t, b, i):
                if later(i):
                    v.wait_ge(S["sk"], (t - 1) * QB)
                nc.vector.tensor_tensor(sel[b][:, :, :], k.iota[:, :].unsqueeze(1).broadcast_to([P, U, P]),
                                        k.dst_in[:, ds(t * U, U)].unsqueeze(2).broadcast_to([P, U, P]),
                                        ALU.is_equal).then_inc(S["sel"], 1)

            def products(t, b, i, q):
                if q == 0:
                    v.wait_ge(g_sem[b], i * (16 * U) + 16 * U)
                v.wait_ge(S["tp"], t * QB + (q + 1))
                if later(i) or b * QB + q >= 2:
                    v.wait_ge(S["mm"], t * U + (2 * q - 2))
                par = (b * QB + q) % 2
                x = rows[b][:, 2 * q:2 * q + 2, :].rearrange("p u (k c) -> p u k c", c=C)
                tp = psT[:, par, :, 0:D].rearrange("p u (k c) -> p u k c", c=C)
                nc.vector.tensor_tensor(prod[:, par, :, 0:8:7, :], tp[:, :, 0:2, :],
                                        x[:, :, 0:1, :].broadcast_to([P, 2, 2, C]), ALU.mult)
                for u in range(2):
                    ins = nc.vector.tensor_tensor(
                        prod[:, par, u, 1:7, :].rearrange("p (k x) c -> p k x c", k=2),
                        tp[:, u, 2:4, :].unsqueeze(2).broadcast_to([P, 2, 3, C]),
                        x[:, u, 1:4, :].unsqueeze(1).broadcast_to([P, 2, 3, C]), ALU.mult)
                ins.then_inc(S["msg"], 1)

            def add(t, b, i, q, at):
                for u in range(2):
                    n = 2 * q + u
                    v.wait_ge(S["mm"], t * U + (n + 1))
                    if isinstance(t, int) and t * U + n == 0:
                        v.wait_ge(S["cl"], 1)
                    else:
                        v.wait_ge(S["acc"], t * U + n)
                    to = k.acc[:, ds(at[n], 1), 0:D].rearrange("p a d -> p (a d)")
                    nc.vector.tensor_tensor(to, to, psA[:, u, 0:D], ALU.add).then_inc(S["acc"], 1)

            select(0, 0, 0)
            products(0, 0, 0, 0)

            def body(t, b, i, more):
                _, at = nc.values_load_multi_w_load_instructions(
                    k.node_tile[0:1, ds(t * U, U)], engines=[DVE], min_val=0, max_val=NT - 1)
                for q in range(QB):
                    if q == 2 and more:
                        select(t + 1, 1 - b, i + b)
                    if q < QB - 1:
                        products(t, b, i, q + 1)
                    elif more:
                        products(t + 1, 1 - b, i + b, 0)
                    add(t, b, i, q, at)

            ends(v, NB, body)
            v.wait_ge(S["acc"], ST)


def contract(nc, k, tag):
    names = ["w", "wz", "cp", "skip0", "skip1", "tr", "at", "lin", "a", "sq", "v", "c", "b0", "b1", "out", "o"]
    es, s = scope(nc, [tag + n for n in names])
    with es:
        S = {n: s[tag + n] for n in names}

        def sb(name, shape):
            return es.enter_context(nc.sbuf_tensor(tag + name, shape, F32))

        skip = [sb(f"skip{b}", [P, D]) for b in range(2)]
        wl = sb("wl", [128, 4, C])
        wb = sb("wb", [C, 2, C])
        c0 = sb("c0", [C, 5])
        c1 = sb("c1", [C, 4])
        sums = sb("sums", [P, 2, D])
        aT = sb("aT", [128, 2, 2, P])
        A = sb("A", [C, 2, 4, P])
        sq = sb("sq", [C, 2, 3, P])
        vv = sb("vv", [C, 2, P])
        q0 = sb("q0", [C, P])
        q1 = sb("q1", [C, P])
        B = sb("B", [C, 2, 4, P])
        psT = es.enter_context(nc.psum_tensor(tag + "psT", [128, 2, 512], F32))
        psL = es.enter_context(nc.psum_tensor(tag + "psL", [C, 2, 512], F32))
        psO = es.enter_context(nc.psum_tensor(tag + "psO", [P, 2, 512], F32))
        block = es.enter_context(nc.Block())
        skips = [S["skip0"], S["skip1"]]

        @block.gpsimd
        def _(g):
            g.memset(wl[:, :, :], 0.0).then_inc(S["wz"], 1)

            def stage(t, b, i):
                if later(i):
                    g.wait_ge(S["tr"], t - 1)
                g.tensor_copy(sums[:, b, :], k.acc[:, ds(t, 1), 0:D].rearrange("p a d -> p (a d)")
                              ).then_inc(S["cp"], 1)

            pairs(g, NT, stage)

        @block.sync
        def _(sp):
            sp.wait_ge(S["wz"], 1)
            for n in range(4):
                half = slice(n % 2 * C, n % 2 * C + C)
                sp.dma_start(wl[half, n, :], k.w["W_lin1" if n else "W_lin0"]).then_inc(S["w"], 16)
            for n in range(2):
                sp.dma_start(wb[:, n, :], k.w[f"WB{n}"]).then_inc(S["w"], 16)
            sp.dma_start(c0[:, :], k.w["Wc0"]).then_inc(S["w"], 16)
            sp.dma_start(c1[:, :], k.w["Wc1"]).then_inc(S["w"], 16)

            def load(t, b, i):
                if later(i):
                    sp.wait_ge(S["o"], t - 1)
                sp.dma_start(skip[b][:, :], k.skip[ds(t * P, P), :]).then_inc(skips[b], 16)

            pairs(sp, NT, load)

        @block.tensor
        def _(pe):
            pe.wait_ge(S["w"], 16 * 8)

            def maps(t, b, i):
                if later(i):
                    pe.wait_ge(S["at"], t - 1)
                pe.wait_ge(S["cp"], t + 1)
                for q in range(2):
                    ins = nc.tensor.transpose(psT[:, b, q * P:(q + 1) * P], sums[:, b, q * 128:(q + 1) * 128],
                                              k.ident[0:P, 0:P])
                ins.then_inc(S["tr"], 1)
                pe.wait_ge(S["at"], t + 1)
                if later(i):
                    pe.wait_ge(S["sq"], t - 1)
                for n in range(4):
                    ins = nc.tensor.matmul(psL[:, b, n * P:(n + 1) * P], wl[:, n, :], aT[:, b, n // 2, :],
                                           start=True, stop=True)
                ins.then_inc(S["lin"], 1)

            def out(t, b, i):
                pe.wait_ge(S["b1"], t + 1)
                if later(i):
                    pe.wait_ge(S["o"], t - 1)
                for n in range(4):
                    ins = nc.tensor.matmul(psO[:, b, n * C:(n + 1) * C], B[:, b, n, :], wb[:, min(n, 1), :],
                                           start=True, stop=True)
                ins.then_inc(S["out"], 1)

            skewed(pe, NT, maps, out)

        @block.scalar
        def _(a):
            def leave(t, b, i):
                a.wait_ge(S["tr"], t + 1)
                if later(i):
                    a.wait_ge(S["lin"], t - 1)
                nc.scalar.activation(aT[:, b, :, :].rearrange("p q c -> p (q c)"), psT[:, b, 0:2 * P],
                                     ACT.Copy).then_inc(S["at"], 1)
                a.wait_ge(S["lin"], t + 1)
                if later(i):
                    a.wait_ge(S["b1"], t - 1)
                nc.scalar.activation(A[:, b, :, :].rearrange("p n e -> p (n e)"), psL[:, b, 0:4 * P],
                                     ACT.Copy).then_inc(S["a"], 1)
                nc.scalar.activation(sq[:, b, :, :].rearrange("p n e -> p (n e)"), psL[:, b, P:4 * P],
                                     ACT.Square).then_inc(S["sq"], 1)

            pairs(a, NT, leave)

        @block.vector
        def _(v):
            v.wait_ge(S["w"], 16 * 8)
            chain = Count(S["c"])

            def step(ins):
                chain.inc(ins)
                v.wait_ge(chain.sem, chain.value())

            def polynomials(t, b, i, per):
                a0, a1, w = A[:, b, 0, :], A[:, b, 1:4, :], vv[:, b, :]
                v.wait_ge(S["sq"], t + 1)
                v.wait_ge(S["a"], t + 1)
                step(nc.vector.tensor_reduce(w, sq[:, b].rearrange("p x e -> p e x"), AX.X, ALU.add))
                if later(i):
                    v.wait_ge(S["out"], t - 1)

                def mul_add(out, in_, m, plus):
                    return nc.vector.tensor_scalar(out, in_, m, plus, ALU.mult, ALU.add)

                def stt(out, in0, scalar, in1, op0, op1):
                    return nc.vector.scalar_tensor_tensor(out=out, in0=in0, scalar=scalar, in1=in1, op0=op0, op1=op1)

                chain.inc(mul_add(q0[:, :], a0, c0[:, 3:4], c0[:, 1:2]))
                step(mul_add(q1[:, :], a0, c1[:, 2:3], c1[:, 1:2]))
                chain.inc(nc.vector.tensor_tensor(q0[:, :], q0[:, :], a0, ALU.mult))
                step(nc.vector.tensor_tensor(q1[:, :], q1[:, :], a0, ALU.mult))
                chain.inc(stt(q0[:, :], w, c0[:, 4:5], q0[:, :], ALU.mult, ALU.add))
                step(stt(q1[:, :], w, c1[:, 3:4], q1[:, :], ALU.mult, ALU.add))
                step(stt(q0[:, :], q0[:, :], c0[:, 0:1], a0, ALU.add, ALU.mult))
                chain.inc(stt(B[:, b, 0, :], w, c0[:, 2:3], q0[:, :], ALU.mult, ALU.add))
                stt(B[:, b, 1:4, :], q1[:, :].unsqueeze(1).broadcast_to([C, 3, P]), c1[:, 0:1], a1,
                    ALU.add, ALU.mult).then_inc(S["b1"], 1)
                v.wait_ge(S["b1"], t + 1)
                v.wait_ge(chain.sem, chain.value())

            def finish(t, b, i):
                v.wait_ge(S["out"], t + 1)
                v.wait_ge(skips[b], i * 16 + 16)
                nc.vector.tensor_tensor(k.acc[:, ds(t, 1), 0:D].rearrange("p a d -> p (a d)"), psO[:, b, 0:D],
                                        skip[b][:, :], ALU.add).then_inc(S["o"], 1)

            per = 9
            polynomials(0, 0, 0, per)
            for t in range(1, 4):
                polynomials(t, t % 2, t // 2, per)
                finish(t - 1, (t - 1) % 2, (t - 1) // 2)
            with v.Fori(2, NT // 2) as i:
                chain.enter(i - 2, 2 * per)
                polynomials(i * 2, 0, i, per)
                finish(i * 2 - 1, 1, i - 1)
                polynomials(i * 2 + 1, 1, i, per)
                finish(i * 2, 0, i)
                chain.leave(NT // 2 - 2)
            finish(NT - 1, 1, NT // 2 - 1)
            v.wait_ge(S["o"], NT)


def batch_norm(nc, k, tag, gammas, betas, vectors):
    names = ["row", "deg", "h", "y", "sum", "m", "d", "sq", "sum2", "r", "sd", "t", "u", "x"]
    es, s = scope(nc, [tag + n for n in names])
    with es:
        S = {n: s[tag + n] for n in names}

        def sb(name, shape):
            return es.enter_context(nc.sbuf_tensor(tag + name, shape, F32))

        gamma = sb("gamma", [P, D])
        beta = sb("beta", [P, D])
        mean = sb("mean", [P, D])
        scale = sb("scale", [P, D])
        std = sb("std", [P, D])
        h = sb("h", [P, 2, D])
        sq = sb("sq", [P, 2, D])
        tt = sb("tt", [P, 2, D])
        rdeg = sb("rdeg", [P, NT])
        ps = es.enter_context(nc.psum_tensor(tag + "ps", [P, 2, 512], F32))
        block = es.enter_context(nc.Block())

        def row(t):
            return k.acc[:, ds(t, 1), 0:D].rearrange("p a d -> p (a d)")

        @block.sync
        def _(sp):
            for dst, parts in ((gamma, gammas), (beta, betas)):
                for off, a in parts:
                    sp.dma_start(dst[:, off:off + a.shape[0]], a.partition_broadcast(P)).then_inc(S["row"], 16)

        @block.scalar
        def _(a):
            if not vectors:
                def again(t, b, i):
                    if later(i):
                        a.wait_ge(S["y"], t - 1)
                    nc.scalar.activation(h[:, b, :], k.x[:, ds(t, 1), :].rearrange("p a d -> p (a d)"), ACT.Relu,
                                         bias=k.shift[:, ds(t, 1)], scale=k.rstd[:, ds(t, 1)]).then_inc(S["h"], 1)

                pairs(a, NT, again)

            def square(t, b, i):
                a.wait_ge(S["d"], t + 1)
                if later(i):
                    a.wait_ge(S["sum2"], t - 1)
                nc.scalar.activation(sq[:, b, :], row(t), ACT.Square).then_inc(S["sq"], 1)

            pairs(a, NT, square)
            a.wait_ge(S["r"], 4)
            nc.scalar.activation(std[:, :], scale[:, :], ACT.Sqrt).then_inc(S["sd"], 1)

        @block.tensor
        def _(pe):
            def total(t, b, i, more):
                if not vectors:
                    pe.wait_ge(S["y"], t + 1)
                first = isinstance(t, int) and t == 0
                nc.tensor.matmul(ps[:, 0, 0:D], k.ones[0:P, 0:P], row(t), start=first,
                                 stop=not more).then_inc(S["sum"], 1)

            ends(pe, NT, total)

            def total2(t, b, i, more):
                pe.wait_ge(S["sq"], t + 1)
                first = isinstance(t, int) and t == 0
                nc.tensor.matmul(ps[:, 1, 0:D], k.ones[0:P, 0:P], sq[:, b, :], start=first,
                                 stop=not more).then_inc(S["sum2"], 1)

            ends(pe, NT, total2)

        @block.vector
        def _(v):
            if vectors:
                nc.vector.memset(mean[:, :], 0.0).then_inc(S["m"], 1)
            else:
                nc.vector.tensor_scalar(rdeg[:, :], k.deg[:, :], 1.0, None, ALU.max).then_inc(S["deg"], 1)
                v.wait_ge(S["deg"], 1)
                nc.vector.reciprocal(rdeg[:, :], rdeg[:, :]).then_inc(S["deg"], 1)
                v.wait_ge(S["deg"], 2)

                def average(t, b, i):
                    v.wait_ge(S["h"], t + 1)
                    nc.vector.scalar_tensor_tensor(out=row(t), in0=row(t), scalar=rdeg[:, ds(t, 1)], in1=h[:, b, :],
                                                   op0=ALU.mult, op1=ALU.add).then_inc(S["y"], 1)

                pairs(v, NT, average)
                v.wait_ge(S["y"], NT)
            v.wait_ge(S["sum"], NT)
            if vectors:
                v.wait_ge(S["m"], 1)
            wd = C if vectors else D
            nc.vector.tensor_scalar(mean[:, 0:wd], ps[:, 0, 0:wd], 1.0 / N, None, ALU.mult).then_inc(S["m"], 1)
            v.wait_ge(S["m"], 2 if vectors else 1)

            def center(t, b, i):
                out = k.acc[:, ds(t, 1), 0:wd].rearrange("p a d -> p (a d)")
                nc.vector.tensor_tensor(out, out, mean[:, 0:wd], ALU.subtract).then_inc(S["d"], 1)

            pairs(v, NT, center)
            v.wait_ge(S["sum2"], NT)
            if vectors:
                three = ps[:, 1, C:D].rearrange("p (x c) -> p c x", x=3)
                nc.vector.tensor_reduce(std[:, 0:C], three, AX.X, ALU.add).then_inc(S["r"], 1)
                nc.vector.tensor_scalar(scale[:, 0:C], ps[:, 1, 0:C], 1.0 / N, EPS, ALU.mult, ALU.add).then_inc(S["r"], 1)
                v.wait_ge(S["r"], 2)
                nc.vector.tensor_scalar(scale[:, C:D].rearrange("p (x c) -> p x c", x=3),
                                        std[:, 0:C].unsqueeze(1).broadcast_to([P, 3, C]),
                                        1.0 / (3.0 * N), EPS, ALU.mult, ALU.add).then_inc(S["r"], 2)
            else:
                nc.vector.tensor_scalar(scale[:, :], ps[:, 1, 0:D], 1.0 / N, EPS, ALU.mult, ALU.add).then_inc(S["r"], 4)
            v.wait_ge(S["sd"], 1)
            v.wait_ge(S["row"], 16 * (len(gammas) + len(betas)))
            nc.vector.reciprocal(scale[:, :], std[:, :]).then_inc(S["r"], 1)
            v.wait_ge(S["r"], 5)
            nc.vector.tensor_tensor(scale[:, :], scale[:, :], gamma[:, :], ALU.mult).then_inc(S["r"], 1)
            v.wait_ge(S["r"], 6)
            v.wait_ge(S["d"], NT)

            def apply(t, b, i):
                if later(i):
                    v.wait_ge(S["x"], t - 1)
                nc.vector.tensor_tensor(tt[:, b, :], row(t), scale[:, :], ALU.mult).then_inc(S["t"], 1)

            def residual(t, b, i):
                v.wait_ge(S["t"], t + 1)
                nc.vector.tensor_tensor(tt[:, b, 0:wd], tt[:, b, 0:wd], beta[:, 0:wd], ALU.add).then_inc(S["u"], 1)
                v.wait_ge(S["u"], t + 1)
                x = k.x[:, ds(t, 1), :].rearrange("p a d -> p (a d)")
                if vectors:
                    nc.vector.tensor_tensor(x[:, 0:C], x[:, 0:C], tt[:, b, 0:C], ALU.add)
                    xv = x[:, C:D].rearrange("p (c x) -> p x c", x=3)
                    nc.vector.tensor_tensor(xv, xv, tt[:, b, C:D].rearrange("p (x c) -> p x c", x=3),
                                            ALU.add).then_inc(S["x"], 1)
                else:
                    nc.vector.scalar_tensor_tensor(out=x, in0=tt[:, b, :], scalar=0.0, in1=x, op0=ALU.max,
                                                   op1=ALU.add).then_inc(S["x"], 1)

            skewed(v, NT, apply, residual)
            v.wait_ge(S["x"], NT)


def scores(nc, k, tag, out, R, edge=None):
    XB = NT // U
    names = ["bc0", "bc1", "on", "sp", "rc", "xl0", "xl1", "xon", "xmm", "xadd", "xc", "is0", "is1", "w", "wz", "lf0", "lf1", "sum", "lk", "sc", "ft", "fe", "al", "ev", "s0", "s1",
             "v", "go"]
    es, s = scope(nc, [tag + n for n in names], [(tag + "ga0", k.gathered.pop()), (tag + "ga1", k.gathered.pop())])
    with es:
        S = {n: s[tag + n] for n in names + ["ga0", "ga1"]}

        def sb(name, shape, dt=F32):
            return es.enter_context(nc.sbuf_tensor(tag + name, shape, dt))

        RD = H if edge else 2 * H
        idx = [sb(f"idx{b}", [P, U], I32) for b in range(2)]
        ga = [sb(f"ga{b}", [P, U, H]) for b in range(2)]
        gd = [sb(f"gd{b}", [P, U, RD]) for b in range(2)]
        bc = [sb(f"bc{b}", [P, U * P]) for b in range(2)]
        to = [sb(f"to{b}", [P, U * P]) for b in range(2)]
        at_edge = sb("at_edge", [P, ET, RD])
        both = sb("both", [P, 2, U, H])
        sc = sb("sc", [P, 2, U, R])
        res = [sb(f"res{b}", [R, U, P]) for b in range(2)]
        if edge:
            f = [sb(f"f{b}", [P, U, C]) for b in range(2)]
            fT = sb("fT", [128, U // 2, P])
            we = sb("we", [128, D])
            av = sb("av", [128, D])
            fold = sb("fold", [128, H])
            V = sb("V", [128, 2, H])
            psF = es.enter_context(nc.psum_tensor(tag + "psF", [128, 2, 512], F32))
        psS = es.enter_context(nc.psum_tensor(tag + "psS", [R, 3, 512], F32))
        psE = es.enter_context(nc.psum_tensor(tag + "psE", [P, 2, 512], F32))
        block = es.enter_context(nc.Block())
        i_sem, g_sem, f_sem, s_sem, b_sem = ([S[n + str(b)] for b in range(2)]
                                             for n in ("is", "ga", "lf", "s", "bc"))
        parts = [(0, 4), (4, 8), (8, U)]

        @block.sync
        def _(sp):
            if edge:
                for o in (0, 1):
                    sp.dma_start(we[o * C:(o + 1) * C, :], edge[0]).then_inc(S["w"], 16)
                sp.dma_start(av[:, :], edge[1].rearrange("h c -> (h c)").partition_broadcast(128)
                             ).then_inc(S["w"], 16)

            def broad(b, t, sem):
                sp.dma_start(bc[b][:, :], k.dst_rows[ds(t * U, U)].rearrange("t e -> (t e)").partition_broadcast(P)
                             ).then_inc(sem, 16)

            for n in range(XB):
                if n >= 2:
                    sp.wait_ge(S["xon"], n - 1)
                broad(n % 2, EB + n, S["xl%d" % (n % 2)])
            sp.wait_ge(S["xon"], XB)

            def load(t, b, i):
                if later(i):
                    sp.wait_ge(g_sem[b], i * (16 * U))
                sp.dma_start(idx[b][:, :], k.src_of[:, ds(t * U, U)]).then_inc(i_sem[b], 16)
                if later(i):
                    sp.wait_ge(S["on"], t - 1)
                    sp.sem_inc(S["go"], 1)
                broad(b, t, b_sem[b])
                if edge:
                    if later(i):
                        sp.wait_ge(S["ft"], t - 1)
                        sp.sem_inc(S["go"], 1)
                    sp.dma_start(f[b][:, :, :], tiles(k.attr[ds(t * (U * P), U * P), :])).then_inc(f_sem[b], 16)

            pairs(sp, EB, load)

        @block.gpsimd
        def _(g):
            def gather(t, b, i):
                g.wait_ge(i_sem[b], i * 16 + 16)
                if later(i):
                    g.wait_ge(S["lk"], t - 1)
                g.sem_inc(S["go"], 1)
                for u in range(U):
                    g.indirect_dma_start(ga[b][:, u, :], None, k.senders,
                                         bass.IndirectOffsetOnAxis(ap=idx[b][:, u:u + 1], axis=0)
                                         ).then_inc(g_sem[b], 16)

            pairs(g, EB, gather)

        @block.tensor
        def _(pe):
            if edge:
                pe.wait_ge(S["v"], 3)
            for n in range(XB):
                pe.wait_ge(S["xon"], n + 1)
                for u in range(U):
                    if n >= 2 and u == 0:
                        pe.wait_ge(S["xadd"], (n - 1) * U)
                    ins = nc.tensor.matmul(psE[:, n % 2, u * RD:(u + 1) * RD], to[n % 2][:, u * P:(u + 1) * P],
                                           k.recv[:, n * U + u, 0:RD], start=True, stop=True)
                ins.then_inc(S["xmm"], 1)
            pe.wait_ge(S["xadd"], NT)

            def spread(t, b, i):
                _, at = nc.values_load_multi_w_load_instructions(
                    k.node_tile[0:1, ds(t * U, U)], engines=[PE], min_val=0, max_val=NT - 1)
                pe.wait_ge(S["on"], t + 1)
                if later(i):
                    pe.wait_ge(S["rc"], t - 1)
                for u in range(U):
                    ins = nc.tensor.matmul(psE[:, b, u * RD:(u + 1) * RD], to[b][:, u * P:(u + 1) * P],
                                           k.recv[:, ds(at[u], 1), 0:RD].rearrange("p a h -> p (a h)"),
                                           start=True, stop=True)
                ins.then_inc(S["sp"], 1)

            def score(t, b, i):
                spread(t, b, i)
                if edge:
                    pe.wait_ge(f_sem[b], i * 16 + 16)
                    if not isinstance(t, int) or t:
                        pe.wait_ge(S["fe"], t)
                    for n in range(U // 2):
                        ins = nc.tensor.transpose(psF[:, n // 3, (n % 3) * P:(n % 3 + 1) * P],
                                                  f[b][:, 2 * n:2 * n + 2, :].rearrange("p u f -> p (u f)"),
                                                  k.ident[0:P, 0:P])
                    ins.then_inc(S["ft"], 1)
                    pe.wait_ge(S["fe"], t + 1)
                pe.wait_ge(S["lk"], t + 1)
                if not isinstance(t, int) or t:
                    pe.wait_ge(S["ev"], t)
                for u in range(U):
                    to = psS[:, u // 4, (u % 4) * P:(u % 4 + 1) * P]
                    if edge:
                        nc.tensor.matmul(to, V[:, u % 2, :], fT[:, u // 2, :], start=True, stop=False)
                        ins = nc.tensor.matmul(to, sc[:, b, u, :], k.ident[0:P, 0:P], start=False, stop=True)
                    else:
                        ins = nc.tensor.transpose(to, sc[:, b, u, :], k.ident[0:P, 0:P])
                ins.then_inc(S["al"], 1)

            pairs(pe, EB, score)

        @block.scalar
        def _(a):
            def leave(t, b, i):
                if edge:
                    a.wait_ge(S["ft"], t + 1)
                    if not isinstance(t, int) or t:
                        a.wait_ge(S["al"], t)
                    nc.scalar.activation(fT[:, 0:3, :], psF[:, 0, 0:3 * P].rearrange("p (n e) -> p n e", e=P), ACT.Copy)
                    nc.scalar.activation(fT[:, 3:5, :], psF[:, 1, 0:2 * P].rearrange("p (n e) -> p n e", e=P),
                                         ACT.Copy).then_inc(S["fe"], 1)
                    a.wait_ge(S["ev"], t + 1)
                else:
                    a.wait_ge(S["al"], t + 1)
                    if later(i):
                        a.wait_ge(s_sem[b], i * 16)
                    for n, (u0, u1) in enumerate(parts):
                        ins = nc.scalar.activation(res[b][:, u0:u1, :],
                                                   psS[:, n, 0:(u1 - u0) * P].rearrange("r (u e) -> r u e", e=P),
                                                   ACT.Copy)
                    ins.then_inc(S["ev"], 1)
                    a.wait_ge(S["ev"], t + 1)
                a.dma_start(out[ds(t * U, U)].rearrange("t r e -> r t e"), res[b][:, :, :]).then_inc(s_sem[b], 16)

            pairs(a, EB, leave)
            a.wait_ge(s_sem[0], 16 * (EB - EB // 2))
            a.wait_ge(s_sem[1], 16 * (EB // 2))

        @block.vector
        def _(v):
            if edge:
                nc.vector.memset(V[:, :, :], 0.0).then_inc(S["wz"], 1)
                v.wait_ge(S["w"], 48)
                nc.vector.tensor_tensor(we[:, :], we[:, :], av[:, :], ALU.mult).then_inc(S["wz"], 1)
                v.wait_ge(S["wz"], 2)
                nc.vector.tensor_reduce(fold[:, :], we[:, :].rearrange("p (h c) -> p h c", c=CH), AX.X,
                                        ALU.add).then_inc(S["v"], 1)
                v.wait_ge(S["v"], 1)
                for o in (0, 1):
                    nc.vector.tensor_copy(V[o * C:(o + 1) * C, o, :], fold[o * C:(o + 1) * C, :]).then_inc(S["v"], 1)

            nc.vector.memset(at_edge[:, :, :], 0.0).then_inc(S["xc"], 1)
            for n in range(XB):
                v.wait_ge(S["xl%d" % (n % 2)], 16 * (n // 2 + 1))
                if n >= 2:
                    v.wait_ge(S["xmm"], n - 1)
                nc.vector.tensor_scalar(to[n % 2][:, :], bc[n % 2][:, :], k.lane[:, 0:1], None,
                                        ALU.is_equal).then_inc(S["xon"], 1)
                _, at = nc.values_load_multi_w_load_instructions(
                    k.extra_at[0:1, n * U:(n + 1) * U], engines=[DVE], min_val=0, max_val=ET - 1)
                v.wait_ge(S["xmm"], n + 1)
                for u in range(U):
                    if n * U + u == 0:
                        v.wait_ge(S["xc"], 1)
                    else:
                        v.wait_ge(S["xadd"], n * U + u)
                    dst = at_edge[:, ds(at[u], 1), :].rearrange("p a h -> p (a h)")
                    nc.vector.tensor_tensor(dst, dst, psE[:, n % 2, u * RD:(u + 1) * RD],
                                            ALU.add).then_inc(S["xadd"], 1)
            v.wait_ge(S["xadd"], NT)

            def one_hot(t, b, i):
                v.wait_ge(b_sem[b], i * 16 + 16)
                if later(i):
                    v.wait_ge(S["sp"], t - 1)
                nc.vector.tensor_scalar(to[b][:, :], bc[b][:, :], k.lane[:, 0:1], None,
                                        ALU.is_equal).then_inc(S["on"], 1)

            def gathered(t, b, i):
                one_hot(t, b, i)
                if later(i):
                    v.wait_ge(S["al"], t - 1)
                v.wait_ge(S["sp"], t + 1)
                nc.vector.tensor_tensor(gd[b][:, :, :], at_edge[:, ds(t * U, U), :],
                                        psE[:, b, 0:U * RD].rearrange("p (u r) -> p u r", r=RD),
                                        ALU.add).then_inc(S["rc"], 1)
                v.wait_ge(S["rc"], t + 1)
                v.wait_ge(g_sem[b], i * (16 * U) + 16 * U)
                if edge:
                    nc.vector.tensor_tensor(sc[:, b], ga[b][:, :, :], gd[b][:, :, :], ALU.add).then_inc(S["lk"], 1)
                else:
                    nc.vector.tensor_tensor(both[:, b], ga[b][:, :, :], gd[b][:, :, 0:H], ALU.add).then_inc(S["sum"], 1)
                    v.wait_ge(S["sum"], t + 1)
                    nc.vector.scalar_tensor_tensor(out=sc[:, b, :, 0:H], in0=both[:, b], scalar=0.2, in1=both[:, b],
                                                   op0=ALU.mult, op1=ALU.max).then_inc(S["sc"], 1)
                    v.wait_ge(S["sc"], t + 1)
                    nc.vector.tensor_tensor(sc[:, b, :, H:R], sc[:, b, :, 0:H], gd[b][:, :, H:2 * H],
                                            ALU.max).then_inc(S["lk"], 1)

            def leaky(t, b, i):
                v.wait_ge(S["al"], t + 1)
                if later(i):
                    v.wait_ge(s_sem[b], i * 16)
                for n, (u0, u1) in enumerate(parts):
                    ps = psS[:, n, 0:(u1 - u0) * P].rearrange("r (u e) -> r u e", e=P)
                    ins = nc.vector.tensor_scalar(res[b][:, u0:u1, :], ps, 0.2, None, ALU.mult)
                    ins.then_inc(S["sc"], 1)
                    v.wait_ge(S["sc"], t * 3 + (n + 1))
                    ins = nc.vector.tensor_tensor(res[b][:, u0:u1, :], res[b][:, u0:u1, :], ps, ALU.max)
                ins.then_inc(S["ev"], 1)

            def body(t, b, i):
                gathered(t, b, i)
                if edge:
                    leaky(t, b, i)

            pairs(v, EB, body)


def softmax_weights(nc, k, tag, src, out, out_extra, R):
    names = ["ld", "halo", "hz", "pen", "f", "end", "tr", "row", "rs", "cin", "cc", "a", "e", "x", "st", "sx", "ex"]
    es, s = scope(nc, [tag + n for n in names], [(tag + "gx", k.gathered.pop())])
    Q = H * CK
    with es:
        S = {n: s[tag + n] for n in names + ["gx"]}

        def sb(name, shape, dt=F32):
            return es.enter_context(nc.sbuf_tensor(tag + name, shape, dt))

        A = sb("A", [Q, CE])
        M = sb("M", [Q, CE + 2])
        pen = sb("pen", [Q, CE + 1], BF16)
        ends_ = sb("ends", [Q, 4])
        rows = sb("rows", [1, 4, Q])
        cin = sb("cin", [Q, 2])
        extra = sb("extra", [NT, R * P])
        ps = es.enter_context(nc.psum_tensor(tag + "ps", [128, 4, 512], F32))
        block = es.enter_context(nc.Block())
        D32 = M[:, :].bitcast(I32)
        dst = k.dst.rearrange("(c e) -> c e", e=CE)

        def rows_of(t, r, to_sb, sp, sem, sbuf):
            for h in range(H):
                d = t[:, r + h, :].rearrange("(c t) e -> c t e", t=CT)
                x = sbuf[h * CK:(h + 1) * CK, 0:CE].rearrange("c (t e) -> c t e", e=P)
                if to_sb:
                    sp.dma_start(x, d).then_inc(sem, 16)
                else:
                    sp.dma_start(d, x).then_inc(sem, 16)

        @block.sync
        def _(sp):
            sp.wait_ge(S["hz"], 1)
            for h in range(H):
                o = h * CK
                sp.dma_start(D32[o:o + CK, 1:CE + 1], dst).then_inc(S["halo"], 16)
                sp.dma_start(D32[o + 1:o + CK, 0:1], dst[0:CK - 1, CE - 1:CE],
                             allow_slow_non_contiguous=True).then_inc(S["halo"], 16)
                sp.dma_start(D32[o:o + CK - 1, CE + 1:CE + 2], dst[1:CK, 0:1],
                             allow_slow_non_contiguous=True).then_inc(S["halo"], 16)
            rows_of(src, R - H, True, sp, S["ld"], A)
            if R > H:
                sp.wait_ge(S["f"], 2)
                rows_of(src, 0, True, sp, S["ld"], A)
            sp.wait_ge(S["ex"], 1)
            rows_of(out, 0, False, sp, S["st"], A)
            if R > H:
                sp.wait_ge(S["x"], 2)
                rows_of(out, H, False, sp, S["st"], M)
            sp.wait_ge(S["st"], 16 * R)
            sp.sem_inc(S["sx"], 1)
            sp.wait_ge(S["gx"], 16)
            sp.dma_start(out_extra.rearrange("t r e -> t (r e)"), extra[:, :]).then_inc(S["st"], 16)
            sp.wait_ge(S["st"], 16 * R + 16)

        @block.gpsimd
        def _(g):
            g.wait_ge(S["sx"], 1)
            g.indirect_dma_start(extra[:, :], None, out.rearrange("t r e -> t (r e)"),
                                 bass.IndirectOffsetOnAxis(ap=k.tile_of[:, :], axis=0)).then_inc(S["gx"], 16)

        @block.tensor
        def _(pe):
            for n in range(2):
                pe.wait_ge(S["end"], 2 * n + 2)
                for c in range(2):
                    ins = nc.tensor.transpose(ps[0:1, n, c * Q:(c + 1) * Q], ends_[:, 2 * n + c:2 * n + c + 1],
                                              k.ident[0:Q, 0:Q])
                ins.then_inc(S["tr"], 1)
                pe.wait_ge(S["cin"], n + 1)
                nc.tensor.transpose(ps[0:Q, 2 + n, 0:1], rows[0:1, 2 + n, :], k.ident[0:1, 0:1]).then_inc(S["tr"], 1)

        @block.scalar
        def _(a):
            a.wait_ge(S["e"], 1)
            nc.scalar.activation(A[:, :], A[:, :], ACT.Exp).then_inc(S["ex"], 1)

        @block.vector
        def _(v):
            nc.vector.memset(D32[:, 0:CE + 2:CE + 1], -5).then_inc(S["hz"], 1)
            v.wait_ge(S["halo"], 16 * 3 * H)
            nc.vector.tensor_tensor(pen[:, :], D32[:, 1:CE + 2], D32[:, 0:CE + 1], ALU.not_equal).then_inc(S["pen"], 1)
            v.wait_ge(S["pen"], 1)
            nc.vector.tensor_scalar(pen[:, :], pen[:, :], LOW, None, ALU.mult).then_inc(S["pen"], 1)
            v.wait_ge(S["pen"], 2)
            v.wait_ge(S["ld"], 16 * H)

            def scan(n, initial, sem):
                if n == 0:
                    o, d0, d1 = M[:, 0:CE], pen[:, 0:CE], A[:, 0:CE]
                else:
                    o, d0, d1 = M[:, 0:CE][:, ::-1], pen[:, 1:CE + 1][:, ::-1], M[:, 0:CE][:, ::-1]
                return nc.vector.tensor_tensor_scan(o, d0, d1, initial, ALU.add, ALU.max)

            for n in range(2):
                first = scan(n, LOW, None)
                first.then_inc(S["a"], 1)
                v.wait_ge(S["a"], 2 * n + 1)
                last = slice(CE - 1, CE) if n == 0 else slice(0, 1)
                nc.vector.tensor_copy(ends_[:, 2 * n:2 * n + 1], M[:, last]).then_inc(S["end"], 1)
                nc.vector.tensor_reduce(ends_[:, 2 * n + 1:2 * n + 2], pen[:, n:CE + n], AX.X, ALU.min
                                        ).then_inc(S["end"], 1)
                v.wait_ge(S["tr"], 2 * n + 1)
                r0, r1, r2 = rows[0:1, 0, :], rows[0:1, 1, :], rows[0:1, 2 + n, :]
                nc.vector.tensor_copy(r0, ps[0:1, n, 0:Q]).then_inc(S["row"], 1)
                nc.vector.tensor_copy(r1, ps[0:1, n, Q:2 * Q]).then_inc(S["row"], 1)
                v.wait_ge(S["row"], 5 * n + 2)
                edge_ = slice(0, Q, CK) if n == 0 else slice(CK - 1, Q, CK)
                nc.vector.memset(rows[0:1, 1, edge_], LOW).then_inc(S["row"], 1)
                v.wait_ge(S["row"], 5 * n + 3)
                flip = (lambda t: t) if n == 0 else (lambda t: t[:, ::-1])
                nc.vector.tensor_tensor_scan(flip(r0), flip(r1), flip(r0), LOW, ALU.add, ALU.max
                                             ).then_inc(S["row"], 1)
                v.wait_ge(S["row"], 5 * n + 4)
                if n == 0:
                    nc.vector.tensor_copy(r2[:, 1:Q], r0[:, 0:Q - 1]).then_inc(S["row"], 1)
                else:
                    nc.vector.tensor_copy(r2[:, 0:Q - 1], r0[:, 1:Q]).then_inc(S["row"], 1)
                v.wait_ge(S["row"], 5 * n + 5)
                nc.vector.memset(rows[0:1, 2 + n, edge_], LOW).then_inc(S["cin"], 1)
                v.wait_ge(S["tr"], 2 * n + 2)
                nc.vector.tensor_copy(cin[:, n:n + 1], ps[0:Q, 2 + n, 0:1]).then_inc(S["cc"], 1)
                v.wait_ge(S["cc"], n + 1)
                scan(n, cin[:, n:n + 1], None).then_inc(S["a"], 1)
                v.wait_ge(S["a"], 2 * n + 2)
                if n == 0:
                    v.sem_inc(S["f"], 2)
            if R > H:
                v.wait_ge(S["ld"], 32 * H)
            nc.vector.tensor_tensor(A[:, :], A[:, :], M[:, 0:CE], ALU.subtract).then_inc(S["e"], 1)
            if R > H:
                v.wait_ge(S["e"], 1)
                nc.vector.scalar_tensor_tensor(out=M[:, 0:CE], in0=pen[:, 0:CE], scalar=-1.0, in1=M[:, 0:CE],
                                               op0=ALU.is_lt, op1=ALU.mult).then_inc(S["x"], 2)
                v.wait_ge(S["x"], 2)


def attend(nc, k, tag, bias, gamma, beta, own, out=None):
    names = ["row", "own", "xp0", "xp1", "h", "d", "e", "ex", "t", "u", "y"]
    es, s = scope(nc, [tag + n for n in names])
    with es:
        S = {n: s[tag + n] for n in names}

        def sb(name, shape):
            return es.enter_context(nc.sbuf_tensor(tag + name, shape, F32))

        bias_row = sb("bias", [P, D])
        rden = sb("rden", [P, NT, H])
        tt = sb("tt", [P, 2, D])
        h = sb("h", [P, 2, D])
        if own:
            score = sb("score", [P, NT, H])
            top = sb("top", [P, NT, H])
            alone = sb("alone", [P, NT])
        block = es.enter_context(nc.Block())
        x_sem = [S["xp0"], S["xp1"]]
        sums = k.acc[:, :, D:D + H]

        def row(t):
            return k.acc[:, ds(t, 1), 0:D].rearrange("p a d -> p (a d)")

        @block.sync
        def _(sp):
            sp.dma_start(bias_row[:, :], bias.partition_broadcast(P)).then_inc(S["row"], 16)
            if own:
                def load(t, b, i):
                    if later(i):
                        sp.wait_ge(S["t"], t - 1)
                    sp.dma_start(h[:, b, :], k.table[ds(t * P, P), :]).then_inc(x_sem[b], 16)

                pairs(sp, NT, load)

        @block.scalar
        def _(a):
            if own:
                a.wait_ge(S["e"], 4)
                nc.scalar.activation(score[:, :, :], score[:, :, :], ACT.Exp).then_inc(S["ex"], 1)
            else:
                def again(t, b, i):
                    if later(i):
                        a.wait_ge(S["y"], t - 1)
                    nc.scalar.activation(h[:, b, :], k.x[:, ds(t, 1), :].rearrange("p a d -> p (a d)"), ACT.Relu,
                                         bias=k.shift[:, ds(t, 1)], scale=k.rstd[:, ds(t, 1)]).then_inc(S["h"], 1)

                pairs(a, NT, again)

        @block.vector
        def _(v):
            if own:
                nc.vector.tensor_copy(score[:, :, :], k.recv[:, :, H:2 * H]).then_inc(S["own"], 1)
                nc.vector.tensor_scalar(alone[:, :], k.deg[:, :], 0.5, None, ALU.is_lt).then_inc(S["e"], 1)
                v.wait_ge(S["e"], 1)
                v.wait_ge(S["own"], 1)
                nc.vector.tensor_tensor(top[:, :, :], alone[:, :].unsqueeze(2).broadcast_to([P, NT, H]),
                                        score[:, :, :], ALU.mult).then_inc(S["e"], 1)
                v.wait_ge(S["e"], 2)
                nc.vector.tensor_tensor(top[:, :, :], top[:, :, :], k.acc[:, :, D + H:D + 2 * H],
                                        ALU.add).then_inc(S["e"], 1)
                v.wait_ge(S["e"], 3)
                nc.vector.tensor_tensor(score[:, :, :], score[:, :, :], top[:, :, :],
                                        ALU.subtract).then_inc(S["e"], 1)
                v.wait_ge(S["ex"], 1)
                nc.vector.tensor_tensor(rden[:, :, :], sums, score[:, :, :], ALU.add).then_inc(S["d"], 1)
            else:
                nc.vector.tensor_scalar(rden[:, :, :], sums, 1e-16, None, ALU.add).then_inc(S["d"], 1)
            v.wait_ge(S["d"], 1)
            nc.vector.reciprocal(rden[:, :, :], rden[:, :, :]).then_inc(S["d"], 1)
            v.wait_ge(S["d"], 2)
            v.wait_ge(S["row"], 16)
            chain = Count(S["u"])

            def by_head(t):
                return t.rearrange("p (h c) -> p h c", c=CH)

            def spread(t, per_node):
                return (per_node[:, ds(t, 1), :].rearrange("p a h -> p (a h)").unsqueeze(2)
                        .broadcast_to([P, H, CH]))

            def first(t, b, i):
                if own:
                    v.wait_ge(x_sem[b], i * 16 + 16)
                    nc.vector.tensor_tensor(by_head(tt[:, b, :]), by_head(h[:, b, :]), spread(t, score),
                                            ALU.mult).then_inc(S["t"], 1)
                    v.wait_ge(S["t"], t + 1)
                    chain.inc(nc.vector.tensor_tensor(tt[:, b, :], tt[:, b, :], row(t), ALU.add))
                    v.wait_ge(chain.sem, chain.value())
                    chain.inc(nc.vector.tensor_tensor(by_head(tt[:, b, :]), by_head(tt[:, b, :]), spread(t, rden),
                                                      ALU.mult))
                    v.wait_ge(chain.sem, chain.value())
                else:
                    chain.inc(nc.vector.tensor_tensor(by_head(tt[:, b, :]), by_head(row(t)), spread(t, rden),
                                                      ALU.mult))
                    v.wait_ge(chain.sem, chain.value())
                    v.wait_ge(S["h"], t + 1)
                    chain.inc(nc.vector.tensor_tensor(tt[:, b, :], tt[:, b, :], h[:, b, :], ALU.add))
                    v.wait_ge(chain.sem, chain.value())
                nc.vector.tensor_tensor(row(t), tt[:, b, :], bias_row[:, :], ALU.add).then_inc(S["y"], 1)

            first(0, 0, 0)
            first(1, 1, 0)
            v.wait_ge(S["y"], 2)
            with v.Fori(1, NT // 2) as i:
                chain.enter(i - 1, 4)
                first(i * 2, 0, i)
                first(i * 2 + 1, 1, i)
                chain.leave(NT // 2 - 1)
            v.wait_ge(S["y"], NT)

    row_stats(nc, k, tag + "n", k.acc, D)

    names = ["w", "n", "t", "u", "x", "s0", "s1"]
    es, s = scope(nc, [tag + "f" + n for n in names])
    with es:
        S = {n: s[tag + "f" + n] for n in names}
        gamma_row = es.enter_context(nc.sbuf_tensor(tag + "gamma", [P, D], F32))
        beta_row = es.enter_context(nc.sbuf_tensor(tag + "beta", [P, D], F32))
        y = es.enter_context(nc.sbuf_tensor(tag + "yn", [P, 2, D], F32))
        block = es.enter_context(nc.Block())

        def xrow(t):
            return k.x[:, ds(t, 1), :].rearrange("p a d -> p (a d)")

        @block.sync
        def _(sp):
            sp.dma_start(gamma_row[:, :], gamma.partition_broadcast(P)).then_inc(S["w"], 16)
            sp.dma_start(beta_row[:, :], beta.partition_broadcast(P)).then_inc(S["w"], 16)
            if out is not None:
                def store(t, b, i):
                    sp.wait_ge(S["x"], t + 1)
                    sp.dma_start(out[ds(t * P, P), :], xrow(t)).then_inc(S[f"s{b}"], 16)

                pairs(sp, NT, store)
                sp.wait_ge(S["s0"], 16 * (NT // 2))
                sp.wait_ge(S["s1"], 16 * (NT // 2))

        @block.scalar
        def _(a):
            def norm(t, b, i):
                if later(i):
                    a.wait_ge(S["x"], t - 1)
                nc.scalar.activation(y[:, b, :], k.acc[:, ds(t, 1), 0:D].rearrange("p a d -> p (a d)"), ACT.Identity,
                                     bias=k.shift[:, ds(t, 1)], scale=k.rstd[:, ds(t, 1)]).then_inc(S["n"], 1)

            pairs(a, NT, norm)

        @block.gpsimd
        def _(g):
            g.wait_ge(S["w"], 32)

            def shifted(t, b, i):
                g.tensor_tensor(xrow(t), xrow(t), beta_row[:, :], ALU.add).then_inc(S["u"], 1)

            pairs(g, NT, shifted)

        @block.vector
        def _(v):
            v.wait_ge(S["w"], 32)

            def scaled(t, b, i):
                v.wait_ge(S["n"], t + 1)
                nc.vector.tensor_tensor(y[:, b, :], y[:, b, :], gamma_row[:, :], ALU.mult).then_inc(S["t"], 1)

            def residual(t, b, i):
                v.wait_ge(S["t"], t + 1)
                v.wait_ge(S["u"], t + 1)
                nc.vector.tensor_tensor(xrow(t), xrow(t), y[:, b, :], ALU.add).then_inc(S["x"], 1)

            skewed(v, NT, scaled, residual)
            v.wait_ge(S["x"], NT)


def build(nc, ins, out, stop=None):
    k = Net()
    k.x_in, k.src, k.dst = ins["x"], ins["src"], ins["dst"]
    k.rbf, k.sh, k.attr = ins["edge_attr_16"], ins["edge_attr_4"], ins["edge_attr_64"]
    w0 = {n[7:]: a for n, a in ins.items() if n.startswith("L0_")}
    k.w = w0

    def dram(name, shape, dt=F32):
        return nc.dram_tensor(name, shape, dt).ap()

    k.rbf_extra = dram("rbf_extra", [NT, P * 16])
    k.sh_extra = dram("sh_extra", [NT, P * 4])
    k.table = dram("rows", [N, D])
    k.skip = dram("skip", [N, D])
    k.senders = dram("senders", [N, H])
    k.dst_rows = dram("dst_rows", [ST, P])
    k.scores = {n: dram(f"scores{n}", [ET, r, P]) for n, r in ((2, H), (3, 2 * H))}
    k.weights = {n: dram(f"weights{n}", [ET, r, P]) for n, r in ((2, H), (3, 2 * H))}
    k.weights_extra = {n: dram(f"weights_extra{n}", [NT, r, P]) for n, r in ((2, H), (3, 2 * H))}
    with ExitStack() as es:
        def sb(name, shape, dt=F32):
            return es.enter_context(nc.sbuf_tensor(name, shape, dt))

        k.gathered = [es.enter_context(nc.semaphore(f"gathered{b}")) for b in range(15)]
        k.x = sb("x_nodes", [P, NT, D])
        k.src_of = sb("src_of", [P, ST], I32)
        k.dst_in = sb("dst_in", [P, ST])
        k.node_tile = sb("node_tile", [1, ST], I32)
        k.tile_of = sb("tile_of", [NT, 1], I32)
        k.ident = sb("ident", [128, 128])
        k.ones = sb("ones", [128, 128])
        k.iota = sb("iota", [P, P])
        k.mean = sb("mean", [P, NT])
        k.rstd = sb("rstd", [P, NT])
        k.shift = sb("shift", [P, NT])
        k.deg = sb("deg", [P, NT])
        k.lane = sb("lane", [P, 1])
        k.extra_at = sb("extra_at", [1, NT], I32)
        k.recv = sb("recv", [P, NT, 2 * H])
        prepare(nc, k)
        if stop == "prep":
            k.dump(k.src_of, k.dst_in, k.node_tile, k.tile_of, k.extra_at)
            return k
        row_stats(nc, k, "n0", k.x, D)

        def weights0(sp, w, sem):
            for q in range(2):
                for o, n in ((0, 0 if q == 0 else 1), (1, 1)):
                    for m, name in enumerate(("W_up", "Wsc")):
                        sp.dma_start(w[o * C:(o + 1) * C, q, m * 128 + o * C:m * 128 + (o + 1) * C],
                                     w0[f"{name}{n}"]).then_inc(sem, 16)

        project(nc, k, "p0", weights0, 8, [(k.table, 0, D), (k.skip, D, D)], 2 * D, split=True)
        if stop == "p0":
            return k
        with nc.sbuf_tensor("acc0", [P, NT, AW], F32) as k.acc:
            convolve(nc, k, "c0")
            if stop == "c0":
                k.dump(k.acc[:, :, 0:D])
                return k
            contract(nc, k, "t0")
            batch_norm(nc, k, "b0", [(0, w0["gamma0"])] + [(C * n, w0["gamma1"]) for n in (1, 2, 3)],
                       [(0, w0["beta0"])], vectors=True)
        if stop == "l0":
            k.dump(k.x)
            return k
        row_stats(nc, k, "n1", k.x, D)

        def dense(name):
            def load(sp, w, sem):
                for q in range(2):
                    sp.dma_start(w[:, q, 0:D], ins[name][q * 128:(q + 1) * 128, :]).then_inc(sem, 16)
            return load

        project(nc, k, "p1", dense("L1_gnn_W_src"), 2, [(k.table, 0, D)], D)
        with nc.sbuf_tensor("acc1", [P, NT, AW], F32) as k.acc:
            aggregate(nc, k, "g1", k.table, degree=True)
            batch_norm(nc, k, "b1", [(0, ins["L1_gnn_gamma"])], [(0, ins["L1_gnn_beta"])], vectors=False)
        if stop == "l1":
            k.dump(k.x)
            return k
        for layer, R in ((2, H), (3, 2 * H)):
            g = {n[7:]: a for n, a in ins.items() if n.startswith(f"L{layer}_")}
            last = layer == 3
            row_stats(nc, k, f"n{layer}", k.x, D)
            pieces = [(k.table, 0, D), (k.senders, D, H)]
            project(nc, k, f"p{layer}", dense(f"L{layer}_gnn_W"), 2, pieces, D + 2 * H,
                    att=(g["att_src"], g["att_dst"]), self_score=last)
            scores(nc, k, f"s{layer}", k.scores[layer], R, None if last else (g["W_e"], g["att_edge"]))
            softmax_weights(nc, k, f"m{layer}", k.scores[layer], k.weights[layer], k.weights_extra[layer], R)
            with nc.sbuf_tensor(f"acc{layer}", [P, NT, AW], F32) as k.acc:
                aggregate(nc, k, f"g{layer}", k.table, (k.weights[layer], k.weights_extra[layer]), R)
                attend(nc, k, f"a{layer}", g["bias"], g["gamma"], g["beta"], own=last, out=out if last else None)
            if stop == f"l{layer}":
                k.dump(k.x)
                return k
    return k


def kernel(**inputs):
    import concourse.bacc as bacc
    from concourse.bass_utils import run_bass_kernel_spmd

    nc = bacc.Bacc("TRN2", target_bir_lowering=False, num_devices=1)
    arrays, aps = {}, {}
    for name, a in inputs.items():
        a = np.ascontiguousarray(a)
        arrays[f"in_{name}"] = a
        aps[name] = nc.dram_tensor(f"in_{name}", a.shape, mybir.dt.from_np(a.dtype), kind="ExternalInput").ap()
    out = nc.dram_tensor("out_x", (N, D), F32, kind="ExternalOutput").ap()
    build(nc, aps, out)
    return run_bass_kernel_spmd(nc, [arrays], core_ids=[0]).results[0]["out_x"]
```

```python
from contextlib import ExitStack

import numpy as np
import concourse.bass as bass
from concourse import mybir

F32 = mybir.dt.float32
BF16 = mybir.dt.bfloat16
I32 = mybir.dt.int32
ALU = mybir.AluOpType
ACT = mybir.ActivationFunctionType
AX = mybir.AxisListType
DVE = mybir.EngineType.DVE
PE = mybir.EngineType.PE
ds = bass.ds

P = 125
N, E, D = 6250, 106250, 256
NT, ET = N // P, E // P
ST = ET + NT
U = 10
NB = ST // U
EB = ET // U
C = 64
H, CH = 8, 32
AW = D + 2 * H
G = 5
NG = NT // G
CK = 10
CE, CT = E // CK, ET // CK
FAR = 1.0e6
LOW = -1.0e38
EPS = 1e-5


class Count:

    def __init__(self, sem):
        self.sem, self.base, self.n = sem, 0, 0

    def inc(self, ins, by=1):
        ins.then_inc(self.sem, by)
        self.n += by
        return ins

    def value(self):
        return self.base + self.n

    def enter(self, i, per):
        self.outer = self.base + self.n
        self.base, self.n, self.per = self.outer + i * per, 0, per

    def leave(self, times):
        assert self.n == self.per, (self.n, self.per)
        self.base, self.n = self.outer + times * self.per, 0


def scope(nc, sems, gathers=()):
    es = ExitStack()
    got = {s: es.enter_context(nc.semaphore(s)) for s in sems}

    def clear():
        ids = sorted(h.num for h in got.values())
        start = ids[0]
        for a, b in zip(ids, ids[1:] + [None]):
            if b != a + 1:
                nc.all_engine_barrier(sems_to_clear=range(start, a + 1))
                start = b

    es.callback(clear)
    return es, got | dict(gathers)


def pairs(eng, times, body):
    for b in range(2):
        body(b, b, 0)
    with eng.Fori(1, times // 2) as i:
        for b in range(2):
            body(i * 2 + b, b, i)
    if times % 2:
        body(times - 1, 0, times // 2)


def ends(eng, times, body):
    body(0, 0, 0, True)
    body(1, 1, 0, True)
    with eng.Fori(1, times // 2 - 1) as i:
        body(i * 2, 0, i, True)
        body(i * 2 + 1, 1, i, True)
    body(times - 2, 0, times // 2 - 1, True)
    body(times - 1, 1, times // 2 - 1, False)


def skewed(eng, times, ahead, behind):
    ahead(0, 0, 0)
    for t in range(1, 4):
        ahead(t, t % 2, t // 2)
        behind(t - 1, (t - 1) % 2, (t - 1) // 2)
    with eng.Fori(2, times // 2) as i:
        ahead(i * 2, 0, i)
        behind(i * 2 - 1, 1, i - 1)
        ahead(i * 2 + 1, 1, i)
        behind(i * 2, 0, i)
    if times % 2:
        ahead(times - 1, 0, times // 2)
        behind(times - 2, 1, times // 2 - 1)
    behind(times - 1, (times - 1) % 2, (times - 1) // 2)


def lagged(eng, times, ahead, behind):
    for t in range(4):
        ahead(t, t % 2, t // 2)
        if t >= 2:
            behind(t - 2, t % 2, 0)
    with eng.Fori(2, times // 2) as i:
        for b in range(2):
            ahead(i * 2 + b, b, i)
            behind(i * 2 + (b - 2), b, i - 1)
    for t in (times - 2, times - 1):
        behind(t, t % 2, t // 2)


def later(i):
    return not isinstance(i, int) or i > 0


class Net:
    pass


def tiles(ap):
    return ap.rearrange("(t p) f -> p t f", p=P)


def prepare(nc, k):
    names = ["ld", "pool", "cast", "tr", "ev", "bc", "cmp", "red", "jw", "tb", "gx", "trx", "st", "v", "row",
             "rt", "rd"]
    es, s = scope(nc, ["prep_" + n for n in names], [("prep_gat", k.gathered.pop())])
    with es:
        S = {n: s["prep_" + n] for n in names + ["gat"]}

        def sb(name, shape, dt=F32):
            return es.enter_context(nc.sbuf_tensor(name, shape, dt))

        Q = ET // U
        nat = sb("prep_nat", [Q, 2, U, P], I32)
        natf = sb("prep_natf", [Q, 2, U, P])
        dstf = sb("prep_dstf", [P, ET])
        first = sb("prep_first", [P, P])
        last = sb("prep_last", [P, P])
        thr = sb("prep_thr", [P, 1])
        ioti = sb("prep_ioti", [P, 128], I32)
        thri = sb("prep_thri", [P, 1], I32)
        pi = sb("prep_pi", [P, 1], I32)
        cmp = sb("prep_cmp", [NT, 2, ET])
        cnt = sb("prep_cnt", [NT, 2])
        jb = sb("prep_jb", [P, ET])
        tj = sb("prep_tj", [NT, 1])
        tji = k.tile_of
        base = sb("prep_base", [NT, 1])
        ok = sb("prep_ok", [NT, 1])
        gx = sb("prep_gx", [NT, 2, P], I32)
        gxf = sb("prep_gxf", [NT, 2, P])
        rbx = sb("prep_rbx", [NT, P * 16])
        shx = sb("prep_shx", [NT, P * 4])
        jrow = sb("prep_jrow", [1, NT], I32)
        Z = ST // 9
        rows = sb("prep_rows", [Z, 9, P], BF16)
        ps = [es.enter_context(nc.psum_tensor(f"prep_ps{i}", [P, 512], F32)) for i in range(8)]
        block = es.enter_context(nc.Block())

        @block.sync
        def _(sp):
            sp.dma_start(nat[:, 0], k.src.rearrange("(q r p) -> q r p", r=U, p=P)).then_inc(S["ld"], 16)
            sp.dma_start(nat[:, 1], k.dst.rearrange("(q r p) -> q r p", r=U, p=P)).then_inc(S["ld"], 16)
            sp.dma_start(k.x[:, :, :], tiles(k.x_in)).then_inc(S["st"], 16)
            sp.wait_ge(S["gat"], 64)
            sp.dma_start(k.rbf_extra, rbx[:, :]).then_inc(S["st"], 16)
            sp.dma_start(k.sh_extra, shx[:, :]).then_inc(S["st"], 16)
            sp.wait_ge(S["rd"], 3)
            sp.dma_start(k.dst_rows.rearrange("(m q) p -> q m p", q=Z), rows[:, :, :]).then_inc(S["st"], 16)
            sp.wait_ge(S["st"], 64)

        @block.gpsimd
        def _(g):
            c = Count(S["pool"])
            c.inc(g.memset(k.ident[:, :], 0.0))
            c.inc(g.memset(k.ones[:, :], 1.0))
            c.inc(g.memset(first[:, :], 0.0))
            c.inc(g.memset(last[:, :], 0.0))
            c.inc(g.iota(ioti[:, :], pattern=[[1, 128]], base=0, channel_multiplier=0))
            c.inc(g.iota(thri[:, :], pattern=[[0, 1]], base=0, channel_multiplier=P))
            c.inc(g.iota(jrow[:, :], pattern=[[1, NT]], base=0, channel_multiplier=0))
            c.inc(g.iota(pi[:, :], pattern=[[0, 1]], base=0, channel_multiplier=1))
            g.wait_ge(c.sem, 4)
            c.inc(g.affine_select(out=k.ident[:, :], in_=k.ident[:, :], compare_op=ALU.not_equal, fill=1.0,
                                  base=0, pattern=[[-1, 128]], channel_multiplier=1))
            c.inc(g.affine_select(out=first[:, :], in_=first[:, :], compare_op=ALU.not_equal, fill=1.0,
                                  base=0, pattern=[[0, P]], channel_multiplier=1))
            c.inc(g.affine_select(out=last[:, :], in_=last[:, :], compare_op=ALU.not_equal, fill=1.0,
                                  base=1 - P, pattern=[[0, P]], channel_multiplier=1))
            g.wait_ge(S["tb"], 1)
            at = bass.IndirectOffsetOnAxis(ap=tji[:, :], axis=0)
            for out, table in ((gx[:, 0, :], k.src.rearrange("(t p) -> t p", p=P)),
                               (gx[:, 1, :], k.dst.rearrange("(t p) -> t p", p=P)),
                               (rbx[:, :], k.rbf.rearrange("(t p) f -> t (p f)", p=P)),
                               (shx[:, :], k.sh.rearrange("(t p) f -> t (p f)", p=P))):
                g.indirect_dma_start(out, None, table, at).then_inc(S["gat"], 16)

        @block.tensor
        def _(pe):
            pe.wait_ge(S["pool"], 11)
            pe.wait_ge(S["cast"], 2)
            for a in range(2):
                for r in range(U):
                    ins = nc.tensor.transpose(ps[2 * a + r // 5][:, (r % 5) * Q:(r % 5 + 1) * Q],
                                              natf[:, a, r, :], k.ident[0:Q, 0:Q])
            ins.then_inc(S["tr"], 1)
            pe.wait_ge(S["ev"], 4)
            for a, pick in enumerate((first, last)):
                for hf in range(2):
                    ins = nc.tensor.matmul(ps[4 + 2 * a + hf][:, 0:ET // 2], pick[:, :],
                                           dstf[:, hf * (ET // 2):(hf + 1) * (ET // 2)], start=True, stop=True)
            ins.then_inc(S["bc"], 1)
            pe.wait_ge(S["cmp"], 4)
            for hf in range(2):
                ins = nc.tensor.matmul(ps[hf][:, 0:ET // 2], k.ones[0:NT, 0:P],
                                       cmp[:, 0, hf * (ET // 2):(hf + 1) * (ET // 2)], start=True, stop=True)
            ins.then_inc(S["jw"], 1)
            pe.wait_ge(S["gx"], 2)
            for a in range(2):
                nc.tensor.transpose(ps[2][:, a * NT:(a + 1) * NT], gxf[:, a, :], k.ident[0:NT, 0:NT])
            nc.tensor.transpose(ps[3][0:1, 0:NT], tj[:, :], k.ident[0:NT, 0:NT]).then_inc(S["trx"], 1)
            pe.wait_ge(S["row"], 7)
            for m in range(9):
                ins = nc.tensor.transpose(ps[4 + m // 4][0:Z, (m % 4) * P:(m % 4 + 1) * P],
                                          k.dst_in[:, m * Z:(m + 1) * Z], k.ident[0:P, 0:P])
            ins.then_inc(S["rt"], 1)

        @block.vector
        def _(v):
            v.wait_ge(S["ld"], 32)
            nc.vector.tensor_copy(natf[:, 0], nat[:, 0]).then_inc(S["cast"], 1)
            nc.vector.tensor_copy(natf[:, 1], nat[:, 1]).then_inc(S["cast"], 1)
            v.wait_ge(S["pool"], 8)
            nc.vector.tensor_copy(k.iota[:, :], ioti[:, 0:P]).then_inc(S["v"], 1)
            nc.vector.tensor_copy(thr[:, :], thri[:, :]).then_inc(S["v"], 1)
            v.wait_ge(S["tr"], 1)
            for hf in range(2):
                r5 = slice(5 * hf, 5 * hf + 5)

                def by_tile(t):
                    return t[:, 0:ET].rearrange("p (q r) -> p r q", r=U)[:, r5, :]

                def of(n):
                    return ps[n][:, 0:5 * Q].rearrange("p (r q) -> p r q", q=Q)

                nc.vector.tensor_copy(by_tile(k.src_of), of(hf)).then_inc(S["ev"], 1)
                nc.vector.tensor_copy(by_tile(dstf), of(2 + hf)).then_inc(S["ev"], 1)
            v.wait_ge(S["ev"], 4)
            nc.vector.tensor_copy(k.lane[:, :], pi[:, :]).then_inc(S["row"], 1)
            v.wait_ge(S["bc"], 1)
            v.wait_ge(S["v"], 2)
            for a in range(2):
                for hf in range(2):
                    nc.vector.tensor_scalar(cmp[:, a, hf * (ET // 2):(hf + 1) * (ET // 2)],
                                            ps[4 + 2 * a + hf][0:NT, 0:ET // 2], thr[0:NT, 0:1], None,
                                            ALU.is_lt).then_inc(S["cmp"], 1)
            v.wait_ge(S["cmp"], 4)
            nc.vector.tensor_reduce(cnt[:, :], cmp[:, :, :], AX.X, ALU.add).then_inc(S["red"], 1)
            v.wait_ge(S["red"], 1)
            nc.vector.tensor_scalar(tj[:, :], cnt[:, 1:2], float(ET - 1), None, ALU.min).then_inc(S["red"], 1)
            nc.vector.tensor_tensor(ok[:, :], cnt[:, 0:1], cnt[:, 1:2], ALU.is_le).then_inc(S["red"], 1)
            v.wait_ge(S["red"], 3)
            nc.vector.tensor_copy(tji[:, :], tj[:, :]).then_inc(S["tb"], 1)
            nc.vector.scalar_tensor_tensor(out=base[:, :], in0=ok[:, :], scalar=FAR, in1=thr[0:NT, :],
                                           op0=ALU.mult, op1=ALU.add).then_inc(S["red"], 1)
            v.wait_ge(S["jw"], 1)
            for hf in range(2):
                nc.vector.tensor_scalar(jb[:, hf * (ET // 2):(hf + 1) * (ET // 2)], ps[hf][:, 0:ET // 2],
                                        -1.0, float(NT - 1), ALU.mult, ALU.add).then_inc(S["red"], 1)
            v.wait_ge(S["red"], 6)
            nc.vector.tensor_copy(k.node_tile[:, 0:ET], jb[0:1, :]).then_inc(S["row"], 1)
            nc.vector.tensor_copy(k.node_tile[:, ET:ST], jrow[:, :]).then_inc(S["row"], 1)
            nc.vector.scalar_tensor_tensor(out=k.dst_in[:, 0:ET], in0=jb[:, :], scalar=-float(P),
                                           in1=dstf[:, :], op0=ALU.mult, op1=ALU.add).then_inc(S["row"], 1)
            v.wait_ge(S["gat"], 64)
            nc.vector.tensor_copy(gxf[:, 0], gx[:, 0]).then_inc(S["gx"], 1)
            nc.vector.tensor_scalar(gxf[:, 1], gx[:, 1], base[:, 0:1], None, ALU.subtract).then_inc(S["gx"], 1)
            v.wait_ge(S["trx"], 1)
            nc.vector.tensor_copy(k.src_of[:, ET:ST], ps[2][:, 0:NT]).then_inc(S["row"], 1)
            nc.vector.tensor_copy(k.dst_in[:, ET:ST], ps[2][:, NT:2 * NT]).then_inc(S["row"], 1)
            nc.vector.tensor_copy(k.extra_at[:, :], ps[3][0:1, 0:NT]).then_inc(S["row"], 1)
            v.wait_ge(S["rt"], 1)
            for n, (m0, m1) in enumerate(((0, 4), (4, 8), (8, 9))):
                nc.vector.tensor_copy(rows[:, m0:m1, :], ps[4 + n][0:Z, 0:(m1 - m0) * P].rearrange(
                    "q (m p) -> q m p", p=P)).then_inc(S["rd"], 1)


def row_stats(nc, k, tag, src, width):
    es, s = scope(nc, [tag + n for n in ("st", "ag", "ep", "sq", "rc")])
    with es:
        raw = es.enter_context(nc.sbuf_tensor(tag + "raw", [P, NT, 6], F32))
        mv = es.enter_context(nc.sbuf_tensor(tag + "mv", [P, NT, 2], F32))
        std = es.enter_context(nc.sbuf_tensor(tag + "std", [P, NT], F32))
        block = es.enter_context(nc.Block())

        @block.vector
        def _(v):
            for j in range(NT):
                nc.vector.bn_stats(raw[:, j, :], src[:, j, 0:width]).then_inc(s[tag + "st"], 1)
            for j in range(NT):
                v.wait_ge(s[tag + "st"], j + 1)
                nc.vector.bn_aggr(mv[:, j, :], raw[:, j, :]).then_inc(s[tag + "ag"], 1)
            v.wait_ge(s[tag + "ag"], NT)
            nc.vector.tensor_copy(k.mean[:, :], mv[:, :, 0]).then_inc(s[tag + "ep"], 1)
            nc.vector.tensor_scalar(k.rstd[:, :], mv[:, :, 1], EPS, None, ALU.add).then_inc(s[tag + "ep"], 1)
            v.wait_ge(s[tag + "sq"], 1)
            nc.vector.reciprocal(k.rstd[:, :], std[:, :]).then_inc(s[tag + "rc"], 1)
            v.wait_ge(s[tag + "rc"], 1)
            nc.vector.scalar_tensor_tensor(out=k.shift[:, :], in0=k.mean[:, :], scalar=-1.0, in1=k.rstd[:, :],
                                           op0=ALU.mult, op1=ALU.mult).then_inc(s[tag + "rc"], 1)
            v.wait_ge(s[tag + "rc"], 2)

        @block.scalar
        def _(a):
            a.wait_ge(s[tag + "ep"], 2)
            nc.scalar.activation(std[:, :], k.rstd[:, :], ACT.Sqrt).then_inc(s[tag + "sq"], 1)


def project(nc, k, tag, load_weights, weight_loads, outputs, width, split=False, att=None, self_score=False):
    names = ["w", "h", "tr", "ht", "mm", "sc", "o", "sum", "fold", "st0", "st1", "kp"]
    es, s = scope(nc, [tag + n for n in names])
    with es:
        S = {n: s[tag + n] for n in names}

        def sb(name, shape, dt=F32):
            return es.enter_context(nc.sbuf_tensor(tag + name, shape, dt))

        w = sb("w", [128, 2, width // 2 if split else width])
        h = sb("hh", [P, 2, D])
        hT = sb("hT", [128, 2, 2, P])
        ow = width + (2 * H if self_score else 0)
        o = sb("o", [P, 2, ow])
        if att:
            vec = sb("vec", [128, 2, D])
            prod = sb("prod", [128, 2, 2, D])
        psT = es.enter_context(nc.psum_tensor(tag + "psT", [128, 2, 512], F32))
        psO = es.enter_context(nc.psum_tensor(tag + "psO", [P, 2, 512], F32))
        block = es.enter_context(nc.Block())
        stores = [S["st0"], S["st1"]]

        if split:
            @block.gpsimd
            def _(g):
                g.memset(w[:, :, :], 0.0).then_inc(S["fold"], 1)

        @block.sync
        def _(sp):
            if split:
                sp.wait_ge(S["fold"], 1)
            load_weights(sp, w, S["w"])
            if att:
                for q in range(2):
                    sp.dma_start(vec[:, q, :], att[q].rearrange("h c -> (h c)").partition_broadcast(128)
                                 ).then_inc(S["w"], 16)

            def store(t, b, i):
                sp.wait_ge(S["o"], t + 1)
                for table, off, wd in outputs:
                    sp.dma_start(table[ds(t * P, P), :], o[:, b, off:off + wd]).then_inc(stores[b], 16)

            pairs(sp, NT, store)
            for b in range(2):
                sp.wait_ge(stores[b], 16 * len(outputs) * (NT // 2))

        @block.scalar
        def _(a):
            def work(t, b, i):
                if later(i):
                    a.wait_ge(S["tr"], t - 1)
                hv = h[:, b, :]
                xv = k.x[:, ds(t, 1), :].rearrange("p a d -> p (a d)")
                sc, sh = k.rstd[:, ds(t, 1)], k.shift[:, ds(t, 1)]
                if split:
                    nc.scalar.activation(hv[:, 0:C], xv[:, 0:C], ACT.Relu, bias=sh, scale=sc)
                    nc.scalar.activation(hv[:, C:D].rearrange("p (x c) -> p x c", x=3),
                                         xv[:, C:D].rearrange("p (c x) -> p x c", x=3), ACT.Relu, bias=sh,
                                         scale=sc).then_inc(S["h"], 1)
                else:
                    nc.scalar.activation(hv, xv, ACT.Relu, bias=sh, scale=sc).then_inc(S["h"], 1)

            def evacuate(t, b, i):
                a.wait_ge(S["mm"], t + 1)
                if later(i):
                    a.wait_ge(stores[b], i * (16 * len(outputs)))
                    if att:
                        a.wait_ge(S["kp"], t - 1)
                done = S["sc" if self_score else "o"]
                if split:
                    pv = psO[:, b, :].rearrange("p (k q c) -> p q k c", k=2, q=2)
                    ov = o[:, b, 0:2 * D].rearrange("p (q k c) -> p q k c", k=2, q=2)
                    nc.scalar.activation(ov[:, 0], pv[:, 0], ACT.Copy)
                    nc.scalar.activation(ov[:, 1], pv[:, 1], ACT.Copy).then_inc(done, 1)
                else:
                    nc.scalar.activation(o[:, b, 0:width], psO[:, b, 0:width], ACT.Copy).then_inc(done, 1)

            lagged(a, NT, work, evacuate)

        @block.tensor
        def _(pe):
            pe.wait_ge(S["w"], 16 * (weight_loads + (2 if att else 0)))
            if att:
                pe.wait_ge(S["fold"], 2)

            def turn(t, b, i):
                pe.wait_ge(S["h"], t + 1)
                if later(i):
                    pe.wait_ge(S["ht"], t - 1)
                for q in range(2):
                    ins = nc.tensor.transpose(psT[:, b, q * P:(q + 1) * P], h[:, b, q * 128:(q + 1) * 128],
                                              k.ident[0:P, 0:P])
                ins.then_inc(S["tr"], 1)

            def multiply(t, b, i):
                pe.wait_ge(S["ht"], t + 1)
                if later(i):
                    pe.wait_ge(S["sc" if self_score else "o"], t - 1)
                for q in range(2):
                    if split:
                        ins = nc.tensor.matmul(psO[:, b, q * D:(q + 1) * D], hT[:, b, q, :], w[:, q, :],
                                               start=True, stop=True)
                    else:
                        ins = nc.tensor.matmul(psO[:, b, 0:width], hT[:, b, q, :], w[:, q, :],
                                               start=(q == 0), stop=(q == 1))
                ins.then_inc(S["mm"], 1)

            skewed(pe, NT, turn, multiply)

        @block.vector
        def _(v):
            if att:
                v.wait_ge(S["w"], 16 * (weight_loads + 2))
                for q in range(2):
                    for blk in range(2):
                        nc.vector.tensor_tensor(prod[:, blk, q, :], w[:, blk, 0:D], vec[:, q, :],
                                                ALU.mult).then_inc(S["sum"], 1)
                v.wait_ge(S["sum"], 4)
                for blk in range(2):
                    nc.vector.tensor_reduce(w[:, blk, D:D + 2 * H],
                                            prod[:, blk].rearrange("p q (h c) -> p (q h) c", c=CH),
                                            AX.X, ALU.add).then_inc(S["fold"], 1)

            def copy(t, b, i):
                v.wait_ge(S["tr"], t + 1)
                if later(i):
                    v.wait_ge(S["mm"], t - 1)
                nc.vector.tensor_copy(hT[:, b, :, :].rearrange("p q c -> p (q c)"),
                                      psT[:, b, 0:2 * P]).then_inc(S["ht"], 1)

            def own_score(t, b, i):
                v.wait_ge(S["sc"], t + 1)
                both = o[:, b, D + 3 * H:D + 4 * H]
                nc.vector.tensor_tensor(both, o[:, b, D:D + H], o[:, b, D + H:D + 2 * H],
                                        ALU.add).then_inc(S["sum"], 1)
                v.wait_ge(S["sum"], t + 5)
                nc.vector.scalar_tensor_tensor(out=o[:, b, D + 2 * H:D + 3 * H], in0=both, scalar=0.2, in1=both,
                                               op0=ALU.mult, op1=ALU.max).then_inc(S["o"], 1)

            def keep(t, b, i):
                v.wait_ge(S["o"], t + 1)
                w = 2 * H if self_score else H
                nc.vector.tensor_copy(k.recv[:, ds(t, 1), 0:w].rearrange("p a h -> p (a h)"),
                                      o[:, b, D + H:D + H + w]).then_inc(S["kp"], 1)

            def own(t, b, i):
                if self_score:
                    own_score(t, b, i)
                keep(t, b, i)

            if att:
                lagged(v, NT, copy, own)
            else:
                pairs(v, NT, copy)


def aggregate(nc, k, tag, table, weights=None, R=0, degree=False):
    names = ["idx0", "idx1", "lw0", "lw1", "lr0", "lr1", "sel", "off", "msg", "mm", "acc", "wt", "ww", "cl", "go"]
    streams = [] if weights else ["gat0", "gat1"]
    es, s = scope(nc, [tag + n for n in names], [(tag + n, k.gathered.pop()) for n in streams])
    with es:
        S = {n: s[tag + n] for n in names + streams}

        def sb(name, shape, dt=F32):
            return es.enter_context(nc.sbuf_tensor(tag + name, shape, dt))

        def pt(name, shape):
            return es.enter_context(nc.psum_tensor(tag + name, shape, F32))

        att = weights is not None
        W = D + R + (1 if degree else 0)
        idx = [sb(f"idx{b}", [P, U], I32) for b in range(2)]
        rows = [sb(f"rows{b}", [P, U, D + (1 if degree else 0)]) for b in range(2)]
        sel = [sb(f"sel{b}", [P, U, P]) for b in range(2)]
        if att:
            off = sb("off", [P, U, P])
            msg = [sb(f"msg{b}", [P, U, AW]) for b in range(2)]
            wT = [sb(f"wT{b}", [R, U, P]) for b in range(2)]
            psW = pt("psW", [P, 2, 512])
        psA = pt("psA", [P, 4, 512])
        block = es.enter_context(nc.Block())
        i_sem, l_sem = [S["idx0"], S["idx1"]], [S["lw0"], S["lw1"]]
        r_sem = [S["lr0"], S["lr1"]] if att else [S["gat0"], S["gat1"]]
        per = 16 if att else 16 * U

        def times_weights(eng, b, steps):
            return eng.tensor_tensor(
                msg[b][:, steps, 0:D].rearrange("p u (h c) -> p u h c", c=CH),
                rows[b][:, steps, 0:D].rearrange("p u (h c) -> p u h c", c=CH),
                msg[b][:, steps, D:D + H].unsqueeze(3).broadcast_to([P, steps.stop - steps.start, H, CH]), ALU.mult)

        @block.sync
        def _(sp):
            def load(t, b, i):
                if not att:
                    if later(i):
                        sp.wait_ge(r_sem[b], i * per)
                    sp.dma_start(idx[b][:, :], k.src_of[:, ds(t * U, U)]).then_inc(i_sem[b], 16)
                else:
                    if later(i):
                        sp.wait_ge(S["msg"], t - 1)
                        sp.sem_inc(S["go"], 1)
                    sp.dma_start(rows[b][:, :, :], tiles(k.edge_rows[ds(t * (U * P), U * P), :])).then_inc(r_sem[b], 16)
                    if later(i):
                        sp.wait_ge(S["wt"], t - 1)
                    last = (weights[0][ds(t * U, U)] if not isinstance(t, int) or t < EB else
                            weights[1][(t - EB) * U:(t - EB + 1) * U])
                    sp.dma_start(wT[b][:, :, :], last.rearrange("t r e -> r t e")).then_inc(l_sem[b], 16)

            if att:
                load(0, 0, 0)
                load(1, 1, 0)
                with sp.Fori(1, EB // 2) as i:
                    load(i * 2, 0, i)
                    load(i * 2 + 1, 1, i)
                for t in range(EB // 2 * 2, NB):
                    load(t, t % 2, t // 2)
            else:
                pairs(sp, NB, load)

        @block.gpsimd
        def _(g):
            def weigh(t, b, i):
                g.wait_ge(r_sem[b], i * per + per)
                g.wait_ge(S["ww"], t + 1)
                times_weights(g, b, slice(0, U)).then_inc(S["msg"], 1)

            def gather(t, b, i):
                g.wait_ge(i_sem[b], i * 16 + 16)
                if later(i):
                    g.wait_ge(S["mm"], (t - 1) * U)
                g.sem_inc(S["go"], 1)
                for u in range(U):
                    g.indirect_dma_start(rows[b][:, u, 0:D], None, table,
                                         bass.IndirectOffsetOnAxis(ap=idx[b][:, u:u + 1], axis=0)
                                         ).then_inc(r_sem[b], 16)

            pairs(g, NB, weigh if att else gather)

        @block.scalar
        def _(a):
            if att:
                def place(t, b, i):
                    a.wait_ge(S["wt"], t + 1)
                    if later(i):
                        a.wait_ge(S["mm"], (t - 1) * U)
                    nc.scalar.activation(msg[b][:, :, D:D + R], psW[:, b, 0:U * R].rearrange(
                        "p (u r) -> p u r", r=R), ACT.Copy).then_inc(S["ww"], 1)

                def one_hot(t, b, i):
                    if not isinstance(t, int) or t:
                        a.wait_ge(S["sel"], t)
                    for u in range(U):
                        ins = nc.scalar.activation(off[:, u, :], k.iota[:, :], ACT.Abs,
                                                   bias=k.dst_in[:, ds(t * U + u, 1)], scale=-1.0)
                    ins.then_inc(S["off"], 1)
                    if later(i):
                        a.wait_ge(S["mm"], (t - 1) * U)
                    a.wait_ge(S["off"], t + 1)
                    nc.scalar.activation(sel[b][:, :, :], off[:, :, :], ACT.Relu, bias=k.ones[0:P, 0:1],
                                         scale=-1.0).then_inc(S["sel"], 1)

                def body(t, b, i):
                    place(t, b, i)
                    one_hot(t, b, i)

                pairs(a, NB, body)

        @block.tensor
        def _(pe):
            def turn(t, b, i):
                pe.wait_ge(l_sem[b], i * 16 + 16)
                if later(i):
                    pe.wait_ge(S["ww"], t - 1)
                pe.sem_inc(S["go"], 1)
                for u in range(U):
                    ins = nc.tensor.transpose(psW[:, b, u * R:(u + 1) * R], wT[b][:, u, :], k.ident[0:R, 0:R])
                ins.then_inc(S["wt"], 1)

            def multiply(t, b, i):
                pe.wait_ge(S["sel"], t + 1)
                if att:
                    pe.wait_ge(S["msg"], t + 1)
                else:
                    pe.wait_ge(r_sem[b], i * per + per)
                for u in range(U):
                    if later(i) or b * U + u >= 4:
                        pe.wait_ge(S["acc"], t * U + (u - 3))
                    slot = psA[:, (b * U + u) % 4, :]
                    value = msg[b][:, u, 0:W] if att else rows[b][:, u, 0:W]
                    nc.tensor.matmul(slot[:, 0:W], sel[b][:, u, :], value, start=True, stop=True).then_inc(S["mm"], 1)

            if att:
                skewed(pe, NB, turn, multiply)
            else:
                pe.wait_ge(S["cl"], 2)
                pairs(pe, NB, multiply)

        @block.vector
        def _(v):
            if degree:
                for b in range(2):
                    nc.vector.memset(rows[b][:, :, D:], 1.0).then_inc(S["cl"], 1)
            nc.vector.memset(k.acc[:, :, 0:W], 0.0).then_inc(S["cl"], 1)

            def prepare_batch(t, b, i):
                if later(i):
                    v.wait_ge(S["mm"], (t - 1) * U)
                nc.vector.tensor_tensor(sel[b][:, :, :], k.iota[:, :].unsqueeze(1).broadcast_to([P, U, P]),
                                        k.dst_in[:, ds(t * U, U)].unsqueeze(2).broadcast_to([P, U, P]),
                                        ALU.is_equal).then_inc(S["sel"], 1)

            def add(t, b, i):
                _, at = nc.values_load_multi_w_load_instructions(
                    k.node_tile[0:1, ds(t * U, U)], engines=[DVE], min_val=0, max_val=NT - 1,
                    skip_runtime_bounds_check_because="made in prepare() from counts of at most NT - 1")
                for u in range(U):
                    if u % 2 == 0:
                        v.wait_ge(S["mm"], t * U + (u + 2))
                    if u == 0 and isinstance(t, int) and t == 0:
                        v.wait_ge(S["cl"], 3 if degree else 1)
                    else:
                        v.wait_ge(S["acc"], t * U + u)
                    to = k.acc[:, ds(at[u], 1), 0:W].rearrange("p a d -> p (a d)")
                    nc.vector.tensor_tensor(to, to, psA[:, (b * U + u) % 4, 0:W], ALU.add).then_inc(S["acc"], 1)

            if att:
                pairs(v, NB, add)
            else:
                skewed(v, NB, prepare_batch, add)
            v.wait_ge(S["acc"], ST)
            if degree:
                nc.vector.tensor_copy(k.deg[:, :], k.acc[:, :, D]).then_inc(S["cl"], 1)
                v.wait_ge(S["cl"], 4)


def convolve(nc, k, tag):
    names = ["idx0", "idx1", "lw0", "lw1", "w", "wf", "sel", "sk", "msg", "mm", "acc",
             "rt", "rx", "m1", "a1", "m2", "a2", "m3", "a3", "tp", "cl", "go"]
    es, s = scope(nc, [tag + n for n in names], [(tag + "gat0", k.gathered.pop()), (tag + "gat1", k.gathered.pop())])
    QB = U // 2
    A, B = 3 * P, 2 * P
    with es:
        S = {n: s[tag + n] for n in names + ["gat0", "gat1"]}

        def sb(name, shape, dt=F32):
            return es.enter_context(nc.sbuf_tensor(tag + name, shape, dt))

        def pt(name, shape):
            return es.enter_context(nc.psum_tensor(tag + name, shape, F32))

        idx = [sb(f"idx{b}", [P, U], I32) for b in range(2)]
        rbf = [sb(f"rbf{b}", [P, U, 16]) for b in range(2)]
        sh = [sb(f"sh{b}", [P, U, 4]) for b in range(2)]
        rows = [sb(f"rows{b}", [P, U, D]) for b in range(2)]
        sel = [sb(f"sel{b}", [P, U, P]) for b in range(2)]
        m1 = sb("m1", [32, 128])
        m2 = sb("m2", [128, 128])
        m3 = sb("m3", [128, 128])
        m4 = sb("m4", [128, D])
        rT = sb("rT", [32, A + B])
        r1 = sb("r1", [128, A + B])
        r2 = sb("r2", [128, A + B])
        r3 = [sb(f"r3{b}", [128, A + B]) for b in range(2)]
        selk = sb("selk", [P, 2, 2, 4, P])
        prod = sb("prod", [P, 2, 2, 8, C])
        psM = pt("psM", [128, 2, 512])
        psT = pt("psT", [P, 2, 2, 512])
        psA = pt("psA", [P, 2, 512])
        block = es.enter_context(nc.Block())
        g_sem, i_sem, l_sem = [S["gat0"], S["gat1"]], [S["idx0"], S["idx1"]], [S["lw0"], S["lw1"]]

        @block.sync
        def _(sp):
            sp.wait_ge(S["wf"], 3)
            for o in (0, 1):
                for w, src, n in ((m1, k.w["M1"], 16), (m2, k.w["M2"], C), (m3, k.w["M3"], C)):
                    sp.dma_start(w[o * n:(o + 1) * n, o * C:(o + 1) * C], src).then_inc(S["w"], 16)
                sp.dma_start(m4[o * C:(o + 1) * C, :], k.w["M4"]).then_inc(S["w"], 16)

            def load(t, b, i):
                if later(i):
                    sp.wait_ge(g_sem[b], i * (16 * U))
                sp.dma_start(idx[b][:, :], k.src_of[:, ds(t * U, U)]).then_inc(i_sem[b], 16)
                if later(i):
                    sp.wait_ge(S["sk"], (t - 1) * QB)
                    sp.wait_ge(S["rt"], t - 1)
                    sp.sem_inc(S["go"], 1)
                if not isinstance(t, int) or t < EB:
                    f = tiles(k.rbf[ds(t * (U * P), U * P), :])
                    y = tiles(k.sh[ds(t * (U * P), U * P), :])
                else:
                    r = slice((t - EB) * U, (t - EB + 1) * U)
                    f = k.rbf_extra[r].rearrange("t (p f) -> p t f", p=P)
                    y = k.sh_extra[r].rearrange("t (p f) -> p t f", p=P)
                sp.dma_start(rbf[b][:, :, :], f).then_inc(l_sem[b], 16)
                sp.dma_start(sh[b][:, :, :], y).then_inc(l_sem[b], 16)

            load(0, 0, 0)
            load(1, 1, 0)
            with sp.Fori(1, EB // 2) as i:
                load(i * 2, 0, i)
                load(i * 2 + 1, 1, i)
            for t in range(EB // 2 * 2, NB):
                load(t, t % 2, t // 2)

        @block.gpsimd
        def _(g):
            for w in (m1, m2, m3):
                g.memset(w[:, :], 0.0).then_inc(S["wf"], 1)

            def gather(t, b, i):
                g.wait_ge(i_sem[b], i * 16 + 16)
                if later(i):
                    g.wait_ge(S["msg"], (t - 1) * QB)
                g.sem_inc(S["go"], 1)
                for u in range(U):
                    g.indirect_dma_start(rows[b][:, u, :], None, k.table,
                                         bass.IndirectOffsetOnAxis(ap=idx[b][:, u:u + 1], axis=0)
                                         ).then_inc(g_sem[b], 16)

            pairs(g, NB, gather)

        @block.scalar
        def _(a):
            def leave(n, out, src, act, free, freed):
                if free is not None:
                    a.wait_ge(S[free], freed)
                nc.scalar.activation(out[:, 0:A], src[:, 0, 0:A], act)
                nc.scalar.activation(out[:, A:A + B], src[:, 1, 0:B], act).then_inc(S[n], 1)

            def stage(q, t, b, i):
                first = isinstance(t, int) and t == 0
                if q == 0:
                    a.wait_ge(S["rt"], t + 1)
                    leave("rx", rT, psM[0:32], ACT.Copy, None if first else "m1", t)
                if q == 1:
                    a.wait_ge(S["m1"], t + 1)
                    leave("a1", r1, psM, ACT.Silu, None if first else "m2", t)
                if q == 2:
                    a.wait_ge(S["m2"], t + 1)
                    leave("a2", r2, psM, ACT.Silu, None if first else "m3", t)
                if q == 3:
                    a.wait_ge(S["m3"], t + 1)
                    leave("a3", r3[b], psM, ACT.Silu, "tp" if later(i) else None, (t - 1) * QB)

            def scale(t, b, i, q):
                if q == 0:
                    a.wait_ge(S["sel"], t + 1)
                    a.wait_ge(l_sem[b], i * 32 + 32)
                if later(i) or b * QB + q >= 2:
                    a.wait_ge(S["mm"], t * U + (2 * q - 2))
                par = (b * QB + q) % 2
                for u in range(2):
                    for y in range(4):
                        ins = nc.scalar.activation(selk[:, par, u, y, :], sel[b][:, 2 * q + u, :], ACT.Copy,
                                                   scale=sh[b][:, 2 * q + u, y:y + 1])
                ins.then_inc(S["sk"], 1)

            for q in range(4):
                stage(q, 0, 0, 0)
            scale(0, 0, 0, 0)

            def body(t, b, i, more):
                for q in range(QB):
                    if more and q < 4:
                        stage(q, t + 1, 1 - b, i + b)
                    if q < QB - 1:
                        scale(t, b, i, q + 1)
                    elif more:
                        scale(t + 1, 1 - b, i + b, 0)

            ends(a, NB, body)

        @block.tensor
        def _(pe):
            pe.wait_ge(S["w"], 16 * 8)
            pe.wait_ge(S["wf"], 4)

            def stage(q, t, b, i):
                first = isinstance(t, int) and t == 0
                if q == 0:
                    pe.wait_ge(l_sem[b], i * 32 + 32)
                    if not first:
                        pe.wait_ge(S["a3"], t)
                    for n in range(QB):
                        ins = nc.tensor.transpose(psM[0:32, n // 3, (n % 3) * P:(n % 3 + 1) * P],
                                                  rbf[b][:, 2 * n:2 * n + 2, :].rearrange("p u f -> p (u f)"),
                                                  k.ident[0:P, 0:P])
                    ins.then_inc(S["rt"], 1)
                else:
                    w, r, before, out = {1: (m1, rT, "rx", "m1"), 2: (m2, r1, "a1", "m2"),
                                         3: (m3, r2, "a2", "m3")}[q] if 1 <= q <= 3 else (None,) * 4
                    if w is None:
                        return
                    pe.wait_ge(S[before], t + 1)
                    nc.tensor.matmul(psM[:, 0, 0:A], w[:, :], r[:, 0:A], start=True, stop=True)
                    nc.tensor.matmul(psM[:, 1, 0:B], w[:, :], r[:, A:A + B], start=True,
                                     stop=True).then_inc(S[out], 1)

            def last_layer(t, b, i, q):
                if q == 0:
                    pe.wait_ge(S["a3"], t + 1)
                if later(i) or b * QB + q >= 2:
                    pe.wait_ge(S["msg"], t * QB + (q - 1))
                for u in range(2):
                    half = slice(u * C, u * C + C)
                    ins = nc.tensor.matmul(psT[:, (b * QB + q) % 2, u, 0:D], r3[b][half, q * P:(q + 1) * P],
                                           m4[half, :], start=True, stop=True)
                ins.then_inc(S["tp"], 1)

            def multiply(t, b, i, q):
                pe.wait_ge(S["msg"], t * QB + (q + 1))
                pe.wait_ge(S["sk"], t * QB + (q + 1))
                par = (b * QB + q) % 2
                for u in range(2):
                    if later(i) or b * U + 2 * q + u >= 2:
                        pe.wait_ge(S["acc"], t * U + (2 * q + u - 1))
                    out = psA[:, u, 0:D]
                    pr = prod[:, par, u, :, :]
                    nc.tensor.matmul(out, selk[:, par, u, 0, :], pr[:, 0:4, :].rearrange("p k c -> p (k c)"),
                                     start=True, stop=False)
                    for x in range(3):
                        ins = nc.tensor.matmul(out.rearrange("p (k c) -> p k c", k=4)[:, 0:x + 2:x + 1, :],
                                               selk[:, par, u, 1 + x, :], pr[:, 4 + x:8:3 - x, :],
                                               start=False, stop=(x == 2))
                    ins.then_inc(S["mm"], 1)

            for q in range(4):
                stage(q, 0, 0, 0)
            last_layer(0, 0, 0, 0)

            def body(t, b, i, more):
                for q in range(QB):
                    if more:
                        stage(q, t + 1, 1 - b, i + b)
                    if q < QB - 1:
                        last_layer(t, b, i, q + 1)
                    elif more:
                        last_layer(t + 1, 1 - b, i + b, 0)
                    multiply(t, b, i, q)

            ends(pe, NB, body)

        @block.vector
        def _(v):
            nc.vector.memset(k.acc[:, :, 0:D], 0.0).then_inc(S["cl"], 1)
            v.wait_ge(S["w"], 16 * 8)
            inv3 = float(1.0 / np.sqrt(np.float32(3.0)))
            nc.vector.tensor_scalar(m4[:, 3 * C:], m4[:, 3 * C:], inv3, None, ALU.mult).then_inc(S["wf"], 1)

            def select(t, b, i):
                if later(i):
                    v.wait_ge(S["sk"], (t - 1) * QB)
                nc.vector.tensor_tensor(sel[b][:, :, :], k.iota[:, :].unsqueeze(1).broadcast_to([P, U, P]),
                                        k.dst_in[:, ds(t * U, U)].unsqueeze(2).broadcast_to([P, U, P]),
                                        ALU.is_equal).then_inc(S["sel"], 1)

            def products(t, b, i, q):
                if q == 0:
                    v.wait_ge(g_sem[b], i * (16 * U) + 16 * U)
                v.wait_ge(S["tp"], t * QB + (q + 1))
                if later(i) or b * QB + q >= 2:
                    v.wait_ge(S["mm"], t * U + (2 * q - 2))
                par = (b * QB + q) % 2
                x = rows[b][:, 2 * q:2 * q + 2, :].rearrange("p u (k c) -> p u k c", c=C)
                tp = psT[:, par, :, 0:D].rearrange("p u (k c) -> p u k c", c=C)
                nc.vector.tensor_tensor(prod[:, par, :, 0:8:7, :], tp[:, :, 0:2, :],
                                        x[:, :, 0:1, :].broadcast_to([P, 2, 2, C]), ALU.mult)
                for u in range(2):
                    ins = nc.vector.tensor_tensor(
                        prod[:, par, u, 1:7, :].rearrange("p (k x) c -> p k x c", k=2),
                        tp[:, u, 2:4, :].unsqueeze(2).broadcast_to([P, 2, 3, C]),
                        x[:, u, 1:4, :].unsqueeze(1).broadcast_to([P, 2, 3, C]), ALU.mult)
                ins.then_inc(S["msg"], 1)

            def add(t, b, i, q, at):
                for u in range(2):
                    n = 2 * q + u
                    v.wait_ge(S["mm"], t * U + (n + 1))
                    if isinstance(t, int) and t * U + n == 0:
                        v.wait_ge(S["cl"], 1)
                    else:
                        v.wait_ge(S["acc"], t * U + n)
                    to = k.acc[:, ds(at[n], 1), 0:D].rearrange("p a d -> p (a d)")
                    nc.vector.tensor_tensor(to, to, psA[:, u, 0:D], ALU.add).then_inc(S["acc"], 1)

            select(0, 0, 0)
            products(0, 0, 0, 0)

            def body(t, b, i, more):
                _, at = nc.values_load_multi_w_load_instructions(
                    k.node_tile[0:1, ds(t * U, U)], engines=[DVE], min_val=0, max_val=NT - 1,
                    skip_runtime_bounds_check_because="made in prepare() from counts of at most NT - 1")
                for q in range(QB):
                    if q == 2 and more:
                        select(t + 1, 1 - b, i + b)
                    if q < QB - 1:
                        products(t, b, i, q + 1)
                    elif more:
                        products(t + 1, 1 - b, i + b, 0)
                    add(t, b, i, q, at)

            ends(v, NB, body)
            v.wait_ge(S["acc"], ST)


def contract(nc, k, tag):
    names = ["w", "wz", "cp", "skip0", "skip1", "tr", "at", "lin", "a", "sq", "v", "c", "b0", "b1", "out", "o"]
    es, s = scope(nc, [tag + n for n in names])
    with es:
        S = {n: s[tag + n] for n in names}

        def sb(name, shape):
            return es.enter_context(nc.sbuf_tensor(tag + name, shape, F32))

        skip = [sb(f"skip{b}", [P, D]) for b in range(2)]
        wl = sb("wl", [128, 4, C])
        wb = sb("wb", [C, 2, C])
        c0 = sb("c0", [C, 5])
        c1 = sb("c1", [C, 4])
        sums = sb("sums", [P, 2, D])
        aT = sb("aT", [128, 2, 2, P])
        A = sb("A", [C, 2, 4, P])
        sq = sb("sq", [C, 2, 3, P])
        vv = sb("vv", [C, 2, P])
        q0 = sb("q0", [C, P])
        q1 = sb("q1", [C, P])
        B = sb("B", [C, 2, 4, P])
        psT = es.enter_context(nc.psum_tensor(tag + "psT", [128, 2, 512], F32))
        psL = es.enter_context(nc.psum_tensor(tag + "psL", [C, 2, 512], F32))
        psO = es.enter_context(nc.psum_tensor(tag + "psO", [P, 2, 512], F32))
        block = es.enter_context(nc.Block())
        skips = [S["skip0"], S["skip1"]]

        @block.gpsimd
        def _(g):
            g.memset(wl[:, :, :], 0.0).then_inc(S["wz"], 1)

            def stage(t, b, i):
                if later(i):
                    g.wait_ge(S["tr"], t - 1)
                g.tensor_copy(sums[:, b, :], k.acc[:, ds(t, 1), 0:D].rearrange("p a d -> p (a d)")
                              ).then_inc(S["cp"], 1)

            pairs(g, NT, stage)

        @block.sync
        def _(sp):
            sp.wait_ge(S["wz"], 1)
            for n in range(4):
                half = slice(n % 2 * C, n % 2 * C + C)
                sp.dma_start(wl[half, n, :], k.w["W_lin1" if n else "W_lin0"]).then_inc(S["w"], 16)
            for n in range(2):
                sp.dma_start(wb[:, n, :], k.w[f"WB{n}"]).then_inc(S["w"], 16)
            sp.dma_start(c0[:, :], k.w["Wc0"]).then_inc(S["w"], 16)
            sp.dma_start(c1[:, :], k.w["Wc1"]).then_inc(S["w"], 16)

            def load(t, b, i):
                if later(i):
                    sp.wait_ge(S["o"], t - 1)
                sp.dma_start(skip[b][:, :], k.skip[ds(t * P, P), :]).then_inc(skips[b], 16)

            pairs(sp, NT, load)

        @block.tensor
        def _(pe):
            pe.wait_ge(S["w"], 16 * 8)

            def maps(t, b, i):
                if later(i):
                    pe.wait_ge(S["at"], t - 1)
                pe.wait_ge(S["cp"], t + 1)
                for q in range(2):
                    ins = nc.tensor.transpose(psT[:, b, q * P:(q + 1) * P], sums[:, b, q * 128:(q + 1) * 128],
                                              k.ident[0:P, 0:P])
                ins.then_inc(S["tr"], 1)
                pe.wait_ge(S["at"], t + 1)
                if later(i):
                    pe.wait_ge(S["sq"], t - 1)
                for n in range(4):
                    ins = nc.tensor.matmul(psL[:, b, n * P:(n + 1) * P], wl[:, n, :], aT[:, b, n // 2, :],
                                           start=True, stop=True)
                ins.then_inc(S["lin"], 1)

            def out(t, b, i):
                pe.wait_ge(S["b1"], t + 1)
                if later(i):
                    pe.wait_ge(S["o"], t - 1)
                for n in range(4):
                    ins = nc.tensor.matmul(psO[:, b, n * C:(n + 1) * C], B[:, b, n, :], wb[:, min(n, 1), :],
                                           start=True, stop=True)
                ins.then_inc(S["out"], 1)

            skewed(pe, NT, maps, out)

        @block.scalar
        def _(a):
            def leave(t, b, i):
                a.wait_ge(S["tr"], t + 1)
                if later(i):
                    a.wait_ge(S["lin"], t - 1)
                nc.scalar.activation(aT[:, b, :, :].rearrange("p q c -> p (q c)"), psT[:, b, 0:2 * P],
                                     ACT.Copy).then_inc(S["at"], 1)
                a.wait_ge(S["lin"], t + 1)
                if later(i):
                    a.wait_ge(S["b1"], t - 1)
                nc.scalar.activation(A[:, b, :, :].rearrange("p n e -> p (n e)"), psL[:, b, 0:4 * P],
                                     ACT.Copy).then_inc(S["a"], 1)
                nc.scalar.activation(sq[:, b, :, :].rearrange("p n e -> p (n e)"), psL[:, b, P:4 * P],
                                     ACT.Square).then_inc(S["sq"], 1)

            pairs(a, NT, leave)

        @block.vector
        def _(v):
            v.wait_ge(S["w"], 16 * 8)
            chain = Count(S["c"])

            def step(ins):
                chain.inc(ins)
                v.wait_ge(chain.sem, chain.value())

            def polynomials(t, b, i, per):
                a0, a1, w = A[:, b, 0, :], A[:, b, 1:4, :], vv[:, b, :]
                v.wait_ge(S["sq"], t + 1)
                v.wait_ge(S["a"], t + 1)
                step(nc.vector.tensor_reduce(w, sq[:, b].rearrange("p x e -> p e x"), AX.X, ALU.add))
                if later(i):
                    v.wait_ge(S["out"], t - 1)

                def mul_add(out, in_, m, plus):
                    return nc.vector.tensor_scalar(out, in_, m, plus, ALU.mult, ALU.add)

                def stt(out, in0, scalar, in1, op0, op1):
                    return nc.vector.scalar_tensor_tensor(out=out, in0=in0, scalar=scalar, in1=in1, op0=op0, op1=op1)

                chain.inc(mul_add(q0[:, :], a0, c0[:, 3:4], c0[:, 1:2]))
                step(mul_add(q1[:, :], a0, c1[:, 2:3], c1[:, 1:2]))
                chain.inc(nc.vector.tensor_tensor(q0[:, :], q0[:, :], a0, ALU.mult))
                step(nc.vector.tensor_tensor(q1[:, :], q1[:, :], a0, ALU.mult))
                chain.inc(stt(q0[:, :], w, c0[:, 4:5], q0[:, :], ALU.mult, ALU.add))
                step(stt(q1[:, :], w, c1[:, 3:4], q1[:, :], ALU.mult, ALU.add))
                step(stt(q0[:, :], q0[:, :], c0[:, 0:1], a0, ALU.add, ALU.mult))
                chain.inc(stt(B[:, b, 0, :], w, c0[:, 2:3], q0[:, :], ALU.mult, ALU.add))
                stt(B[:, b, 1:4, :], q1[:, :].unsqueeze(1).broadcast_to([C, 3, P]), c1[:, 0:1], a1,
                    ALU.add, ALU.mult).then_inc(S["b1"], 1)
                v.wait_ge(S["b1"], t + 1)
                v.wait_ge(chain.sem, chain.value())

            def finish(t, b, i):
                v.wait_ge(S["out"], t + 1)
                v.wait_ge(skips[b], i * 16 + 16)
                nc.vector.tensor_tensor(k.acc[:, ds(t, 1), 0:D].rearrange("p a d -> p (a d)"), psO[:, b, 0:D],
                                        skip[b][:, :], ALU.add).then_inc(S["o"], 1)

            per = 9
            polynomials(0, 0, 0, per)
            for t in range(1, 4):
                polynomials(t, t % 2, t // 2, per)
                finish(t - 1, (t - 1) % 2, (t - 1) // 2)
            with v.Fori(2, NT // 2) as i:
                chain.enter(i - 2, 2 * per)
                polynomials(i * 2, 0, i, per)
                finish(i * 2 - 1, 1, i - 1)
                polynomials(i * 2 + 1, 1, i, per)
                finish(i * 2, 0, i)
                chain.leave(NT // 2 - 2)
            finish(NT - 1, 1, NT // 2 - 1)
            v.wait_ge(S["o"], NT)


def batch_norm(nc, k, tag, gammas, betas, vectors):
    names = ["row", "deg", "h", "y", "sum", "m", "d", "sq", "sum2", "r", "sd", "t", "u", "x"]
    es, s = scope(nc, [tag + n for n in names])
    with es:
        S = {n: s[tag + n] for n in names}

        def sb(name, shape):
            return es.enter_context(nc.sbuf_tensor(tag + name, shape, F32))

        gamma = sb("gamma", [P, D])
        beta = sb("beta", [P, D])
        mean = sb("mean", [P, D])
        scale = sb("scale", [P, D])
        std = sb("std", [P, D])
        h = sb("h", [P, 2, G, D])
        sq = sb("sq", [P, 2, G, D])
        tt = sb("tt", [P, 2, G, D])
        rdeg = sb("rdeg", [P, NT])
        ps = es.enter_context(nc.psum_tensor(tag + "ps", [P, 2, 512], F32))
        block = es.enter_context(nc.Block())

        def group(t):
            return k.acc[:, ds(t * G, G), 0:D]

        def row(t):
            return k.acc[:, ds(t, 1), 0:D].rearrange("p a d -> p (a d)")

        def each(vector):
            return vector.unsqueeze(1).broadcast_to([P, G, vector.shape[1]])

        @block.sync
        def _(sp):
            for dst, parts in ((gamma, gammas), (beta, betas)):
                for off, a in parts:
                    sp.dma_start(dst[:, off:off + a.shape[0]], a.partition_broadcast(P)).then_inc(S["row"], 16)

        @block.scalar
        def _(a):
            if not vectors:
                def again(t, b, i):
                    if later(i):
                        a.wait_ge(S["y"], t - 1)
                    for g in range(G):
                        n = ds(t * G + g, 1)
                        ins = nc.scalar.activation(h[:, b, g, :], k.x[:, n, :].rearrange("p a d -> p (a d)"), ACT.Relu,
                                                   bias=k.shift[:, n], scale=k.rstd[:, n])
                    ins.then_inc(S["h"], 1)

                pairs(a, NG, again)

            def square(t, b, i):
                a.wait_ge(S["d"], t + 1)
                if later(i):
                    a.wait_ge(S["sum2"], t - 1)
                nc.scalar.activation(sq[:, b], group(t), ACT.Square).then_inc(S["sq"], 1)

            pairs(a, NG, square)
            a.wait_ge(S["r"], 4)
            nc.scalar.activation(std[:, :], scale[:, :], ACT.Sqrt).then_inc(S["sd"], 1)

        @block.tensor
        def _(pe):
            def total(t, b, i, more):
                if not vectors:
                    pe.wait_ge(S["y"], t + 1)
                first = isinstance(t, int) and t == 0
                for g in range(G):
                    ins = nc.tensor.matmul(ps[:, 0, 0:D], k.ones[0:P, 0:P], row(t * G + g), start=first and g == 0,
                                           stop=not more and g == G - 1)
                ins.then_inc(S["sum"], 1)

            ends(pe, NG, total)

            def total2(t, b, i, more):
                pe.wait_ge(S["sq"], t + 1)
                first = isinstance(t, int) and t == 0
                for g in range(G):
                    ins = nc.tensor.matmul(ps[:, 1, 0:D], k.ones[0:P, 0:P], sq[:, b, g, :], start=first and g == 0,
                                           stop=not more and g == G - 1)
                ins.then_inc(S["sum2"], 1)

            ends(pe, NG, total2)

        @block.vector
        def _(v):
            if vectors:
                nc.vector.memset(mean[:, :], 0.0).then_inc(S["m"], 1)
            else:
                nc.vector.tensor_scalar(rdeg[:, :], k.deg[:, :], 1.0, None, ALU.max).then_inc(S["deg"], 1)
                v.wait_ge(S["deg"], 1)
                nc.vector.reciprocal(rdeg[:, :], rdeg[:, :]).then_inc(S["deg"], 1)
                v.wait_ge(S["deg"], 2)

                def average(t, b, i):
                    v.wait_ge(S["h"], t + 1)
                    for g in range(G):
                        n = t * G + g
                        ins = nc.vector.scalar_tensor_tensor(out=row(n), in0=row(n), scalar=rdeg[:, ds(n, 1)],
                                                             in1=h[:, b, g, :], op0=ALU.mult, op1=ALU.add)
                    ins.then_inc(S["y"], 1)

                pairs(v, NG, average)
                v.wait_ge(S["y"], NG)
            v.wait_ge(S["sum"], NG)
            if vectors:
                v.wait_ge(S["m"], 1)
            wd = C if vectors else D
            nc.vector.tensor_scalar(mean[:, 0:wd], ps[:, 0, 0:wd], 1.0 / N, None, ALU.mult).then_inc(S["m"], 1)
            v.wait_ge(S["m"], 2 if vectors else 1)

            def center(t, b, i):
                out = k.acc[:, ds(t * G, G), 0:wd]
                nc.vector.tensor_tensor(out, out, each(mean[:, 0:wd]), ALU.subtract).then_inc(S["d"], 1)

            pairs(v, NG, center)
            v.wait_ge(S["sum2"], NG)
            if vectors:
                three = ps[:, 1, C:D].rearrange("p (x c) -> p c x", x=3)
                nc.vector.tensor_reduce(std[:, 0:C], three, AX.X, ALU.add).then_inc(S["r"], 1)
                nc.vector.tensor_scalar(scale[:, 0:C], ps[:, 1, 0:C], 1.0 / N, EPS, ALU.mult, ALU.add).then_inc(S["r"], 1)
                v.wait_ge(S["r"], 2)
                nc.vector.tensor_scalar(scale[:, C:D].rearrange("p (x c) -> p x c", x=3),
                                        std[:, 0:C].unsqueeze(1).broadcast_to([P, 3, C]),
                                        1.0 / (3.0 * N), EPS, ALU.mult, ALU.add).then_inc(S["r"], 2)
            else:
                nc.vector.tensor_scalar(scale[:, :], ps[:, 1, 0:D], 1.0 / N, EPS, ALU.mult, ALU.add).then_inc(S["r"], 4)
            v.wait_ge(S["sd"], 1)
            v.wait_ge(S["row"], 16 * (len(gammas) + len(betas)))
            nc.vector.reciprocal(scale[:, :], std[:, :]).then_inc(S["r"], 1)
            v.wait_ge(S["r"], 5)
            nc.vector.tensor_tensor(scale[:, :], scale[:, :], gamma[:, :], ALU.mult).then_inc(S["r"], 1)
            v.wait_ge(S["r"], 6)
            v.wait_ge(S["d"], NG)

            def apply(t, b, i):
                if later(i):
                    v.wait_ge(S["x"], t - 1)
                nc.vector.tensor_tensor(tt[:, b], group(t), each(scale[:, :]), ALU.mult).then_inc(S["t"], 1)

            def residual(t, b, i):
                v.wait_ge(S["t"], t + 1)
                nc.vector.tensor_tensor(tt[:, b, :, 0:wd], tt[:, b, :, 0:wd], each(beta[:, 0:wd]), ALU.add).then_inc(S["u"], 1)
                v.wait_ge(S["u"], t + 1)
                x = k.x[:, ds(t * G, G), :]
                if vectors:
                    nc.vector.tensor_tensor(x[:, :, 0:C], x[:, :, 0:C], tt[:, b, :, 0:C], ALU.add)
                    xv = x[:, :, C:D].rearrange("p g (c x) -> p g x c", x=3)
                    nc.vector.tensor_tensor(xv, xv, tt[:, b, :, C:D].rearrange("p g (x c) -> p g x c", x=3),
                                            ALU.add).then_inc(S["x"], 1)
                else:
                    nc.vector.scalar_tensor_tensor(out=x, in0=tt[:, b], scalar=0.0, in1=x, op0=ALU.max,
                                                   op1=ALU.add).then_inc(S["x"], 1)

            skewed(v, NG, apply, residual)
            v.wait_ge(S["x"], NG)


def scores(nc, k, tag, out, R, edge=None):
    XB = NT // U
    names = ["bc0", "bc1", "on", "sp", "rc", "xl0", "xl1", "xon", "xmm", "xadd", "xc", "is0", "is1", "w", "wz", "lf0", "lf1", "sum", "lk", "sc", "ft", "fe", "al", "ev", "s0", "s1",
             "v", "go", "sr0", "sr1", "vf"]
    es, s = scope(nc, [tag + n for n in names], [(tag + "ga0", k.gathered.pop()), (tag + "ga1", k.gathered.pop())])
    with es:
        S = {n: s[tag + n] for n in names + ["ga0", "ga1"]}

        def sb(name, shape, dt=F32):
            return es.enter_context(nc.sbuf_tensor(tag + name, shape, dt))

        RD = H if edge else 2 * H
        idx = [sb(f"idx{b}", [P, U], I32) for b in range(2)]
        ga = [sb(f"ga{b}", [P, U, D + H]) for b in range(2)]
        gd = [sb(f"gd{b}", [P, U, RD]) for b in range(2)]
        bc = [sb(f"bc{b}", [P, U * P], BF16) for b in range(2)]
        to = [sb(f"to{b}", [P, U * P]) for b in range(2)]
        at_edge = sb("at_edge", [P, ET, RD])
        both = sb("both", [P, 2, U, H])
        sc = sb("sc", [P, 2, U, R])
        res = [sb(f"res{b}", [R, U, P]) for b in range(2)]
        if edge:
            f = [sb(f"f{b}", [P, U, C]) for b in range(2)]
            fT = sb("fT", [128, 2, U // 2, P])
            we = sb("we", [128, D])
            av = sb("av", [128, D])
            fold = sb("fold", [128, H])
            V = sb("V", [128, 2, H])
            psF = es.enter_context(nc.psum_tensor(tag + "psF", [128, 2, 512], F32))
        psS = es.enter_context(nc.psum_tensor(tag + "psS", [R, 3, 512], F32))
        psE = es.enter_context(nc.psum_tensor(tag + "psE", [P, 2, 512], F32))
        block = es.enter_context(nc.Block())
        i_sem, g_sem, f_sem, s_sem, b_sem, r_sem = ([S[n + str(b)] for b in range(2)]
                                                    for n in ("is", "ga", "lf", "s", "bc", "sr"))
        parts = [(0, 4), (4, 8), (8, U)]

        @block.sync
        def _(sp):
            if edge:
                for o in (0, 1):
                    sp.dma_start(we[o * C:(o + 1) * C, :], edge[0]).then_inc(S["w"], 16)
                sp.dma_start(av[:, :], edge[1].rearrange("h c -> (h c)").partition_broadcast(128)
                             ).then_inc(S["w"], 16)

            def broad(b, t, sem):
                sp.dma_start(bc[b][:, :], k.dst_rows[ds(t * U, U)].rearrange("t e -> (t e)").partition_broadcast(P)
                             ).then_inc(sem, 16)

            for n in range(XB):
                if n >= 2:
                    sp.wait_ge(S["xon"], n - 1)
                broad(n % 2, EB + n, S["xl%d" % (n % 2)])
            sp.wait_ge(S["xon"], XB)

            def store_rows(t, b):
                sp.dma_start(tiles(k.edge_rows[ds(t * (U * P), U * P), :]), ga[b][:, :, 0:D]).then_inc(r_sem[b], 16)

            def load(t, b, i):
                if later(i):
                    sp.wait_ge(g_sem[b], i * (16 * U))
                    sp.sem_inc(S["go"], 1)
                    store_rows(t - 2, b)
                sp.dma_start(idx[b][:, :], k.src_of[:, ds(t * U, U)]).then_inc(i_sem[b], 16)
                if later(i):
                    sp.wait_ge(S["on"], t - 1)
                    sp.sem_inc(S["go"], 1)
                broad(b, t, b_sem[b])
                if edge:
                    if later(i):
                        sp.wait_ge(S["ft"], t - 1)
                        sp.sem_inc(S["go"], 1)
                    sp.dma_start(f[b][:, :, :], tiles(k.attr[ds(t * (U * P), U * P), :])).then_inc(f_sem[b], 16)

            pairs(sp, EB, load)
            for t in (EB - 2, EB - 1):
                sp.wait_ge(g_sem[t % 2], 16 * U * (t // 2 + 1))
                store_rows(t, t % 2)
            sp.wait_ge(r_sem[0], 16 * (EB - EB // 2))
            sp.wait_ge(r_sem[1], 16 * (EB // 2))

        @block.gpsimd
        def _(g):
            def gather(t, b, i):
                g.wait_ge(i_sem[b], i * 16 + 16)
                if later(i):
                    g.wait_ge(S["lk"], t - 1)
                    g.wait_ge(r_sem[b], i * 16)
                g.sem_inc(S["go"], 1)
                for u in range(U):
                    g.indirect_dma_start(ga[b][:, u, :], None, k.sender_rows,
                                         bass.IndirectOffsetOnAxis(ap=idx[b][:, u:u + 1], axis=0)
                                         ).then_inc(g_sem[b], 16)

            pairs(g, EB, gather)

        @block.tensor
        def _(pe):
            if edge:
                pe.wait_ge(S["v"], 3)
            for n in range(XB):
                pe.wait_ge(S["xon"], n + 1)
                for u in range(U):
                    if n >= 2 and u == 0:
                        pe.wait_ge(S["xadd"], (n - 1) * U)
                    ins = nc.tensor.matmul(psE[:, n % 2, u * RD:(u + 1) * RD], to[n % 2][:, u * P:(u + 1) * P],
                                           k.recv[:, n * U + u, 0:RD], start=True, stop=True)
                ins.then_inc(S["xmm"], 1)
            pe.wait_ge(S["xadd"], NT)

            def spread(t, b, i):
                _, at = nc.values_load_multi_w_load_instructions(
                    k.node_tile[0:1, ds(t * U, U)], engines=[PE], min_val=0, max_val=NT - 1,
                    skip_runtime_bounds_check_because="made in prepare() from counts of at most NT - 1")
                pe.wait_ge(S["on"], t + 1)
                if later(i):
                    pe.wait_ge(S["rc"], t - 1)
                for u in range(U):
                    ins = nc.tensor.matmul(psE[:, 0 if edge else b, u * RD:(u + 1) * RD], to[b][:, u * P:(u + 1) * P],
                                           k.recv[:, ds(at[u], 1), 0:RD].rearrange("p a h -> p (a h)"),
                                           start=True, stop=True)
                if edge:
                    pe.wait_ge(S["fe"], t + 1)
                    for n in range(U // 2):
                        ins = nc.tensor.matmul(psE[:, 1, 2 * n * H:(2 * n + 2) * H], fT[:, b, n, :],
                                               V[:, :, :].rearrange("p o h -> p (o h)"), start=True, stop=True)
                ins.then_inc(S["sp"], 1)

            def turn(t, b, i):
                if edge:
                    pe.wait_ge(f_sem[b], i * 16 + 16)
                    if not isinstance(t, int) or t:
                        pe.wait_ge(S["fe"], t)
                    for n in range(U // 2):
                        ins = nc.tensor.transpose(psF[:, n // 3, (n % 3) * P:(n % 3 + 1) * P],
                                                  f[b][:, 2 * n:2 * n + 2, :].rearrange("p u f -> p (u f)"),
                                                  k.ident[0:P, 0:P])
                    ins.then_inc(S["ft"], 1)

            def score(t, b, i):
                spread(t, b, i)
                pe.wait_ge(S["lk"], t + 1)
                if not isinstance(t, int) or t:
                    pe.wait_ge(S["ev"], t)
                for u in range(U):
                    to_ = psS[:, u // 4, (u % 4) * P:(u % 4 + 1) * P]
                    ins = nc.tensor.transpose(to_, sc[:, b, u, :], k.ident[0:P, 0:P])
                ins.then_inc(S["al"], 1)

            skewed(pe, EB, turn, score)

        @block.scalar
        def _(a):
            def turned(t, b, i):
                if edge:
                    a.wait_ge(S["ft"], t + 1)
                    if later(i):
                        a.wait_ge(S["sp"], t - 1)
                    nc.scalar.activation(fT[:, b, 0:3, :], psF[:, 0, 0:3 * P].rearrange("p (n e) -> p n e", e=P), ACT.Copy)
                    nc.scalar.activation(fT[:, b, 3:5, :], psF[:, 1, 0:2 * P].rearrange("p (n e) -> p n e", e=P),
                                         ACT.Copy).then_inc(S["fe"], 1)

            def leave(t, b, i):
                a.wait_ge(S["al"], t + 1)
                if later(i):
                    a.wait_ge(s_sem[b], i * 16)
                for n, (u0, u1) in enumerate(parts):
                    ins = nc.scalar.activation(res[b][:, u0:u1, :],
                                               psS[:, n, 0:(u1 - u0) * P].rearrange("r (u e) -> r u e", e=P),
                                               ACT.Copy)
                ins.then_inc(S["ev"], 1)
                a.wait_ge(S["ev"], t + 1)
                a.dma_start(out[ds(t * U, U)].rearrange("t r e -> r t e"), res[b][:, :, :]).then_inc(s_sem[b], 16)

            skewed(a, EB, turned, leave)
            a.wait_ge(s_sem[0], 16 * (EB - EB // 2))
            a.wait_ge(s_sem[1], 16 * (EB // 2))

        @block.vector
        def _(v):
            if edge:
                nc.vector.memset(V[:, :, :], 0.0).then_inc(S["wz"], 1)
                v.wait_ge(S["w"], 48)
                nc.vector.tensor_tensor(we[:, :], we[:, :], av[:, :], ALU.mult).then_inc(S["wz"], 1)
                v.wait_ge(S["wz"], 2)
                nc.vector.tensor_reduce(fold[:, :], we[:, :].rearrange("p (h c) -> p h c", c=CH), AX.X,
                                        ALU.add).then_inc(S["v"], 1)
                v.wait_ge(S["v"], 1)
                for o in (0, 1):
                    nc.vector.tensor_copy(V[o * C:(o + 1) * C, o, :], fold[o * C:(o + 1) * C, :]).then_inc(S["v"], 1)

            nc.vector.memset(at_edge[:, :, :], 0.0).then_inc(S["xc"], 1)

            def extra_one_hot(n):
                v.wait_ge(S["xl%d" % (n % 2)], 16 * (n // 2 + 1))
                if n >= 2:
                    v.wait_ge(S["xmm"], n - 1)
                nc.vector.tensor_scalar(to[n % 2][:, :], bc[n % 2][:, :], k.lane[:, 0:1], None,
                                        ALU.is_equal).then_inc(S["xon"], 1)

            extra_one_hot(0)
            for n in range(XB):
                if n + 1 < XB:
                    extra_one_hot(n + 1)
                _, at = nc.values_load_multi_w_load_instructions(
                    k.extra_at[0:1, n * U:(n + 1) * U], engines=[DVE], min_val=0, max_val=ET - 1,
                    skip_runtime_bounds_check_because="prepare() takes its minimum with ET - 1")
                v.wait_ge(S["xmm"], n + 1)
                for u in range(U):
                    if n * U + u == 0:
                        v.wait_ge(S["xc"], 1)
                    else:
                        v.wait_ge(S["xadd"], n * U + u)
                    dst = at_edge[:, ds(at[u], 1), :].rearrange("p a h -> p (a h)")
                    nc.vector.tensor_tensor(dst, dst, psE[:, n % 2, u * RD:(u + 1) * RD],
                                            ALU.add).then_inc(S["xadd"], 1)
            v.wait_ge(S["xadd"], NT)

            def one_hot(t, b, i):
                v.wait_ge(b_sem[b], i * 16 + 16)
                if later(i):
                    v.wait_ge(S["sp"], t - 1)
                nc.vector.tensor_scalar(to[b][:, :], bc[b][:, :], k.lane[:, 0:1], None,
                                        ALU.is_equal).then_inc(S["on"], 1)

            def gathered(t, b, i):
                if later(i):
                    v.wait_ge(S["al"], t - 1)
                v.wait_ge(S["sp"], t + 1)
                nc.vector.tensor_tensor(gd[b][:, :, :], at_edge[:, ds(t * U, U), :],
                                        psE[:, 0 if edge else b, 0:U * RD].rearrange("p (u r) -> p u r", r=RD),
                                        ALU.add).then_inc(S["rc"], 1)
                v.wait_ge(S["rc"], t + 1)
                v.wait_ge(g_sem[b], i * (16 * U) + 16 * U)
                nc.vector.tensor_tensor(both[:, b], ga[b][:, :, D:], gd[b][:, :, 0:H], ALU.add).then_inc(S["sum"], 1)
                v.wait_ge(S["sum"], t + 1)
                if edge:
                    nc.vector.tensor_tensor(both[:, b], both[:, b], psE[:, 1, 0:U * H].rearrange(
                        "p (u h) -> p u h", h=H), ALU.add).then_inc(S["vf"], 1)
                    v.wait_ge(S["vf"], t + 1)
                done = S["lk" if edge else "sc"]
                nc.vector.scalar_tensor_tensor(out=sc[:, b, :, 0:H], in0=both[:, b], scalar=0.2, in1=both[:, b],
                                               op0=ALU.mult, op1=ALU.max).then_inc(done, 1)
                if not edge:
                    v.wait_ge(S["sc"], t + 1)
                    nc.vector.tensor_tensor(sc[:, b, :, H:R], sc[:, b, :, 0:H], gd[b][:, :, H:2 * H],
                                            ALU.max).then_inc(S["lk"], 1)

            skewed(v, EB, one_hot, gathered)


def softmax_weights(nc, k, tag, src, out, out_extra, R):
    names = ["ld", "halo", "hz", "pen", "f", "end", "tr", "row", "rs", "cin", "cc", "a", "e", "x", "st", "sx", "ex",
             "xr0", "xr1"]
    es, s = scope(nc, [tag + n for n in names], [(tag + n, k.gathered.pop()) for n in ("gx", "xg0", "xg1")])
    Q = H * CK
    with es:
        S = {n: s[tag + n] for n in names + ["gx", "xg0", "xg1"]}

        def sb(name, shape, dt=F32):
            return es.enter_context(nc.sbuf_tensor(tag + name, shape, dt))

        A = sb("A", [Q, CE])
        M = sb("M", [Q, CE + 2])
        pen = sb("pen", [Q, CE + 1], BF16)
        inner = sb("inner", [Q, 1])
        ends_ = sb("ends", [Q, 4])
        rows = sb("rows", [1, 4, Q])
        cin = sb("cin", [Q, 2])
        extra = sb("extra", [NT, R * P])
        xrows = [sb(f"xrows{b}", [P, U, D + H]) for b in range(2)]
        ps = es.enter_context(nc.psum_tensor(tag + "ps", [128, 4, 512], F32))
        block = es.enter_context(nc.Block())
        D32 = M[:, :].bitcast(I32)
        dst = k.dst.rearrange("(c e) -> c e", e=CE)
        halves = (slice(0, CE // 2), slice(CE // 2, CE))

        def rows_of(t, r, to_sb, sp, sem, sbuf):
            for h in range(H):
                d = t[:, r + h, :].rearrange("(c t) e -> c t e", t=CT)
                x = sbuf[h * CK:(h + 1) * CK, 0:CE].rearrange("c (t e) -> c t e", e=P)
                if to_sb:
                    sp.dma_start(x, d).then_inc(sem, 16)
                else:
                    sp.dma_start(d, x).then_inc(sem, 16)

        @block.sync
        def _(sp):
            sp.wait_ge(S["hz"], 1)
            for h in range(H):
                o = h * CK
                sp.dma_start(D32[o:o + CK, 1:CE + 1], dst).then_inc(S["halo"], 16)
                sp.dma_start(D32[o + 1:o + CK, 0:1], dst[0:CK - 1, CE - 1:CE],
                             allow_slow_non_contiguous=True).then_inc(S["halo"], 16)
                sp.dma_start(D32[o:o + CK - 1, CE + 1:CE + 2], dst[1:CK, 0:1],
                             allow_slow_non_contiguous=True).then_inc(S["halo"], 16)
            rows_of(src, R - H, True, sp, S["ld"], A)
            if R > H:
                sp.wait_ge(S["f"], 2)
                rows_of(src, 0, True, sp, S["ld"], A)
            sp.wait_ge(S["ex"], 2)
            rows_of(out, 0, False, sp, S["st"], A)
            if R > H:
                sp.wait_ge(S["x"], 2)
                rows_of(out, H, False, sp, S["st"], M)
            sp.wait_ge(S["st"], 16 * R)
            sp.sem_inc(S["sx"], 1)
            sp.wait_ge(S["gx"], 16)
            sp.dma_start(out_extra.rearrange("t r e -> t (r e)"), extra[:, :]).then_inc(S["st"], 16)
            sp.wait_ge(S["st"], 16 * R + 16)

        @block.gpsimd
        def _(g):
            for n in range(NT // U):
                if n >= 2:
                    g.wait_ge(S[f"xr{n % 2}"], 16 * (n // 2))
                for u in range(U):
                    at = ET + n * U + u
                    g.indirect_dma_start(xrows[n % 2][:, u, :], None, k.sender_rows,
                                         bass.IndirectOffsetOnAxis(ap=k.src_of[:, at:at + 1], axis=0)
                                         ).then_inc(S[f"xg{n % 2}"], 16)
            g.wait_ge(S["sx"], 1)
            g.indirect_dma_start(extra[:, :], None, out.rearrange("t r e -> t (r e)"),
                                 bass.IndirectOffsetOnAxis(ap=k.tile_of[:, :], axis=0)).then_inc(S["gx"], 16)

        @block.tensor
        def _(pe):
            for n in range(2):
                pe.wait_ge(S["end"], n + 3)
                for c in range(2):
                    ins = nc.tensor.transpose(ps[0:1, n, c * Q:(c + 1) * Q], ends_[:, 2 * n + c:2 * n + c + 1],
                                              k.ident[0:Q, 0:Q])
                ins.then_inc(S["tr"], 1)
                pe.wait_ge(S["cin"], n + 1)
                nc.tensor.transpose(ps[0:Q, 2 + n, 0:1], rows[0:1, 2 + n, :], k.ident[0:1, 0:1]).then_inc(S["tr"], 1)

        @block.scalar
        def _(a):
            for n in range(NT // U):
                a.wait_ge(S[f"xg{n % 2}"], 16 * U * (n // 2 + 1))
                a.dma_start(tiles(k.edge_rows[(EB + n) * U * P:(EB + n + 1) * U * P, :]),
                            xrows[n % 2][:, :, 0:D]).then_inc(S[f"xr{n % 2}"], 16)
            a.wait_ge(S["xr0"], 48)
            a.wait_ge(S["xr1"], 32)
            for n, part in enumerate(halves):
                a.wait_ge(S["e"], n + 1)
                nc.scalar.activation(A[:, part], A[:, part], ACT.Exp).then_inc(S["ex"], 1)

        @block.vector
        def _(v):
            nc.vector.memset(D32[:, 0:CE + 2:CE + 1], -5).then_inc(S["hz"], 1)
            v.wait_ge(S["halo"], 16 * 3 * H)
            nc.vector.tensor_tensor(pen[:, :], D32[:, 1:CE + 2], D32[:, 0:CE + 1], ALU.not_equal).then_inc(S["pen"], 1)
            v.wait_ge(S["pen"], 1)
            nc.vector.tensor_scalar(pen[:, :], pen[:, :], LOW, None, ALU.mult).then_inc(S["pen"], 1)
            v.wait_ge(S["pen"], 2)
            nc.vector.tensor_reduce(inner[:, :], pen[:, 1:CE], AX.X, ALU.min).then_inc(S["pen"], 1)
            v.wait_ge(S["pen"], 3)
            for n in range(2):
                nc.vector.tensor_tensor(ends_[:, 2 * n + 1:2 * n + 2], inner[:, :], pen[:, n * CE:n * CE + 1],
                                        ALU.min).then_inc(S["end"], 1)
            v.wait_ge(S["ld"], 16 * H)

            def scan(n, initial, sem):
                if n == 0:
                    o, d0, d1 = M[:, 0:CE], pen[:, 0:CE], A[:, 0:CE]
                else:
                    o, d0, d1 = M[:, 0:CE][:, ::-1], pen[:, 1:CE + 1][:, ::-1], M[:, 0:CE][:, ::-1]
                return nc.vector.tensor_tensor_scan(o, d0, d1, initial, ALU.add, ALU.max)

            for n in range(2):
                first = scan(n, LOW, None)
                first.then_inc(S["a"], 1)
                v.wait_ge(S["a"], 2 * n + 1)
                last = slice(CE - 1, CE) if n == 0 else slice(0, 1)
                nc.vector.tensor_copy(ends_[:, 2 * n:2 * n + 1], M[:, last]).then_inc(S["end"], 1)
                v.wait_ge(S["tr"], 2 * n + 1)
                r0, r1, r2 = rows[0:1, 0, :], rows[0:1, 1, :], rows[0:1, 2 + n, :]
                nc.vector.tensor_copy(r0, ps[0:1, n, 0:Q]).then_inc(S["row"], 1)
                nc.vector.tensor_copy(r1, ps[0:1, n, Q:2 * Q]).then_inc(S["row"], 1)
                v.wait_ge(S["row"], 5 * n + 2)
                edge_ = slice(0, Q, CK) if n == 0 else slice(CK - 1, Q, CK)
                nc.vector.memset(rows[0:1, 1, edge_], LOW).then_inc(S["row"], 1)
                v.wait_ge(S["row"], 5 * n + 3)
                flip = (lambda t: t) if n == 0 else (lambda t: t[:, ::-1])
                nc.vector.tensor_tensor_scan(flip(r0), flip(r1), flip(r0), LOW, ALU.add, ALU.max
                                             ).then_inc(S["row"], 1)
                v.wait_ge(S["row"], 5 * n + 4)
                if n == 0:
                    nc.vector.tensor_copy(r2[:, 1:Q], r0[:, 0:Q - 1]).then_inc(S["row"], 1)
                else:
                    nc.vector.tensor_copy(r2[:, 0:Q - 1], r0[:, 1:Q]).then_inc(S["row"], 1)
                v.wait_ge(S["row"], 5 * n + 5)
                nc.vector.memset(rows[0:1, 2 + n, edge_], LOW).then_inc(S["cin"], 1)
                v.wait_ge(S["tr"], 2 * n + 2)
                nc.vector.tensor_copy(cin[:, n:n + 1], ps[0:Q, 2 + n, 0:1]).then_inc(S["cc"], 1)
                v.wait_ge(S["cc"], n + 1)
                scan(n, cin[:, n:n + 1], None).then_inc(S["a"], 1)
                v.wait_ge(S["a"], 2 * n + 2)
                if n == 0:
                    v.sem_inc(S["f"], 2)
            if R > H:
                v.wait_ge(S["ld"], 32 * H)
            for part in halves:
                nc.vector.tensor_tensor(A[:, part], A[:, part], M[:, part], ALU.subtract).then_inc(S["e"], 1)
            if R > H:
                v.wait_ge(S["e"], 2)
                nc.vector.scalar_tensor_tensor(out=M[:, 0:CE], in0=pen[:, 0:CE], scalar=-1.0, in1=M[:, 0:CE],
                                               op0=ALU.is_lt, op1=ALU.mult).then_inc(S["x"], 2)
                v.wait_ge(S["x"], 2)


def attend(nc, k, tag, bias, gamma, beta, own, out=None):
    names = ["row", "own", "xp0", "xp1", "h", "d", "e", "ex", "t", "u", "y"]
    es, s = scope(nc, [tag + n for n in names])
    with es:
        S = {n: s[tag + n] for n in names}

        def sb(name, shape):
            return es.enter_context(nc.sbuf_tensor(tag + name, shape, F32))

        bias_row = sb("bias", [P, D])
        rden = sb("rden", [P, NT, H])
        tt = sb("tt", [P, 2, G, D])
        h = sb("h", [P, 2, G, D])
        if own:
            score = sb("score", [P, NT, H])
            top = sb("top", [P, NT, H])
            alone = sb("alone", [P, NT])
        block = es.enter_context(nc.Block())
        x_sem = [S["xp0"], S["xp1"]]
        sums = k.acc[:, :, D:D + H]

        def row(t):
            return k.acc[:, ds(t * G, G), 0:D]

        @block.sync
        def _(sp):
            sp.dma_start(bias_row[:, :], bias.partition_broadcast(P)).then_inc(S["row"], 16)
            if own:
                def load(t, b, i):
                    if later(i):
                        sp.wait_ge(S["t"], t - 1)
                    sp.dma_start(h[:, b], tiles(k.sender_rows[ds(t * (G * P), G * P), 0:D])).then_inc(x_sem[b], 16)

                pairs(sp, NG, load)

        @block.scalar
        def _(a):
            if own:
                a.wait_ge(S["e"], 4)
                nc.scalar.activation(score[:, :, :], score[:, :, :], ACT.Exp).then_inc(S["ex"], 1)
            else:
                def again(t, b, i):
                    if later(i):
                        a.wait_ge(S["y"], t - 1)
                    for g in range(G):
                        n = ds(t * G + g, 1)
                        ins = nc.scalar.activation(h[:, b, g, :], k.x[:, n, :].rearrange("p a d -> p (a d)"), ACT.Relu,
                                                   bias=k.shift[:, n], scale=k.rstd[:, n])
                    ins.then_inc(S["h"], 1)

                pairs(a, NG, again)

        @block.vector
        def _(v):
            if own:
                nc.vector.tensor_copy(score[:, :, :], k.recv[:, :, H:2 * H]).then_inc(S["own"], 1)
                nc.vector.tensor_scalar(alone[:, :], k.deg[:, :], 0.5, None, ALU.is_lt).then_inc(S["e"], 1)
                v.wait_ge(S["e"], 1)
                v.wait_ge(S["own"], 1)
                nc.vector.tensor_tensor(top[:, :, :], alone[:, :].unsqueeze(2).broadcast_to([P, NT, H]),
                                        score[:, :, :], ALU.mult).then_inc(S["e"], 1)
                v.wait_ge(S["e"], 2)
                nc.vector.tensor_tensor(top[:, :, :], top[:, :, :], k.acc[:, :, D + H:D + 2 * H],
                                        ALU.add).then_inc(S["e"], 1)
                v.wait_ge(S["e"], 3)
                nc.vector.tensor_tensor(score[:, :, :], score[:, :, :], top[:, :, :],
                                        ALU.subtract).then_inc(S["e"], 1)
                v.wait_ge(S["ex"], 1)
                nc.vector.tensor_tensor(rden[:, :, :], sums, score[:, :, :], ALU.add).then_inc(S["d"], 1)
            else:
                nc.vector.tensor_scalar(rden[:, :, :], sums, 1e-16, None, ALU.add).then_inc(S["d"], 1)
            v.wait_ge(S["d"], 1)
            nc.vector.reciprocal(rden[:, :, :], rden[:, :, :]).then_inc(S["d"], 1)
            v.wait_ge(S["d"], 2)
            v.wait_ge(S["row"], 16)
            chain = Count(S["u"])

            def by_head(t):
                return t.rearrange("p g (h c) -> p g h c", c=CH)

            def spread(t, per_node):
                return per_node[:, ds(t * G, G), :].unsqueeze(3).broadcast_to([P, G, H, CH])

            def first(t, b, i):
                if own:
                    v.wait_ge(x_sem[b], i * 16 + 16)
                    nc.vector.tensor_tensor(by_head(tt[:, b]), by_head(h[:, b]), spread(t, score),
                                            ALU.mult).then_inc(S["t"], 1)
                    v.wait_ge(S["t"], t + 1)
                    chain.inc(nc.vector.tensor_tensor(tt[:, b], tt[:, b], row(t), ALU.add))
                    v.wait_ge(chain.sem, chain.value())
                    chain.inc(nc.vector.tensor_tensor(by_head(tt[:, b]), by_head(tt[:, b]), spread(t, rden),
                                                      ALU.mult))
                    v.wait_ge(chain.sem, chain.value())
                else:
                    chain.inc(nc.vector.tensor_tensor(by_head(tt[:, b]), by_head(row(t)), spread(t, rden),
                                                      ALU.mult))
                    v.wait_ge(chain.sem, chain.value())
                    v.wait_ge(S["h"], t + 1)
                    chain.inc(nc.vector.tensor_tensor(tt[:, b], tt[:, b], h[:, b], ALU.add))
                    v.wait_ge(chain.sem, chain.value())
                nc.vector.tensor_tensor(row(t), tt[:, b], bias_row[:, :].unsqueeze(1).broadcast_to([P, G, D]), ALU.add).then_inc(S["y"], 1)

            first(0, 0, 0)
            first(1, 1, 0)
            v.wait_ge(S["y"], 2)
            with v.Fori(1, NG // 2) as i:
                chain.enter(i - 1, 4)
                first(i * 2, 0, i)
                first(i * 2 + 1, 1, i)
                chain.leave(NG // 2 - 1)
            v.wait_ge(S["y"], NG)

    row_stats(nc, k, tag + "n", k.acc, D)

    names = ["w", "n", "t", "u", "x", "s0", "s1"]
    es, s = scope(nc, [tag + "f" + n for n in names])
    with es:
        S = {n: s[tag + "f" + n] for n in names}
        gamma_row = es.enter_context(nc.sbuf_tensor(tag + "gamma", [P, D], F32))
        beta_row = es.enter_context(nc.sbuf_tensor(tag + "beta", [P, D], F32))
        y = es.enter_context(nc.sbuf_tensor(tag + "yn", [P, 2, G, D], F32))
        block = es.enter_context(nc.Block())

        def xrow(t):
            return k.x[:, ds(t * G, G), :]

        @block.sync
        def _(sp):
            sp.dma_start(gamma_row[:, :], gamma.partition_broadcast(P)).then_inc(S["w"], 16)
            sp.dma_start(beta_row[:, :], beta.partition_broadcast(P)).then_inc(S["w"], 16)
            if out is not None:
                def store(t, b, i):
                    sp.wait_ge(S["x"], t + 1)
                    sp.dma_start(tiles(out[ds(t * (G * P), G * P), :]), xrow(t)).then_inc(S[f"s{b}"], 16)

                pairs(sp, NG, store)
                sp.wait_ge(S["s0"], 16 * (NG // 2))
                sp.wait_ge(S["s1"], 16 * (NG // 2))

        @block.scalar
        def _(a):
            def norm(t, b, i):
                if later(i):
                    a.wait_ge(S["x"], t - 1)
                for g in range(G):
                    n = ds(t * G + g, 1)
                    ins = nc.scalar.activation(y[:, b, g, :], k.acc[:, n, 0:D].rearrange("p a d -> p (a d)"),
                                               ACT.Identity, bias=k.shift[:, n], scale=k.rstd[:, n])
                ins.then_inc(S["n"], 1)

            pairs(a, NG, norm)

        @block.gpsimd
        def _(g):
            g.wait_ge(S["w"], 32)

            def shifted(t, b, i):
                g.tensor_tensor(xrow(t), xrow(t), beta_row[:, :].unsqueeze(1).broadcast_to([P, G, D]), ALU.add).then_inc(S["u"], 1)

            pairs(g, NG, shifted)

        @block.vector
        def _(v):
            v.wait_ge(S["w"], 32)

            def scaled(t, b, i):
                v.wait_ge(S["n"], t + 1)
                nc.vector.tensor_tensor(y[:, b], y[:, b], gamma_row[:, :].unsqueeze(1).broadcast_to([P, G, D]), ALU.mult).then_inc(S["t"], 1)

            def residual(t, b, i):
                v.wait_ge(S["t"], t + 1)
                v.wait_ge(S["u"], t + 1)
                nc.vector.tensor_tensor(xrow(t), xrow(t), y[:, b], ALU.add).then_inc(S["x"], 1)

            skewed(v, NG, scaled, residual)
            v.wait_ge(S["x"], NG)


def build(nc, ins, out):
    k = Net()
    k.x_in, k.src, k.dst = ins["x"], ins["src"], ins["dst"]
    k.rbf, k.sh, k.attr = ins["edge_attr_16"], ins["edge_attr_4"], ins["edge_attr_64"]
    w0 = {n[7:]: a for n, a in ins.items() if n.startswith("L0_")}
    k.w = w0

    def dram(name, shape, dt=F32):
        return nc.dram_tensor(name, shape, dt).ap()

    k.rbf_extra = dram("rbf_extra", [NT, P * 16])
    k.sh_extra = dram("sh_extra", [NT, P * 4])
    k.table = dram("rows", [N, D])
    k.skip = dram("skip", [N, D])
    k.sender_rows = dram("sender_rows", [N, D + H])
    k.edge_rows = dram("edge_rows", [ST * P, D])
    k.dst_rows = dram("dst_rows", [ST, P], BF16)
    k.scores = {n: dram(f"scores{n}", [ET, r, P]) for n, r in ((2, H), (3, 2 * H))}
    k.weights = {n: dram(f"weights{n}", [ET, r, P]) for n, r in ((2, H), (3, 2 * H))}
    k.weights_extra = {n: dram(f"weights_extra{n}", [NT, r, P]) for n, r in ((2, H), (3, 2 * H))}
    with ExitStack() as es:
        def sb(name, shape, dt=F32):
            return es.enter_context(nc.sbuf_tensor(name, shape, dt))

        k.gathered = [es.enter_context(nc.semaphore(f"gathered{b}")) for b in range(19)]
        k.x = sb("x_nodes", [P, NT, D])
        k.src_of = sb("src_of", [P, ST], I32)
        k.dst_in = sb("dst_in", [P, ST])
        k.node_tile = sb("node_tile", [1, ST], I32)
        k.tile_of = sb("tile_of", [NT, 1], I32)
        k.ident = sb("ident", [128, 128])
        k.ones = sb("ones", [128, 128])
        k.iota = sb("iota", [P, P])
        k.mean = sb("mean", [P, NT])
        k.rstd = sb("rstd", [P, NT])
        k.shift = sb("shift", [P, NT])
        k.deg = sb("deg", [P, NT])
        k.lane = sb("lane", [P, 1])
        k.extra_at = sb("extra_at", [1, NT], I32)
        k.recv = sb("recv", [P, NT, 2 * H])
        prepare(nc, k)
        row_stats(nc, k, "n0", k.x, D)

        def weights0(sp, w, sem):
            for q in range(2):
                for o, n in ((0, 0 if q == 0 else 1), (1, 1)):
                    for m, name in enumerate(("W_up", "Wsc")):
                        sp.dma_start(w[o * C:(o + 1) * C, q, m * 128 + o * C:m * 128 + (o + 1) * C],
                                     w0[f"{name}{n}"]).then_inc(sem, 16)

        project(nc, k, "p0", weights0, 8, [(k.table, 0, D), (k.skip, D, D)], 2 * D, split=True)
        with nc.sbuf_tensor("acc0", [P, NT, AW], F32) as k.acc:
            convolve(nc, k, "c0")
            contract(nc, k, "t0")
            batch_norm(nc, k, "b0", [(0, w0["gamma0"])] + [(C * n, w0["gamma1"]) for n in (1, 2, 3)],
                       [(0, w0["beta0"])], vectors=True)
        row_stats(nc, k, "n1", k.x, D)

        def dense(name):
            def load(sp, w, sem):
                for q in range(2):
                    sp.dma_start(w[:, q, 0:D], ins[name][q * 128:(q + 1) * 128, :]).then_inc(sem, 16)
            return load

        project(nc, k, "p1", dense("L1_gnn_W_src"), 2, [(k.table, 0, D)], D)
        with nc.sbuf_tensor("acc1", [P, NT, AW], F32) as k.acc:
            aggregate(nc, k, "g1", k.table, degree=True)
            batch_norm(nc, k, "b1", [(0, ins["L1_gnn_gamma"])], [(0, ins["L1_gnn_beta"])], vectors=False)
        for layer, R in ((2, H), (3, 2 * H)):
            g = {n[7:]: a for n, a in ins.items() if n.startswith(f"L{layer}_")}
            last = layer == 3
            row_stats(nc, k, f"n{layer}", k.x, D)
            pieces = [(k.sender_rows, 0, D + H)]
            project(nc, k, f"p{layer}", dense(f"L{layer}_gnn_W"), 2, pieces, D + 2 * H,
                    att=(g["att_src"], g["att_dst"]), self_score=last)
            scores(nc, k, f"s{layer}", k.scores[layer], R, None if last else (g["W_e"], g["att_edge"]))
            softmax_weights(nc, k, f"m{layer}", k.scores[layer], k.weights[layer], k.weights_extra[layer], R)
            with nc.sbuf_tensor(f"acc{layer}", [P, NT, AW], F32) as k.acc:
                aggregate(nc, k, f"g{layer}", None, (k.weights[layer], k.weights_extra[layer]), R)
                attend(nc, k, f"a{layer}", g["bias"], g["gamma"], g["beta"], own=last, out=out if last else None)


def kernel(**inputs):
    import concourse.bacc as bacc
    from concourse.bass_utils import run_bass_kernel_spmd

    nc = bacc.Bacc("TRN2", target_bir_lowering=False, num_devices=1)
    arrays, aps = {}, {}
    for name, a in inputs.items():
        a = np.ascontiguousarray(a)
        arrays[f"in_{name}"] = a
        aps[name] = nc.dram_tensor(f"in_{name}", a.shape, mybir.dt.from_np(a.dtype), kind="ExternalInput").ap()
    out = nc.dram_tensor("out_x", (N, D), F32, kind="ExternalOutput").ap()
    build(nc, aps, out)
    return run_bass_kernel_spmd(nc, [arrays], core_ids=[0]).results[0]["out_x"]
```
